# Optimizing a Trainium2 kernel written in Bass

```python
import numpy as np
import jax
import jax.numpy as jnp

def _softmax(x, axis=-1):
    return jax.nn.softmax(x, axis=axis)

def _gelu(x):
    return jax.nn.gelu(x, approximate=True)

def _silu(x):
    return jax.nn.silu(x)

def _sigmoid(x):
    return jax.nn.sigmoid(x)

def _layernorm(x, axis=-1, eps=1e-05):
    m = jnp.mean(x, axis=axis, keepdims=True)
    v = jnp.var(x, axis=axis, keepdims=True)
    return (x - m) / jnp.sqrt(v + eps)

def _scatter_add(tgt, idx, src, axis=0):
    return tgt.at[idx].add(src)

def _segment_sum(src, seg, n):
    return jax.ops.segment_sum(src, seg, n)
kernel_name = 'mk_vit_tower_d1_tok_img256_r4_be659f'

def setup_inputs(seed: int=0):
    np.random.seed(seed)
    _w = jnp.asarray

    def _rec_inputs():
        import jax
        import jax.numpy as jnp
        _rk = jax.random.key(seed)
        x = -7.10856e-05 + 0.999911 * jax.random.normal(jax.random.fold_in(_rk, 1), (16, 64, 128, 64), jnp.float32)
        return x
    x = _rec_inputs()

    def _L0_tok_setup():
        import jax, jax.numpy as jnp
        import numpy as np
        PATCH_LEN = 16
        STRIDE = 8
        PAD = 8
        key = jax.random.key(seed)
        k1, k2 = jax.random.split(key)
        x = jax.random.normal(k1, (32, 64, 128, 64), dtype=jnp.float32)
        in_feat = 64 * (PATCH_LEN // 2 + 1) * 2
        W = jax.random.normal(k2, (64, in_feat), dtype=jnp.float32) * 0.02
        return {'x': x, 'W': W}
    _L0_tok_all = _L0_tok_setup()
    _L0_tok_in = {k: v for k, v in _L0_tok_all.items() if k in ('W',)}
    del _L0_tok_all

    def _L0_attn_setup():
        import jax, jax.numpy as jnp
        import numpy as np
        D = 64
        L = 2
        B, S = (8, 1024)
        LR = 0.001
        WD = 0.01
        MAX_ALR = 0.1
        EPS = 1e-08

        def _lmm(Ws, bs, x):
            for i in range(L):
                x = x + jax.nn.silu(x @ Ws[i] + bs[i])
            return x

        def _reference_tuple_inner(x, Wk, Wq, Wv, Wlr, blr, Ws, bs):
            keys = x @ Wk
            queries = x @ Wq
            values = x @ Wv
            alr = (jax.nn.sigmoid(x @ Wlr + blr) * MAX_ALR).reshape(-1)

            def loss_fn(params):
                Ws_, bs_ = params
                preds = _lmm(Ws_, bs_, keys).reshape(-1, D)
                tgt = values.reshape(-1, D)
                per_tok = jnp.mean((preds - tgt) ** 2, axis=-1)
                return jnp.sum(per_tok * alr)
            gWs, gbs = jax.grad(loss_fn)((Ws, bs))

            def adamw_step(p, g):
                return p * (1.0 - LR * WD) - LR * g / (jnp.sqrt(g * g) + EPS)
            nWs = adamw_step(Ws, gWs)
            nbs = adamw_step(bs, gbs)
            retrieved = _lmm(nWs, nbs, queries)
            return (retrieved, -gWs, -gbs)
        key = jax.random.key(seed)
        ks = jax.random.split(key, 9)
        scale = 0.05
        return {'x': jax.random.normal(ks[0], (B, S, D), dtype=jnp.float32), 'Wk': jax.random.normal(ks[1], (D, D), dtype=jnp.float32) * scale, 'Wq': jax.random.normal(ks[2], (D, D), dtype=jnp.float32) * scale, 'Wv': jax.random.normal(ks[3], (D, D), dtype=jnp.float32) * scale, 'Wlr': jax.random.normal(ks[4], (D, 1), dtype=jnp.float32) * scale, 'blr': jnp.zeros((1,), dtype=jnp.float32), 'Ws': jax.random.normal(ks[5], (L, D, D), dtype=jnp.float32) * scale, 'bs': jnp.zeros((L, D), dtype=jnp.float32)}
    _L0_attn_all = _L0_attn_setup()
    _L0_attn_in = {k: v for k, v in _L0_attn_all.items() if k in ('Wk', 'Wq', 'Wv', 'Wlr', 'blr', 'Ws', 'bs')}
    del _L0_attn_all

    def _L0_ffn_setup():
        import jax, jax.numpy as jnp
        import numpy as np
        D_MODEL = 64
        N_EXPERTS = 16
        HIDDEN = 128
        SCALE = 0.02
        key = jax.random.key(seed)
        ks = jax.random.split(key, 5)
        x = jax.random.normal(ks[0], (4, 2048, D_MODEL), dtype=jnp.float32)
        gate_w = jax.random.normal(ks[1], (D_MODEL, N_EXPERTS), dtype=jnp.float32) * SCALE
        gate_b = jnp.zeros((N_EXPERTS,), dtype=jnp.float32)
        w1 = jax.random.normal(ks[2], (N_EXPERTS, D_MODEL, HIDDEN), dtype=jnp.float32) * SCALE
        w2 = jax.random.normal(ks[3], (N_EXPERTS, D_MODEL, HIDDEN), dtype=jnp.float32) * SCALE
        w3 = jax.random.normal(ks[4], (N_EXPERTS, HIDDEN, D_MODEL), dtype=jnp.float32) * SCALE
        return {'x': x, 'gate_w': gate_w, 'gate_b': gate_b, 'w1': w1, 'w2': w2, 'w3': w3}
    _L0_ffn_all = _L0_ffn_setup()
    _L0_ffn_in = {k: v for k, v in _L0_ffn_all.items() if k in ('gate_w', 'gate_b', 'w1', 'w2', 'w3')}
    del _L0_ffn_all
    return {'x': x, 'L0_tok_W': _L0_tok_in['W'], 'L0_attn_Wk': _L0_attn_in['Wk'], 'L0_attn_Wq': _L0_attn_in['Wq'], 'L0_attn_Wv': _L0_attn_in['Wv'], 'L0_attn_Wlr': _L0_attn_in['Wlr'], 'L0_attn_blr': _L0_attn_in['blr'], 'L0_attn_Ws': _L0_attn_in['Ws'], 'L0_attn_bs': _L0_attn_in['bs'], 'L0_ffn_gate_w': _L0_ffn_in['gate_w'], 'L0_ffn_gate_b': _L0_ffn_in['gate_b'], 'L0_ffn_w1': _L0_ffn_in['w1'], 'L0_ffn_w2': _L0_ffn_in['w2'], 'L0_ffn_w3': _L0_ffn_in['w3']}

def reference(x, L0_tok_W, L0_attn_Wk, L0_attn_Wq, L0_attn_Wv, L0_attn_Wlr, L0_attn_blr, L0_attn_Ws, L0_attn_bs, L0_ffn_gate_w, L0_ffn_gate_b, L0_ffn_w1, L0_ffn_w2, L0_ffn_w3):
    import jax
    import jax.numpy as jnp

    def _L0_tok_ref(x, W):
        import jax, jax.numpy as jnp
        import numpy as np
        PATCH_LEN = 16
        STRIDE = 8
        PAD = 8
        B, C, T, V = x.shape
        xp = jnp.pad(x, ((0, 0), (0, 0), (0, PAD), (0, 0)), mode='edge')
        Tp = T + PAD
        N = (Tp - PATCH_LEN) // STRIDE + 1
        idx = jnp.arange(N)[:, None] * STRIDE + jnp.arange(PATCH_LEN)[None, :]
        patches = xp[:, :, idx, :]
        patches = jnp.transpose(patches, (0, 4, 2, 3, 1))
        xf = jnp.fft.rfft(patches, axis=-2, norm='ortho')
        F = xf.shape[-2]
        x_real = xf.real.reshape(B, V, N, F * C)
        x_imag = xf.imag.reshape(B, V, N, F * C)
        x_emb = jnp.concatenate([x_real, x_imag], axis=-1)
        x_emb = x_emb @ W.T
        return x_emb.reshape(B, V * N, -1)

    def _L0_attn_ref(x, Wk, Wq, Wv, Wlr, blr, Ws, bs):
        import jax, jax.numpy as jnp
        import numpy as np
        D = 64
        L = 2
        B, S = (8, 1024)
        LR = 0.001
        WD = 0.01
        MAX_ALR = 0.1
        EPS = 1e-08

        def _lmm(Ws, bs, x):
            for i in range(L):
                x = x + jax.nn.silu(x @ Ws[i] + bs[i])
            return x

        def _reference_tuple_inner(x, Wk, Wq, Wv, Wlr, blr, Ws, bs):
            keys = x @ Wk
            queries = x @ Wq
            values = x @ Wv
            alr = (jax.nn.sigmoid(x @ Wlr + blr) * MAX_ALR).reshape(-1)

            def loss_fn(params):
                Ws_, bs_ = params
                preds = _lmm(Ws_, bs_, keys).reshape(-1, D)
                tgt = values.reshape(-1, D)
                per_tok = jnp.mean((preds - tgt) ** 2, axis=-1)
                return jnp.sum(per_tok * alr)
            gWs, gbs = jax.grad(loss_fn)((Ws, bs))

            def adamw_step(p, g):
                return p * (1.0 - LR * WD) - LR * g / (jnp.sqrt(g * g) + EPS)
            nWs = adamw_step(Ws, gWs)
            nbs = adamw_step(bs, gbs)
            retrieved = _lmm(nWs, nbs, queries)
            return (retrieved, -gWs, -gbs)
        return _reference_tuple_inner(x, Wk, Wq, Wv, Wlr, blr, Ws, bs)[0]

    def _L0_ffn_ref(x, gate_w, gate_b, w1, w2, w3):
        import jax, jax.numpy as jnp
        import numpy as np
        D_MODEL = 64
        N_EXPERTS = 16
        HIDDEN = 128
        SCALE = 0.02
        n_experts = w1.shape[0]
        logits = jnp.einsum('bsd,de->bse', x, gate_w) + gate_b
        probs = jax.nn.softmax(logits, axis=-1)
        top_probs, top_idx = jax.lax.top_k(probs, 2)
        top_probs = top_probs / jnp.sum(top_probs, axis=-1, keepdims=True)
        dispatch = jnp.sum(jax.nn.one_hot(top_idx, n_experts, dtype=x.dtype) * top_probs[..., None], axis=-2)
        h1 = jnp.einsum('bsd,edh->bseh', x, w1)
        h2 = jnp.einsum('bsd,edh->bseh', x, w2)
        hidden = jax.nn.silu(h1) * h2
        expert_out = jnp.einsum('bseh,eho->bseo', hidden, w3)
        return jnp.einsum('bseo,bse->bso', expert_out, dispatch)
    h = _L0_tok_ref(x, L0_tok_W)
    h = h + _L0_attn_ref(_layernorm(h, axis=-1), L0_attn_Wk, L0_attn_Wq, L0_attn_Wv, L0_attn_Wlr, L0_attn_blr, L0_attn_Ws, L0_attn_bs)
    h = h + _L0_ffn_ref(_layernorm(h, axis=-1), L0_ffn_gate_w, L0_ffn_gate_b, L0_ffn_w1, L0_ffn_w2, L0_ffn_w3)
    return h

_drawn_inputs = setup_inputs


def setup_inputs(seed=0):
    import zlib

    import numpy as np

    out = dict(_drawn_inputs(seed))
    spreads = {'L0_attn_bs': (0.0, 0.1), 'L0_ffn_gate_b': (0.0, 0.8)}
    factors = {'L0_attn_Wk': 8.0,
     'L0_attn_Wv': 8.0,
     'L0_attn_Wlr': 8.0,
     'L0_ffn_gate_w': 8.0,
     'L0_ffn_w1': 8.0,
     'L0_ffn_w2': 8.0,
     'L0_ffn_w3': 8.0}
    for name, (base, spread) in spreads.items():
        noise = np.random.default_rng([zlib.crc32(name.encode()), seed]).standard_normal(out[name].shape)
        drawn = base * np.exp(spread * noise) if base else spread * noise
        out[name] = jnp.asarray(drawn.astype(out[name].dtype))
    for name, factor in factors.items():
        out[name] = (out[name] * factor).astype(out[name].dtype)
    return out
```

```python
import concourse.bass as bass
from concourse import mybir
from contextlib import ExitStack

F32 = mybir.dt.float32
F32R = mybir.dt.float32r
BF16 = mybir.dt.bfloat16
U32 = mybir.dt.uint32
ALU = mybir.AluOpType
ACT = mybir.ActivationFunctionType
AX = mybir.AxisListType

B, C, T, V = 16, 64, 128, 64
D = 64
LEN, STRIDE, NPATCH = 16, 8, 16
NF = LEN // 2 + 1
TOK = V * NPATCH
G = 2
PAIRS = B // G
CH = 512
BLK = CH // 128
NT = BLK * G
Q = 4
RP = STRIDE // Q
SLOTS = NPATCH // 2 + 1
NE, HID = 16, 128
PICKS = 2
LR, WD, EPS_ADAM, MAX_ALR, EPS_LN = 0.001, 0.01, 1e-8, 0.1, 1e-5
GRAD_SCALE = 0.5 * (MAX_ALR * 0.5) * (2.0 / D)

NTOK = B * TOK
ROW = 2 * D + 2
REGION = NTOK + 128
PAD_ROW = NE * REGION
NTILES = NTOK * PICKS // 128 + NE
GT = 4
NO_ROW = 1 << 30

_CONST = dict(ident=128, fold=128, tri=128, ids=2 * NT * PICKS, mask=NE * NT * PICKS, keys=NE, first=NE,
              incl=NE, tile=NTILES, dft=LEN)
CONST_AT, CONST_N = {}, 0
for _name, _n in _CONST.items():
    CONST_AT[_name] = (CONST_N, CONST_N + _n)
    CONST_N += _n


def constants():
    import numpy as np
    c = np.zeros((128, CONST_N), np.float32)

    def put(name, a):
        c[:a.shape[0], CONST_AT[name][0]:CONST_AT[name][1]] = a

    i = np.arange(128)
    put("ident", np.eye(128))
    put("fold", (i[:, None] % D == i[None, :] % D) * 1.0)
    put("tri", (i[:, None] < i[None, :]) * 1.0)
    n2, v = i // V, i % V
    ch, k, g, pk = np.meshgrid(np.arange(2), np.arange(BLK), np.arange(G), np.arange(PICKS), indexing="ij")
    tok = (g * TOK + ch * 8 + 2 * k).reshape(1, -1) + (v * NPATCH + n2)[:, None]
    put("ids", PICKS * tok + pk.reshape(1, -1))
    put("mask", np.tile((np.arange(NE * NT * PICKS) % (NT * PICKS) != 0) * 1.0, (128, 1)))
    put("keys", np.tile(NE - np.arange(NE) * 1.0, (128, 1)))
    put("first", np.tile(np.arange(NE) * float(REGION) - 1, (128, 1)))
    e = np.arange(NE)
    put("incl", (e[:, None] <= e[None, :]) * 1.0)
    put("tile", np.tile(np.arange(NTILES) * 1.0, (NE, 1)))
    f, t = np.arange(NF), np.arange(LEN)
    a = 2 * np.pi * f[:, None] * t[None, :] / LEN
    put("dft", np.concatenate([np.cos(a), -np.sin(a)]) / np.sqrt(LEN))
    return c


def vit_tower(nc, x, tok_W, Wk, Wq, Wv, Wlr, blr, Ws, bs, gate_w, gate_b, w1, w2, w3, consts, out, debug=None):
    xs = nc.dram_tensor("routed_rows", (PAD_ROW + 128, ROW), F32, kind="Internal").ap()
    ys = nc.dram_tensor("expert_rows", (NTOK * PICKS, D), F32, kind="Internal").ap()
    ctx = ExitStack()
    with ctx:
        def sb(name, shape, dt=F32, at=ctx):
            return at.enter_context(nc.sbuf_tensor(name, shape, dt))

        def sem(name):
            return ctx.enter_context(nc.semaphore(name))

        def ps(name, at, shape=(128, CH)):
            return at.enter_context(nc.psum_tensor(name, list(shape), F32))

        cst = sb("cst", [128, CONST_N])

        def const(name, rows=128):
            return cst[0:rows, CONST_AT[name][0]:CONST_AT[name][1]]

        ident, fold = const("ident"), const("fold")
        wkq = sb("wkq", [128, 7, 128])
        WK, WV, WA, W0, W1, W1T, WQ = range(7)
        bias = sb("bias", [128, 4])
        hbias = sb("hbias", [128, 4])
        H = sb("H", [128, PAIRS, 2, CH])
        X = sb("X", [128, PAIRS, 2, CH])
        grads = sb("grads", [128, 2, 128])
        zsum = sb("zsum", [128, 2, 2 * PAIRS])

        nW = sb("nW", [128, 2, 128])
        nb = sb("nb", [128, 2])
        env = dict(x=x, tok_W=tok_W, Wk=Wk, Wq=Wq, Wv=Wv, Wlr=Wlr, blr=blr, Ws=Ws, bs=bs, gate_w=gate_w, gate_b=gate_b,
                   w1=w1, w2=w2, w3=w3, consts=consts, out=out, xs=xs, ys=ys, cst=cst, ident=ident, fold=fold, wkq=wkq,
                   bias=bias, hbias=hbias, H=H, X=X, grads=grads, zsum=zsum, nW=nW, nb=nb)

        phase_a(nc, ctx, sb, sem, ps, const, env)
        phase_g(nc, ctx, sb, sem, ps, const, env)
        w12h = sb("w12h", [128, NE, 2 * HID], F32R)
        w12l = sb("w12l", [128, NE, 2 * HID], F32R)
        w3s = sb("w3s", [HID, (NE + 1) * D])
        carry = sb("carry", [128, NE])
        env.update(w12h=w12h, w12l=w12l, w3s=w3s, carry=carry)
        phase_b(nc, ctx, sb, sem, ps, const, env)
        phase_c(nc, ctx, sb, sem, ps, const, env)
        phase_d(nc, ctx, sb, sem, ps, const, env)
        if debug is not None:
            debug(nc, ctx, sb, sem, ps, env)


def phase_a(nc, ctx, sb, sem, ps, const, env):
    x, tok_W, Wk, Wq, Wv, Wlr, blr, Ws, bs, consts = (env[n] for n in "x tok_W Wk Wq Wv Wlr blr Ws bs consts".split())
    cst, ident, wkq, bias, hbias, H, X, grads, zsum = (env[n] for n in "cst ident wkq bias hbias H X grads zsum".split())
    WK, WV, WA, W0, W1, W1T, WQ = range(7)
    x_rows = x.rearrange("b c (m rp q) v -> b rp c m (q v)", rp=RP, q=Q)
    x_last = x.rearrange("b c t v -> b t c v")
    with ExitStack() as a:
        xb = sb("xb", [128, 2, G, SLOTS, Q * V], at=a)
        M = sb("M", [128, 2, Q, D], at=a)
        wlr = sb("wlr", [128, 1], at=a)

        def two(name):
            return sb(name, [128, 2, CH], at=a)

        hT, xt, sq, keys, s0, q0, x1, s1, q1, dd, tha, Z1, Z0, x1T, Z1T, Z0T = (two(n) for n in (
            "hT xt sq keys s0 q0 x1 s1 q1 dd tha Z1 Z0 x1T Z1T Z0T".split()))
        msum = sb("msum", [128, 2, NT], at=a)
        vsum = sb("vsum", [128, 2, NT], at=a)
        std = sb("std", [128, 2, NT], at=a)
        rstd = sb("rstd", [128, 2, NT], at=a)
        S = [ps(f"tok{c}", a) for c in range(2)]
        Bk = [[ps(f"chain{c}{i}", a) for i in range(2)] for c in range(2)]
        GB = ps("gradbank", a, (128, 2, 128))
        MB = ps("spare", a)

        c_in, w_in, w_in2, zeroed, m_ps, m_done, w_set, t_ps, wt_in = (
            sem("c_in"), sem("w_in"), sem("w_in2"), sem("zeroed"), sem("m_ps"), sem("m_done"), sem("w_set"), sem("t_ps"), sem("wt_in"))
        x_in = [sem("x_in0"), sem("x_in1")]
        s_tok = [sem("s_tok0"), sem("s_tok1")]
        names = ("hT Th Hs msum xc sq vs std rstd xt Tx X K keys z0 a0 p0 q0 x1 z1 a1 p1 q1 V A tha d1 d D Z1 dx E Z0 "
                 "Tx1 TZ1 TZ0 x1T Z1T Z0T g1 g0 gacc").split()
        s = {n: sem("s_" + n) for n in names}
        tw = X[0:2 * NF, 0:PAIRS, :, :].rearrange("p a b (o r c) -> p (a b o) r c", r=RP, c=C)
        tw_src = tok_W.rearrange("o (f c) -> f o c", c=C)
        dft = const("dft", 2 * NF)

        def load_half(q, it, half):
            for g in range(G):
                b = it * G + g
                n = SLOTS if half == 0 else SLOTS - 1
                for rp in range(RP):
                    q.dma_start(xb[rp * C:(rp + 1) * C, half, g, 0:n, :],
                                x_rows[bass.ds(b, 1), rp, :, half * 8:half * 8 + n, :]).then_inc(x_in[half], 16)
                    if half == 1:
                        q.dma_start(xb[rp * C:(rp + 1) * C, half, g, n, :].rearrange("p (q v) -> p q v", q=Q),
                                    x_last[bass.ds(b, 1), T - 1, :, :].rearrange("a c v -> c a v").to_broadcast([C, Q, V])
                                    ).then_inc(x_in[half], 16)

        per_half = [16 * G * RP, 32 * G * RP]

        with nc.Block() as block:

            @block.sync
            def _(sp):
                sp.dma_start(cst[:, :], consts[:, :]).then_inc(c_in, 16)
                for r in range(RP):
                    sp.dma_start(tw[:, :, r, :], tw_src).then_inc(wt_in, 16)
                load_half(sp, 0, 0)
                load_half(sp, 0, 1)
                with sp.Fori(0, PAIRS - 1, 1) as it:
                    for half in range(2):
                        sp.wait_ge(s_tok[half], it + 1)
                        load_half(sp, it + 1, half)

            @block.gpsimd
            def _(pool):
                for name in "x1 d".split():
                    pool.sem_inc(s[name], 1)
                pool.memset(wkq[:, :, :], 0.0).then_inc(zeroed, 1)
                pool.memset(bias[:, 3:4], EPS_LN).then_inc(zeroed, 1)
                with pool.Fori(0, PAIRS, 1) as it:
                    n = [pool.snap(it * 2 + 2), pool.snap(it * 2 + 3)]
                    old = pool.snap(it * 2 + 1)
                    for c in range(2):
                        pool.wait_ge(s["keys"], n[c])
                        pool.wait_ge(s["a0"], n[c])
                        pool.wait_ge(s["Tx1"], old)
                        pool.wait_ge(s["d1"], old)
                        pool.tensor_tensor(x1[:, c, :], keys[:, c, :], s0[:, c, :], ALU.add).then_inc(s["x1"], 1)
                    for c in range(2):
                        pool.wait_ge(s["d1"], n[c])
                        pool.wait_ge(s["a1"], n[c])
                        pool.tensor_tensor(dd[:, c, :], dd[:, c, :], s1[:, c, :], ALU.add).then_inc(s["d"], 1)

            @block.scalar
            def _(act):
                for name in "hT Hs sq std X keys a0 a1 tha x1T Z1T Z0T".split():
                    act.sem_inc(s[name], 1)
                act.wait_ge(zeroed, 2)
                for g in range(G):
                    r = slice(g * D, (g + 1) * D)
                    for k, w in ((WK, Wk), (WV, Wv), (WQ, Wq), (W0, Ws[0]), (W1, Ws[1])):
                        act.dma_start(wkq[r, k, r], w).then_inc(w_in, 16)
                    act.dma_start(wlr[r, :], Wlr).then_inc(w_in2, 16)
                    for l in range(2):
                        act.dma_start(bias[r, l:l + 1], bs[l, :].rearrange("(d a) -> d a", a=1)).then_inc(w_in2, 16)
                act.dma_start(bias[:, 2:3], blr.rearrange("(a n) -> a n", a=1).to_broadcast([128, 1])).then_inc(w_in2, 16)
                with act.Fori(0, PAIRS, 1) as it:
                    n = [act.snap(it * 2 + 2), act.snap(it * 2 + 3)]
                    one = act.snap(it + 2)
                    old = act.snap(it * 2 + 1)
                    for c in range(2):
                        act.wait_ge(s_tok[c], it + 1)
                        act.wait_ge(s["Th"], old)
                        act.activation(hT[:, c, :], S[c][:, :], ACT.Copy).then_inc(s["hT"], 1)
                    for c in range(2):
                        act.wait_ge(s["Th"], n[c])
                        if c == 0:
                            act.wait_ge(m_done, 2)
                        act.activation(H[:, bass.ds(it, 1), c, :], Bk[c][0][:, :], ACT.Copy).then_inc(s["Hs"], 1)
                    for c in range(2):
                        act.wait_ge(s["xc"], n[c])
                        act.wait_ge(s["vs"], old)
                        act.activation(sq[:, c, :], xt[:, c, :], ACT.Square).then_inc(s["sq"], 1)
                    act.wait_ge(s["vs"], n[1])
                    act.wait_ge(s["rstd"], it + 1)
                    act.activation(std[:, :, :], vsum[:, :, :], ACT.Sqrt, bias=bias[:, 3:4], scale=1.0 / D).then_inc(s["std"], 1)
                    for c in range(2):
                        act.wait_ge(s["Tx"], n[c])
                        act.activation(X[:, bass.ds(it, 1), c, :], Bk[c][1][:, :], ACT.Copy).then_inc(s["X"], 1)
                    for c in range(2):
                        act.wait_ge(s["K"], n[c])
                        act.wait_ge(s["z0"], old)
                        act.wait_ge(s["x1"], old)
                        act.activation(keys[:, c, :], Bk[c][0][:, :], ACT.Copy).then_inc(s["keys"], 1)
                    for c in range(2):
                        act.wait_ge(s["z0"], n[c])
                        act.wait_ge(s["q0"], old)
                        act.wait_ge(s["Z0"], old)
                        act.activation(s0[:, c, :], Bk[c][1][:, :], ACT.Silu, bias=bias[:, 0:1])
                        act.activation(q0[:, c, :], Bk[c][1][:, :], ACT.Tanh, bias=hbias[:, 0:1], scale=0.5).then_inc(s["a0"], 1)
                    for c in range(2):
                        act.wait_ge(s["z1"], n[c])
                        act.wait_ge(s["d"], old)
                        act.wait_ge(s["Z1"], old)
                        act.activation(s1[:, c, :], Bk[c][0][:, :], ACT.Silu, bias=bias[:, 1:2])
                        act.activation(q1[:, c, :], Bk[c][0][:, :], ACT.Tanh, bias=hbias[:, 1:2], scale=0.5).then_inc(s["a1"], 1)
                    for c in range(2):
                        act.wait_ge(s["A"], n[c])
                        act.wait_ge(s["D"], old)
                        act.activation(tha[:, c, :], Bk[c][0][:, :], ACT.Tanh, bias=hbias[:, 2:3], scale=0.5).then_inc(s["tha"], 1)
                    for name, src, dst, bank, used in (("x1T", "Tx1", x1T, 0, "g1"), ("Z1T", "TZ1", Z1T, 1, "g1"),
                                                       ("Z0T", "TZ0", Z0T, 0, "g0")):
                        for c in range(2):
                            act.wait_ge(s[src], n[c])
                            act.wait_ge(s[used], old)
                            act.activation(dst[:, c, :], Bk[c][bank][:, :], ACT.Copy).then_inc(s[name], 1)

            @block.vector
            def _(dve):
                for name in "msum xc vs rstd xt p0 q0 d1 p1 q1 D Z1 E Z0 gacc".split():
                    dve.sem_inc(s[name], 1)
                def bc(t):
                    return t.unsqueeze(2).to_broadcast([128, NT, D])

                def tiles(t):
                    return t.rearrange("p (t f) -> p t f", f=D)

                for oh in range(2):
                    dve.wait_ge(m_ps, oh + 1)
                    for r in range(RP):
                        rows = slice(r * C, (r + 1) * C)
                        src = (S[oh][rows, :] if oh < 2 else None).rearrange("p (o hh r q) -> p hh r q o", hh=2, r=RP, q=Q)
                        for hh in range(2):
                            i = dve.tensor_copy(M[rows, hh, :, oh * 32:(oh + 1) * 32], src[:, hh, r, :, :])
                    i.then_inc(m_done, 1)
                dve.wait_ge(w_in2, 16 * 7)
                dve.wait_ge(zeroed, 2)
                for g in range(G):
                    r = slice(g * D, (g + 1) * D)
                    dve.tensor_copy(wkq[r, WA, r], wlr[r, :].to_broadcast([D, D]))
                dve.tensor_scalar(hbias[:, :], bias[:, :], 0.5, None, ALU.mult).then_inc(w_set, 1)
                dve.wait_ge(t_ps, 1)
                dve.tensor_scalar(wkq[:, W1T, :], MB[:, 0:128], 0.5, None, ALU.mult).then_inc(w_set, 1)
                dve.memset(grads[:, :, :], 0.0).then_inc(s["gacc"], 1)
                with dve.Fori(0, PAIRS, 1) as it:
                    n = [dve.snap(it * 2 + 2), dve.snap(it * 2 + 3)]
                    old = dve.snap(it * 2 + 1)
                    one = dve.snap(it + 2)
                    for c in range(2):
                        h = tiles(H[:, bass.ds(it, 1), c, :].rearrange("p a n -> p (a n)"))
                        dve.wait_ge(s["Hs"], n[c])
                        dve.tensor_reduce(msum[:, c, :], h, AX.X, ALU.add).then_inc(s["msum"], 1)
                    for c in range(2):
                        h = tiles(H[:, bass.ds(it, 1), c, :].rearrange("p a n -> p (a n)"))
                        dve.wait_ge(s["msum"], n[c])
                        dve.wait_ge(s["g0"], old)
                        dve.scalar_tensor_tensor(tiles(xt[:, c, :]), bc(msum[:, c, :]), -1.0 / D, h, ALU.mult, ALU.add).then_inc(s["xc"], 1)
                    for c in range(2):
                        dve.wait_ge(s["sq"], n[c])
                        dve.wait_ge(s["std"], it + 1)
                        dve.tensor_reduce(vsum[:, c, :], tiles(sq[:, c, :]), AX.X, ALU.add).then_inc(s["vs"], 1)
                    dve.wait_ge(s["std"], one)
                    dve.reciprocal(rstd[:, :, :], std[:, :, :]).then_inc(s["rstd"], 1)
                    dve.wait_ge(s["rstd"], one)
                    for c in range(2):
                        dve.tensor_tensor(tiles(xt[:, c, :]), tiles(xt[:, c, :]), bc(rstd[:, c, :]), ALU.mult).then_inc(s["xt"], 1)

                    def slopes(sl, th, ready, p, q):
                        for c in range(2):
                            dve.wait_ge(s[ready], n[c])
                            dve.scalar_tensor_tensor(th[:, c, :], sl[:, c, :], -1.0, th[:, c, :], ALU.add, ALU.mult).then_inc(s[p], 1)
                        for c in range(2):
                            dve.wait_ge(s[p], n[c])
                            dve.scalar_tensor_tensor(th[:, c, :], sl[:, c, :], 1.0, th[:, c, :], ALU.add, ALU.subtract).then_inc(s[q], 1)

                    slopes(s0, q0, "a0", "p0", "q0")
                    for c in range(2):
                        dve.wait_ge(s["V"], n[c])
                        dve.wait_ge(s["x1"], n[c])
                        dve.wait_ge(s["Z1"], old)
                        dve.tensor_tensor(dd[:, c, :], x1[:, c, :], Bk[c][1][:, :], ALU.subtract).then_inc(s["d1"], 1)
                    slopes(s1, q1, "a1", "p1", "q1")
                    for c in range(2):
                        dve.wait_ge(s["tha"], n[c])
                        dve.wait_ge(s["d"], n[c])
                        dve.scalar_tensor_tensor(dd[:, c, :], tha[:, c, :], 1.0, dd[:, c, :], ALU.add, ALU.mult).then_inc(s["D"], 1)
                    for c in range(2):
                        dve.wait_ge(s["D"], n[c])
                        dve.wait_ge(s["q1"], n[c])
                        dve.wait_ge(s["TZ1"], old)
                        dve.scalar_tensor_tensor(Z1[:, c, :], q1[:, c, :], 1.0, dd[:, c, :], ALU.mult, ALU.mult,
                                                 accum_out=zsum[:, 0, bass.ds(it * 2 + c, 1)]).then_inc(s["Z1"], 1)
                    for c in range(2):
                        dve.wait_ge(s["dx"], n[c])
                        dve.wait_ge(s["TZ0"], old)
                        dve.tensor_tensor(Z0[:, c, :], dd[:, c, :], Bk[c][1][:, :], ALU.add).then_inc(s["E"], 1)
                    for c in range(2):
                        dve.wait_ge(s["E"], n[c])
                        dve.scalar_tensor_tensor(Z0[:, c, :], q0[:, c, :], 1.0, Z0[:, c, :], ALU.mult, ALU.mult,
                                                 accum_out=zsum[:, 1, bass.ds(it * 2 + c, 1)]).then_inc(s["Z0"], 1)
                    dve.wait_ge(s["g0"], n[1])
                    dve.wait_ge(s["gacc"], one)
                    dve.tensor_tensor(grads[:, :, :], grads[:, :, :], GB[:, :, :], ALU.add).then_inc(s["gacc"], 1)

            @block.tensor
            def _(pe):
                for name in "Th Tx K z0 z1 V A dx Tx1 TZ1 TZ0 g1 g0".split():
                    pe.sem_inc(s[name], 1)
                def stage1(half):
                    for hh in range(2):
                        for q in range(Q):
                            for g in range(G):
                                last = pe.matmul(S[half][g * D:(g + 1) * D, :].rearrange("p (m v) -> p m v", v=V), M[:, hh, q, :],
                                                 xb[:, half, g, hh:hh + 8, q * V:(q + 1) * V],
                                                 start=(hh == 0 and q == 0), stop=(hh == 1 and q == Q - 1))
                            if hh == 1 and q == Q - 1:
                                last.then_inc(s_tok[half], 1)
                            yield

                pe.wait_ge(c_in, 16)
                pe.wait_ge(wt_in, 16 * RP)
                for o in range(D):
                    last = pe.matmul(S[o // 32][:, (o % 32) * LEN:(o % 32 + 1) * LEN], tw[:, o, :, :], dft,
                                     start=True, stop=True)
                    if o % 32 == 31:
                        last.then_inc(m_ps, 1)
                pe.wait_ge(w_in, 16 * 10)
                pe.transpose(MB[:, 0:128], wkq[:, W1, :], ident).then_inc(t_ps, 1)
                pe.wait_ge(m_done, 2)
                for half in range(2):
                    pe.wait_ge(x_in[half], per_half[half])
                    for _ in stage1(half):
                        pass
                pe.wait_ge(w_set, 2)

                def transposes(c, bank, src):
                    for k in range(BLK):
                        last = pe.transpose(Bk[c][bank][:, k * 128:(k + 1) * 128], src[:, c, k * 128:(k + 1) * 128], ident)
                    return last

                def body(it, more):
                    n = [pe.snap(it * 2 + 2), pe.snap(it * 2 + 3)] if more else [it * 2 + 2, it * 2 + 3]
                    old = pe.snap(it * 2 + 1) if more else it * 2 + 1

                    def mm(c, bank, w, mov):
                        return pe.matmul(Bk[c][bank][:, :], wkq[:, w, :], mov, start=True, stop=True)

                    def xk(c):
                        return X[:, bass.ds(it, 1), c, :].rearrange("p a n -> p (a n)")

                    def t_h(c):
                        pe.wait_ge(s["hT"], n[c])
                        pe.wait_ge(s["Z0T"], old)
                        transposes(c, 0, hT).then_inc(s["Th"], 1)

                    def t_x(c):
                        pe.wait_ge(s["xt"], n[c])
                        transposes(c, 1, xt).then_inc(s["Tx"], 1)

                    def k_(c):
                        pe.wait_ge(s["X"], n[c])
                        mm(c, 0, WK, xk(c)).then_inc(s["K"], 1)

                    def z_0(c):
                        pe.wait_ge(s["keys"], n[c])
                        mm(c, 1, W0, keys[:, c, :]).then_inc(s["z0"], 1)

                    def z_1(c):
                        pe.wait_ge(s["x1"], n[c])
                        mm(c, 0, W1, x1[:, c, :]).then_inc(s["z1"], 1)

                    def v_(c):
                        pe.wait_ge(s["a0"], n[c])
                        mm(c, 1, WV, xk(c)).then_inc(s["V"], 1)

                    def a_(c):
                        pe.wait_ge(s["a1"], n[c])
                        mm(c, 0, WA, xk(c)).then_inc(s["A"], 1)

                    def dx(c):
                        pe.wait_ge(s["Z1"], n[c])
                        mm(c, 1, W1T, Z1[:, c, :]).then_inc(s["dx"], 1)

                    def t_x1(c):
                        pe.wait_ge(s["tha"], n[c])
                        transposes(c, 0, x1).then_inc(s["Tx1"], 1)

                    def t_z1(c):
                        pe.wait_ge(s["E"], n[c])
                        transposes(c, 1, Z1).then_inc(s["TZ1"], 1)

                    def t_z0(c):
                        pe.wait_ge(s["Z0"], n[c])
                        pe.wait_ge(s["x1T"], n[c])
                        transposes(c, 0, Z0).then_inc(s["TZ0"], 1)

                    def grad(c, slot, lhs, rhs, name):
                        for k in range(BLK):
                            cols = slice(k * 128, (k + 1) * 128)
                            last = pe.matmul(GB[:, slot, :], lhs[:, c, cols], rhs[:, c, cols],
                                             start=(c == 0 and k == 0), stop=(c == 1 and k == BLK - 1))
                        last.then_inc(s[name], 1)

                    def g_1(c):
                        pe.wait_ge(s["x1T"], n[c])
                        pe.wait_ge(s["Z1T"], n[c])
                        pe.wait_ge(s["gacc"], pe.snap(it + 2) if more else it + 2)
                        grad(c, 0, x1T, Z1T, "g1")

                    def g_0(c):
                        pe.wait_ge(s["Z0T"], n[c])
                        grad(c, 1, xt, Z0T, "g0")

                    steps = [t_h, t_x, k_, z_0, z_1, v_, a_, dx, t_x1, t_z1, t_z0, g_1, g_0]
                    fill = iter(())
                    for i, step in enumerate(steps):
                        for c in range(2):
                            step(c)
                            if more and i == 0 and c == 1:
                                pe.wait_ge(x_in[0], (it + 2) * per_half[0])
                                fill = stage1(0)
                            if more and i == 6 and c == 0:
                                for _ in fill:
                                    pass
                                pe.wait_ge(x_in[1], (it + 2) * per_half[1])
                                fill = stage1(1)
                            next(fill, None)
                    for _ in fill:
                        pass

                with pe.Fori(0, PAIRS - 1, 1) as it:
                    body(it, True)
                body(PAIRS - 1, False)


def phase_g(nc, ctx, sb, sem, ps, const, env):
    wkq, bias, grads, zsum, fold, nW, nb = (env[n] for n in "wkq bias grads zsum fold nW nb".split())
    WK, W0, W1 = 0, 3, 4
    with ExitStack() as a:
        pack = sb("pack", [128, 2, D + 1], at=a)
        x0 = sb("gx0", [128, D], at=a)
        gr = sb("gr", [128, 2, D + 1], at=a)
        par = sb("par", [128, 2, D + 1], at=a)
        den = sb("den", [128, 2, D + 1], at=a)
        sgn = sb("sgn", [128, 2, D + 1], at=a)
        P = ps("gfold", a, (128, 2, D + 1))
        P2 = ps("gw0", a, (128, D))
        v, p_, z = sem("g_vec"), sem("g_pe"), sem("g_zero")
        with nc.Block() as block:
            @block.gpsimd
            def _(pool):
                pool.memset(nW[:, :, :], 0.0).then_inc(z, 1)

            @block.tensor
            def _(pe):
                pe.wait_ge(v, 1)
                pe.matmul(P[:, :, :], fold, pack[:, :, :], start=True, stop=True).then_inc(p_, 1)
                pe.wait_ge(v, 2)
                pe.matmul(P2[:, :], wkq[:, WK, :], x0[:, :], start=True, stop=True).then_inc(p_, 1)

            @block.vector
            def _(dve):
                for g in range(G):
                    r = slice(g * D, (g + 1) * D)
                    dve.tensor_copy(pack[r, 0, 0:D], grads[r, 1, r])
                    dve.tensor_copy(pack[r, 1, 0:D], grads[r, 0, r])
                    for l, w in ((0, W0), (1, W1)):
                        dve.tensor_copy(par[r, l, 0:D], wkq[r, w, r])
                dve.tensor_copy(par[:, :, D:D + 1], bias[:, 0:2].unsqueeze(2))
                dve.tensor_reduce(pack[:, 0, D:D + 1], zsum[:, 1, :], AX.X, ALU.add)
                dve.tensor_reduce(pack[:, 1, D:D + 1], zsum[:, 0, :], AX.X, ALU.add).then_inc(v, 1)
                dve.wait_ge(p_, 1)
                dve.tensor_copy(x0[:, :], P[:, 0, 0:D]).then_inc(v, 1)
                dve.tensor_scalar(gr[:, 1, :], P[:, 1, :], GRAD_SCALE, None, ALU.mult)
                dve.tensor_scalar(gr[:, 0, D:D + 1], P[:, 0, D:D + 1], GRAD_SCALE, None, ALU.mult)
                dve.wait_ge(p_, 2)
                dve.tensor_scalar(gr[:, 0, 0:D], P2[:, :], GRAD_SCALE, None, ALU.mult).then_inc(v, 1)
                dve.wait_ge(v, 3)
                dve.scalar_tensor_tensor(sgn[:, :, :], gr[:, :, :], -1.0, gr[:, :, :], ALU.mult, ALU.max).then_inc(v, 1)
                dve.wait_ge(v, 4)
                dve.tensor_scalar(den[:, :, :], sgn[:, :, :], EPS_ADAM, None, ALU.add).then_inc(v, 1)
                dve.wait_ge(v, 5)
                dve.reciprocal(sgn[:, :, :], den[:, :, :]).then_inc(v, 1)
                dve.wait_ge(v, 6)
                dve.scalar_tensor_tensor(den[:, :, :], sgn[:, :, :], -LR, gr[:, :, :], ALU.mult, ALU.mult).then_inc(v, 1)
                dve.wait_ge(v, 7)
                dve.wait_ge(z, 1)
                for g in range(G):
                    r = slice(g * D, (g + 1) * D)
                    dve.scalar_tensor_tensor(nW[r, :, r], par[r, :, 0:D], 1.0 - LR * WD, den[r, :, 0:D], ALU.mult, ALU.add)
                dve.scalar_tensor_tensor(nb[:, :].unsqueeze(2), par[:, :, D:D + 1], 1.0 - LR * WD, den[:, :, D:D + 1],
                                         ALU.mult, ALU.add).then_inc(v, 1)


def phase_b(nc, ctx, sb, sem, ps, const, env):
    wkq, H, X, nW, nb, bias, ident, xs, w12h, w12l, w3s, carry = (env[n] for n in
        "wkq H X nW nb bias ident xs w12h w12l w3s carry".split())
    WQ = 6
    J = NT * PICKS
    with ExitStack() as a:
        def two(name, n=CH):
            return sb(name, [128, 2, n], at=a)

        w12 = sb("w12", [128, NE, 2 * HID], at=a)
        wg = sb("wg", [128, 2 * NE], at=a)
        gb = sb("gb", [128, NE], at=a)
        tri = sb("tri", [128, 128], BF16, at=a)
        ones = sb("ones", [128, 128], BF16, at=a)
        cnt = sb("cnt", [128, 2, NE], BF16, at=a)
        q, s0, x1, s1, r, xt, sq, x2 = (two(n) for n in "bq bs0 bx1 bs1 br bxt bsq bx2".split())
        rows = [sb(f"rows{c}", [128, PICKS, NT, ROW], at=a) for c in range(2)]
        msum, vsum, std, rstd, m1, m2, dm, th, km = (two(n, NT) for n in "bm bv bstd brstd bm1 bm2 bdm bth bkm".split())
        L, ge = (two(n, NT * NE) for n in "bL bge".split())
        OH, SC, SL = (two(n, NE * J) for n in "bOH bSC bSL".split())
        base = two("bbase", NE)
        slotf = two("bslotf", J)
        slot = sb("bslot", [128, 2, J], U32, at=a)
        ids = sb("bids", [128, 2 * J], at=a)
        Bk = [[ps(f"bchain{c}{i}", a) for i in range(2)] for c in range(2)]
        RK = [ps(f"brank{c}", a, (128, 2, NE)) for c in range(2)]
        w_in, w_in2, z, z2, v0 = sem("bw_in"), sem("bw_in2"), sem("b_zero"), sem("b_gate_in"), sem("b_set")
        s = {n: sem("b_" + n) for n in ("Q q z0 s0 z1 s1 T h2 sq std hi x2 Tx x2T LG th cnt RK slot half2 w_hi v go go_sum".split())}
        sent = [sem("b_sent0"), sem("b_sent1")]
        free = [sem("b_free0"), sem("b_free1")]
        keys, mask, first = const("keys"), const("mask"), const("first")

        with nc.Block() as block:

            @block.sync
            def _(sp):
                for g in range(G):
                    rs = slice(g * D, (g + 1) * D)
                    for k, w in ((0, env["w1"]), (1, env["w2"])):
                        sp.dma_start(w12[rs, :, k * HID:(k + 1) * HID], w.rearrange("e d h -> d e h")).then_inc(w_in, 16)
                sp.dma_start(gb[:, :], env["gate_b"].rearrange("(a n) -> a n", a=1).to_broadcast([128, NE])).then_inc(w_in2, 16)
                sp.wait_ge(z, 1)
                for g in range(G):
                    sp.dma_start(wg[g * D:(g + 1) * D, g * NE:(g + 1) * NE], env["gate_w"]).then_inc(z2, 16)
                sp.dma_start(w3s[:, 0:NE * D].rearrange("h (e o) -> h e o", o=D), env["w3"].rearrange("e h o -> h e o")).then_inc(w_in2, 16)
                for c in range(2):
                    sp.sem_inc(free[c], 1)
                with sp.Fori(0, PAIRS, 1) as it:
                    for c in range(2):
                        sp.wait_ge(sent[c], (it + 1) * (16 * J))
                        sp.sem_inc(free[c], 1)

            @block.gpsimd
            def _(pool):
                pool.memset(wg[:, :], 0.0).then_inc(z, 1)
                pool.memset(w3s[:, NE * D:], 0.0).then_inc(z, 1)
                pool.memset(ones[:, :], 1.0).then_inc(z, 1)
                with pool.Fori(0, PAIRS, 1) as it:
                    n = [pool.snap(it * 2 + 2), pool.snap(it * 2 + 3)]
                    for c in range(2):
                        pool.wait_ge(s["slot"], n[c])
                        pool.wait_ge(s["half2"], n[c])
                        pool.sem_inc(s["go"], 1)
                        for t in range(NT):
                            for k in range(PICKS):
                                pool.indirect_dma_start(
                                    out=xs, out_offset=bass.IndirectOffsetOnAxis(ap=slot[:, c, t * PICKS + k:t * PICKS + k + 1], axis=0),
                                    in_=rows[c][:, k, t, :], in_offset=None).then_inc(sent[c], 16)
                for c in range(2):
                    pool.wait_ge(sent[c], 16 * J * PAIRS)

            @block.scalar
            def _(act):
                for name in "q s0 s1 sq std x2T half2 th w_hi".split():
                    act.sem_inc(s[name], 1)
                act.wait_ge(w_in, 16 * 2 * G)
                with act.Fori(0, PAIRS, 1) as it:
                    n = [act.snap(it * 2 + 2), act.snap(it * 2 + 3)]
                    old = act.snap(it * 2 + 1)
                    for c in range(2):
                        act.wait_ge(s["Q"], n[c])
                        act.wait_ge(s["s0"], old)
                        act.activation(q[:, c, :], Bk[c][0][:, :], ACT.Copy).then_inc(s["q"], 1)
                    act.activation(w12h[:, bass.ds(it * 2, 2), :], w12[:, bass.ds(it * 2, 2), :], ACT.Copy).then_inc(s["w_hi"], 1)
                    for c in range(2):
                        act.wait_ge(s["z0"], n[c])
                        act.wait_ge(s["v"], it * K + 1)
                        act.activation(s0[:, c, :], Bk[c][1][:, :], ACT.Silu, bias=nb[:, 0:1]).then_inc(s["s0"], 1)
                    for c in range(2):
                        act.wait_ge(s["z1"], n[c])
                        act.activation(s1[:, c, :], Bk[c][0][:, :], ACT.Silu, bias=nb[:, 1:2]).then_inc(s["s1"], 1)
                    for c in range(2):
                        act.wait_ge(s["v"], it * K + 1 + AT["xc"][c])
                        act.activation(sq[:, c, :], xt[:, c, :], ACT.Square).then_inc(s["sq"], 1)
                    act.wait_ge(s["v"], it * K + 1 + AT["vsum"][1])
                    act.activation(std[:, :, :], vsum[:, :, :], ACT.Sqrt, bias=bias[:, 3:4], scale=1.0 / D).then_inc(s["std"], 1)
                    for c in range(2):
                        act.wait_ge(s["Tx"], n[c])
                        act.wait_ge(s["LG"], old)
                        act.activation(x2[:, c, :], Bk[c][0][:, :], ACT.Copy).then_inc(s["x2T"], 1)
                    for c in range(2):
                        act.wait_ge(s["v"], it * K + 1 + AT["lo"][c])
                        act.wait_ge(free[c], it + 1)
                        act.activation(rows[c][:, 1, :, 0:2 * D], rows[c][:, 0, :, 0:2 * D], ACT.Copy).then_inc(s["half2"], 1)
                    for c in range(2):
                        act.wait_ge(s["v"], it * K + 1 + AT["dm"][c])
                        act.activation(th[:, c, :], dm[:, c, :], ACT.Tanh, scale=0.5).then_inc(s["th"], 1)

            @block.vector
            def _(dve):
                for name in "v slot".split():
                    dve.sem_inc(s[name], 1)
                def bc(t, n=D):
                    return t.unsqueeze(2).to_broadcast([128, NT, n])

                def per_e(t):
                    return t.unsqueeze(1).to_broadcast([128, NT, NE])

                def tiles(t, f=D):
                    return t.rearrange("p (t f) -> p t f", f=f)

                dve.wait_ge(z, 3)
                dve.tensor_copy(tri[:, :], const("tri"))
                dve.tensor_copy(ids[:, :], const("ids"))
                dve.tensor_copy(carry[:, :], first).then_inc(v0, 1)
                dve.wait_ge(v0, 1)
                dve.wait_ge(w_in2, 32)
                with dve.Fori(0, PAIRS, 1) as it:
                    n = [dve.snap(it * 2 + 2), dve.snap(it * 2 + 3)]
                    done = dve.snap(it * K + 1)

                    def step(name, c, ins):
                        assert AT[name][c] == step.count + 1, (name, c, step.count)
                        step.count += 1
                        ins.then_inc(s["v"], 1)

                    step.count = 0

                    def after(name, c):
                        dve.wait_ge(s["v"], done + AT[name][c])

                    for c in range(2):
                        dve.wait_ge(s["q"], n[c])
                        dve.wait_ge(s["s0"], n[c])
                        step("x1", c, dve.tensor_tensor(x1[:, c, :], q[:, c, :], s0[:, c, :], ALU.add))
                    dve.wait_ge(s["w_hi"], it + 2)
                    for c in range(2):
                        e = bass.ds(it * 2 + c, 1)
                        step("wlo", c, dve.tensor_tensor(w12l[:, e, :], w12[:, e, :], w12h[:, e, :].bitcast(F32), ALU.subtract))
                    for c in range(2):
                        dve.wait_ge(s["s1"], n[c])
                        step("r", c, dve.tensor_tensor(r[:, c, :], x1[:, c, :], s1[:, c, :], ALU.add))

                    def Hc(c):
                        return H[:, bass.ds(it, 1), c, :].rearrange("p a n -> p (a n)")

                    for c in range(2):
                        dve.wait_ge(s["T"], n[c])
                        step("h2", c, dve.tensor_tensor(Hc(c), Hc(c), Bk[c][1][:, :], ALU.add))
                    for c in range(2):
                        after("h2", c)
                        dve.sem_inc(s["go_sum"], 1)
                        step("msum", c, dve.tensor_reduce(msum[:, c, :], tiles(Hc(c)), AX.X, ALU.add))
                    for c in range(2):
                        after("msum", c)
                        step("xc", c, dve.scalar_tensor_tensor(tiles(xt[:, c, :]), bc(msum[:, c, :]), -1.0 / D, tiles(Hc(c)), ALU.mult, ALU.add))
                    for c in range(2):
                        dve.wait_ge(s["sq"], n[c])
                        step("vsum", c, dve.tensor_reduce(vsum[:, c, :], tiles(sq[:, c, :]), AX.X, ALU.add))
                    dve.wait_ge(s["std"], it + 2)
                    for c in range(2):
                        step("rstd", c, dve.reciprocal(rstd[:, c, :], std[:, c, :]))
                    for c in range(2):
                        after("rstd", c)
                        step("x2", c, dve.tensor_tensor(tiles(xt[:, c, :]), tiles(xt[:, c, :]), bc(rstd[:, c, :]), ALU.mult))
                    for c in range(2):
                        after("x2", c)
                        dve.wait_ge(free[c], it + 1)
                        step("hi", c, dve.tensor_copy(rows[c][:, 0, :, 0:D].bitcast(F32R), tiles(xt[:, c, :])))
                    for c in range(2):
                        after("hi", c)
                        step("lo", c, dve.tensor_tensor(rows[c][:, 0, :, D:2 * D], tiles(xt[:, c, :]), rows[c][:, 0, :, 0:D], ALU.subtract))
                    for c in range(2):
                        dve.wait_ge(s["LG"], n[c])
                        step("L", c, dve.tensor_tensor(tiles(L[:, c, :], NE), tiles(Bk[c][1][:, 0:NT * NE], NE), per_e(gb[:, :]), ALU.add))
                    for pick, m in ((0, m1), (1, m2)):
                        p = f"p{pick}"
                        for c in range(2):
                            after("L" if pick == 0 else "L2", c)
                            step(p + "m", c, dve.tensor_reduce(m[:, c, :], tiles(L[:, c, :], NE), AX.X, ALU.max))
                        for c in range(2):
                            after(p + "m", c)
                            step(p + "ge", c, dve.tensor_tensor(tiles(ge[:, c, :], NE), tiles(L[:, c, :], NE), bc(m[:, c, :], NE), ALU.is_equal))
                        for c in range(2):
                            after(p + "ge", c)
                            step(p + "key", c, dve.tensor_tensor(tiles(ge[:, c, :], NE), tiles(ge[:, c, :], NE), per_e(keys), ALU.mult))
                        for c in range(2):
                            after(p + "key", c)
                            step(p + "km", c, dve.tensor_reduce(km[:, c, :], tiles(ge[:, c, :], NE), AX.X, ALU.max))
                        for c in range(2):
                            after(p + "km", c)
                            oh = OH[:, c, :].rearrange("p (e t k) -> p k t e", e=NE, k=PICKS)[:, pick]
                            step(p + "oh", c, dve.tensor_tensor(oh, tiles(ge[:, c, :], NE), bc(km[:, c, :], NE), ALU.is_equal))
                        if pick == 0:
                            for c in range(2):
                                after(p + "oh", c)
                                oh = OH[:, c, :].rearrange("p (e t k) -> p k t e", e=NE, k=PICKS)[:, 0]
                                step("L2", c, dve.scalar_tensor_tensor(tiles(L[:, c, :], NE), oh, -3.0e38, tiles(L[:, c, :], NE), ALU.mult, ALU.add))
                    for c in range(2):
                        after("p1m", c)
                        step("dm", c, dve.tensor_tensor(dm[:, c, :], m1[:, c, :], m2[:, c, :], ALU.subtract))
                    for c in range(2):
                        after("p1oh", c)
                        step("scan", c, dve.tensor_tensor_scan(SC[:, c, :], mask, OH[:, c, :], 0.0, ALU.mult, ALU.add))
                    for c in range(2):
                        after("scan", c)
                        step("cnt", c, dve.tensor_copy(cnt[:, c, :], SC[:, c, :].rearrange("p (e j) -> p e j", j=J)[:, :, J - 1]))
                    for c in range(2):
                        dve.wait_ge(s["th"], n[c])
                        step("wt1", c, dve.tensor_scalar(rows[c][:, 0, :, 2 * D], th[:, c, :], 0.5, 0.5, ALU.mult, ALU.add))
                    for c in range(2):
                        dve.wait_ge(s["half2"], n[c])
                        step("wt2", c, dve.tensor_scalar(rows[c][:, 1, :, 2 * D], th[:, c, :], -0.5, 0.5, ALU.mult, ALU.add))
                    for c in range(2):
                        step("id", c, dve.tensor_copy(rows[c][:, :, :, 2 * D + 1].bitcast(U32),
                                                      ids[:, c * J:(c + 1) * J].rearrange("p (t k) -> p k t", k=PICKS)))
                    for c in range(2):
                        dve.wait_ge(s["RK"], n[c])
                        if c:
                            after("carry", 0)
                        step("base", c, dve.tensor_tensor(base[:, c, :], RK[c][:, 0, :], carry[:, :], ALU.add))
                        if c == 0:
                            after("base", 0)
                        else:
                            after("base", 1)
                        step("carry", c, dve.tensor_tensor(carry[:, :], RK[c][:, 1, :], carry[:, :], ALU.add))
                    for c in range(2):
                        ej = SC[:, c, :].rearrange("p (e j) -> p e j", j=J)
                        step("sl", c, dve.tensor_tensor(SL[:, c, :].rearrange("p (e j) -> p e j", j=J), ej,
                                                        base[:, c, :].unsqueeze(2).to_broadcast([128, NE, J]), ALU.add))
                    for c in range(2):
                        after("sl", c)
                        step("pick", c, dve.tensor_tensor(SL[:, c, :], SL[:, c, :], OH[:, c, :], ALU.mult))
                    for c in range(2):
                        after("pick", c)
                        step("slotf", c, dve.tensor_reduce(slotf[:, c, :], SL[:, c, :].rearrange("p (e j) -> p j e", j=J), AX.X, ALU.add))
                    for c in range(2):
                        after("slotf", c)
                        step("slot", c, dve.tensor_copy(slot[:, c, :], slotf[:, c, :]))
                    for c in range(2):
                        after("slot", c)
                        dve.tensor_scalar(ids[:, c * J:(c + 1) * J], ids[:, c * J:(c + 1) * J], float(PICKS * G * TOK), None,
                                          ALU.add).then_inc(s["slot"], 1)
                    dve.wait_ge(s["slot"], n[1])
                    assert step.count == K, step.count

            @block.tensor
            def _(pe):
                for name in "Q z0 z1 T Tx LG RK".split():
                    pe.sem_inc(s[name], 1)
                pe.wait_ge(v0, 1)
                pe.wait_ge(z2, 32)
                pe.wait_ge(z, 3)
                with pe.Fori(0, PAIRS, 1) as it:
                    n = [pe.snap(it * 2 + 2), pe.snap(it * 2 + 3)]
                    old = pe.snap(it * 2 + 1)
                    done = pe.snap(it * K + 1)
                    for c in range(2):
                        pe.wait_ge(s["x2T"], old)
                        pe.matmul(Bk[c][0][:, :], wkq[:, WQ, :], X[:, bass.ds(it, 1), c, :].rearrange("p a n -> p (a n)"),
                                  start=True, stop=True).then_inc(s["Q"], 1)
                    for c in range(2):
                        pe.wait_ge(s["q"], n[c])
                        pe.wait_ge(s["v"], done)
                        pe.matmul(Bk[c][1][:, :], nW[:, 0, :], q[:, c, :], start=True, stop=True).then_inc(s["z0"], 1)
                    for c in range(2):
                        pe.wait_ge(s["v"], done + AT["x1"][c])
                        pe.matmul(Bk[c][0][:, :], nW[:, 1, :], x1[:, c, :], start=True, stop=True).then_inc(s["z1"], 1)
                    for name, bank, src, ready in (("T", 1, r, "r"), ("Tx", 0, xt, "x2")):
                        for c in range(2):
                            pe.wait_ge(s["v"], done + AT[ready][c])
                            for k in range(BLK):
                                last = pe.transpose(Bk[c][bank][:, k * 128:(k + 1) * 128], src[:, c, k * 128:(k + 1) * 128], ident)
                            last.then_inc(s[name], 1)
                    for c in range(2):
                        pe.wait_ge(s["x2T"], n[c])
                        for k in range(BLK):
                            last = pe.matmul(Bk[c][1][:, k * 2 * NE:(k + 1) * 2 * NE], x2[:, c, k * 128:(k + 1) * 128], wg[:, :],
                                             start=True, stop=True)
                        last.then_inc(s["LG"], 1)
                    for c in range(2):
                        pe.wait_ge(s["v"], done + AT["cnt"][c])
                        pe.matmul(RK[c][:, 0, :], tri[:, :], cnt[:, c, :], start=True, stop=True)
                        pe.matmul(RK[c][:, 1, :], ones[:, :], cnt[:, c, :], start=True, stop=True).then_inc(s["RK"], 1)


_STEPS = ("x1 wlo r h2 msum xc vsum rstd x2 hi lo L p0m p0ge p0key p0km p0oh L2 p1m p1ge p1key p1km p1oh dm scan cnt "
          "wt1 wt2 id").split()
AT = {name: (2 * i + 1, 2 * i + 2) for i, name in enumerate(_STEPS)}
_N = 2 * len(_STEPS)
AT["base"], AT["carry"] = (_N + 1, _N + 3), (_N + 2, _N + 4)
for _i, _name in enumerate(("sl", "pick", "slotf", "slot")):
    AT[_name] = (_N + 5 + 2 * _i, _N + 6 + 2 * _i)
K = _N + 12


def phase_c(nc, ctx, sb, sem, ps, const, env):
    ident, xs, ys, w12h, w12l, w3s, carry = (env[n] for n in "ident xs ys w12h w12l w3s carry".split())
    GROUPS = NTILES // (2 * GT)
    with ExitStack() as a:
        pad = sb("pad", [128, ROW], at=a)
        xt = [sb(f"cx{c}", [128, GT, ROW], at=a) for c in range(2)]
        tag = [sb(f"ctag{c}", [128, GT, 2], at=a) for c in range(2)]
        xT = sb("cxT", [128, 2, GT * 128], F32R, at=a)
        gl, hid, hT = (sb(n, [128, 2, GT * HID], at=a) for n in ("cgl", "chid", "chT"))
        y = [sb(f"cy{c}", [128, GT, D], at=a) for c in range(2)]
        nf = sb("nf", [128, NE], at=a)
        nd = sb("nd", [NE, NE], at=a)
        ncol, nt, endc, both = (sb(n, [NE, w], at=a) for n, w in (("ncol", 1), ("ntl", 1), ("endc", 1), ("both", 2)))
        nu = sb("nu", [NE, 1], U32, at=a)
        GE = sb("GE", [NE, NTILES], at=a)
        xf = sb("xf", [1, NTILES], at=a)
        table = sb("table", [1, 2, NTILES], U32, at=a)
        padrow = sb("padrow", [1, NE], U32, at=a)
        E_, XR = 0, 1
        TP = [ps(f"ct{c}", a, (128, GT * 128)) for c in range(2)]
        HP = [ps(f"ch{c}", a, (128, GT, 2 * HID)) for c in range(2)]
        YP = [ps(f"cyp{c}", a, (128, GT, 128)) for c in range(2)]
        v, p_, z, pads, ef_done = sem("c_vec"), sem("c_pe"), sem("c_zero"), sem("c_pads"), sem("c_rowf")
        x_in = [sem("c_in0"), sem("c_in1")]
        y_out = [sem("c_out0"), sem("c_out1")]
        free = [sem("c_free0"), sem("c_free1")]
        s = {n: sem("c_" + n) for n in "T1 xT tag H gl hid T2 hT Y y go".split()}

        with nc.Block() as block:

            @block.sync
            def _(sp):
                sp.wait_ge(z, 2)
                sp.wait_ge(v, 2)
                sp.dma_start(xs[PAD_ROW:PAD_ROW + 128, :], pad[:, :]).then_inc(pads, 16)
                for e in range(NE):
                    row = sp.value_load(padrow[0:1, e:e + 1], min_val=0, max_val=PAD_ROW - 128)
                    sp.dma_start(xs[bass.ds(row, 128), :], pad[:, :]).then_inc(pads, 16)
                sp.wait_ge(pads, 16 * (NE + 1))
                sp.wait_ge(v, 10)

                def load(it, c):
                    for t in range(GT):
                        row = sp.value_load(table[0:1, XR, bass.ds(it * (2 * GT) + (c * GT + t), 1)], min_val=0, max_val=PAD_ROW)
                        sp.dma_start(xt[c][:, t, :], xs[bass.ds(row, 128), :]).then_inc(x_in[c], 16)

                for c in range(2):
                    load(0, c)
                    sp.sem_inc(free[c], 1)
                with sp.Fori(1, GROUPS, 1) as it:
                    for c in range(2):
                        sp.wait_ge(s["T1"], it * 2 + c)
                        sp.wait_ge(s["tag"], it * 2 + c)
                        load(it, c)
                    for c in range(2):
                        sp.wait_ge(y_out[c], it * (16 * GT))
                        sp.sem_inc(free[c], 1)

            @block.gpsimd
            def _(pool):
                pool.memset(pad[:, 0:2 * D + 1], 0.0).then_inc(z, 1)
                pool.memset(pad[:, 2 * D + 1:], 2.0).then_inc(z, 1)
                with pool.Fori(0, GROUPS, 1) as it:
                    for c in range(2):
                        pool.wait_ge(s["y"], it * 2 + (c + 2))
                        pool.sem_inc(s["go"], 1)
                        for t in range(GT):
                            pool.indirect_dma_start(
                                out=ys, out_offset=bass.IndirectOffsetOnAxis(ap=tag[c][:, t, 1:2].bitcast(U32), axis=0),
                                in_=y[c][:, t, :], in_offset=None, bounds_check=NTOK * PICKS - 1, oob_is_err=False).then_inc(y_out[c], 16)
                for c in range(2):
                    pool.wait_ge(y_out[c], 16 * GT * GROUPS)

            @block.scalar
            def _(act):
                for name in "xT gl hT".split():
                    act.sem_inc(s[name], 1)
                with act.Fori(0, GROUPS, 1) as it:
                    n = [act.snap(it * 2 + 2), act.snap(it * 2 + 3)]
                    old = act.snap(it * 2 + 1)
                    for c in range(2):
                        act.wait_ge(s["T1"], n[c])
                        act.wait_ge(s["H"], old)
                        act.activation(xT[:, c, :], TP[c][:, :], ACT.Copy).then_inc(s["xT"], 1)
                    for c in range(2):
                        act.wait_ge(s["H"], n[c])
                        act.wait_ge(s["hid"], old)
                        act.activation(gl[:, c, :].rearrange("p (t h) -> p t h", h=HID), HP[c][:, :, 0:HID], ACT.Silu).then_inc(s["gl"], 1)
                    for c in range(2):
                        act.wait_ge(s["T2"], n[c])
                        act.wait_ge(s["Y"], old)
                        act.activation(hT[:, c, :], TP[c][:, :], ACT.Copy).then_inc(s["hT"], 1)

            @block.vector
            def _(dve):
                for name in "tag hid y".split():
                    dve.sem_inc(s[name], 1)
                dve.tensor_scalar(padrow[:, :], carry[0:1, :], 1.0, None, ALU.add).then_inc(v, 1)
                dve.tensor_tensor(nf[:, :], carry[:, :], const("first"), ALU.subtract).then_inc(v, 1)
                dve.wait_ge(v, 2)
                dve.tensor_tensor(nd[:, :], nf[0:NE, :], ident[0:NE, 0:NE], ALU.mult).then_inc(v, 1)
                dve.wait_ge(v, 3)
                dve.tensor_reduce(ncol[:, :], nd[:, :], AX.X, ALU.add).then_inc(v, 1)
                dve.wait_ge(v, 4)
                dve.tensor_copy(nu[:, :], ncol[:, :]).then_inc(v, 1)
                dve.wait_ge(v, 5)
                dve.tensor_scalar(nu[:, :], nu[:, :], 7, None, ALU.logical_shift_right).then_inc(v, 1)
                dve.wait_ge(v, 6)
                dve.tensor_scalar(nt[:, :], nu[:, :], 1.0, None, ALU.add).then_inc(v, 1)
                dve.wait_ge(v, 7)
                dve.memset(both[:, 0:1], 1.0)
                dve.tensor_scalar(both[:, 1:2], nt[:, :], -128.0, float(REGION), ALU.mult, ALU.add)
                dve.wait_ge(p_, 1)
                dve.tensor_copy(endc[:, :], YP[0][0:NE, 0, 0:1]).then_inc(v, 1)
                dve.wait_ge(v, 8)
                dve.tensor_scalar(GE[:, :], const("tile", NE), endc[:, 0:1], None, ALU.is_ge).then_inc(v, 1)
                dve.wait_ge(p_, 2)
                dve.tensor_scalar(table[:, E_, :], TP[0][0:1, 0:NTILES], float(NE - 1), None, ALU.min)
                dve.scalar_tensor_tensor(xf[:, :], const("tile", 1), 128.0, TP[1][0:1, 0:NTILES], ALU.mult, ALU.add).then_inc(ef_done, 1)
                dve.wait_ge(ef_done, 1)
                dve.tensor_scalar(table[:, XR, :], xf[:, :], float(PAD_ROW), None, ALU.min).then_inc(v, 1)
                with dve.Fori(0, GROUPS, 1) as it:
                    n = [dve.snap(it * 2 + 2), dve.snap(it * 2 + 3)]
                    old = dve.snap(it * 2 + 1)
                    for c in range(2):
                        dve.wait_ge(x_in[c], (it + 1) * (16 * GT))
                        dve.wait_ge(free[c], it + 1)
                        dve.tensor_copy(tag[c][:, :, :].bitcast(U32), xt[c][:, :, 2 * D:].bitcast(U32)).then_inc(s["tag"], 1)
                    for c in range(2):
                        dve.wait_ge(s["gl"], n[c])
                        dve.wait_ge(s["T2"], old)
                        g = gl[:, c, :].rearrange("p (t h) -> p t h", h=HID)
                        dve.tensor_tensor(hid[:, c, :].rearrange("p (t h) -> p t h", h=HID), g, HP[c][:, :, HID:], ALU.mult).then_inc(s["hid"], 1)
                    for c in range(2):
                        dve.wait_ge(s["Y"], n[c])
                        dve.wait_ge(s["tag"], n[c])
                        dve.tensor_tensor(y[c][:, :, :], YP[c][:, :, 0:D], tag[c][:, :, 0:1].to_broadcast([128, GT, D]),
                                          ALU.mult).then_inc(s["y"], 1)

            @block.tensor
            def _(pe):
                for name in "T1 H T2 Y".split():
                    pe.sem_inc(s[name], 1)
                pe.wait_ge(v, 7)
                pe.matmul(YP[0][0:NE, 0, 0:1], const("incl", NE), nt[:, :], start=True, stop=True).then_inc(p_, 1)
                pe.wait_ge(v, 9)
                pe.matmul(TP[0][0:1, 0:NTILES], both[:, 0:1], GE[:, :], start=True, stop=True)
                pe.matmul(TP[1][0:1, 0:NTILES], both[:, 1:2], GE[:, :], start=True, stop=True).then_inc(p_, 1)
                pe.wait_ge(v, 10)
                with pe.Fori(0, GROUPS, 1) as it:
                    n = [pe.snap(it * 2 + 2), pe.snap(it * 2 + 3)]
                    old = pe.snap(it * 2 + 1)
                    for c in range(2):
                        pe.wait_ge(x_in[c], (it + 1) * (16 * GT))
                        pe.wait_ge(s["hT"], old)
                        for t in range(GT):
                            last = pe.transpose(TP[c][:, t * 128:(t + 1) * 128], xt[c][:, t, 0:2 * D], ident)
                        last.then_inc(s["T1"], 1)
                    es = []
                    for c in range(2):
                        pe.wait_ge(s["xT"], n[c])
                        pe.wait_ge(s["hid"], old)
                        es.append([])
                        for t in range(GT):
                            e = pe.value_load(table[0:1, E_, bass.ds(it * (2 * GT) + (c * GT + t), 1)], min_val=0, max_val=NE - 1)
                            es[c].append(e)
                            lhs = xT[:, c, t * 128:(t + 1) * 128]
                            pe.matmul(HP[c][:, t, :], lhs, w12h[:, bass.ds(e, 1), :].rearrange("p a n -> p (a n)"), start=True, stop=False)
                            last = pe.matmul(HP[c][:, t, :], lhs, w12l[:, bass.ds(e, 1), :].rearrange("p a n -> p (a n)"), start=False, stop=True)
                        last.then_inc(s["H"], 1)
                    for c in range(2):
                        pe.wait_ge(s["hid"], n[c])
                        for t in range(GT):
                            last = pe.transpose(TP[c][:, t * 128:(t + 1) * 128], hid[:, c, t * 128:(t + 1) * 128], ident)
                        last.then_inc(s["T2"], 1)
                    for c in range(2):
                        pe.wait_ge(s["hT"], n[c])
                        pe.wait_ge(s["y"], old)
                        for t in range(GT):
                            last = pe.matmul(YP[c][:, t, :], hT[:, c, t * 128:(t + 1) * 128], w3s[:, bass.ds(es[c][t] * D, 128)],
                                             start=True, stop=True)
                        last.then_inc(s["Y"], 1)


def phase_d(nc, ctx, sb, sem, ps, const, env):
    H, ys, out = env["H"], env["ys"], env["out"]
    y_v = ys.rearrange("(b v c k n2 p) f -> b c n2 v k (p f)", v=V, c=2, k=BLK, n2=2, p=PICKS)
    o_v = out.rearrange("b (v c k n2) f -> b c n2 v k f", v=V, c=2, k=BLK, n2=2)
    with ExitStack() as a:
        slots = [(par, c) for par in range(2) for c in range(2)]
        yb = {k: sb(f"yb{k[0]}{k[1]}", [128, G, BLK, PICKS, D], at=a) for k in slots}
        o = {k: sb(f"o{k[0]}{k[1]}", [128, BLK, G, D], at=a) for k in slots}
        y_in = {k: sem(f"d_in{k[0]}{k[1]}") for k in slots}
        o_out = {k: sem(f"d_out{k[0]}{k[1]}") for k in slots}
        part, summed = sem("d_part"), sem("d_sum")
        with nc.Block() as block:
            @block.sync
            def _(sp):
                with sp.Fori(0, PAIRS // 2, 1) as i:
                    for j, (par, c) in enumerate(slots):
                        sp.wait_ge(summed, i * 4 + 1)
                        for g in range(G):
                            b = bass.ds(i * 4 + (par * 2 + g), 1)
                            for n2 in range(2):
                                sp.dma_start(yb[par, c][n2 * V:(n2 + 1) * V, g].rearrange("v k p f -> v k (p f)"),
                                             y_v[b, c, n2, :, :, :]).then_inc(y_in[par, c], 16)

            @block.scalar
            def _(act):
                for k in slots:
                    act.sem_inc(o_out[k], 1)
                with act.Fori(0, PAIRS // 2, 1) as i:
                    for j, (par, c) in enumerate(slots):
                        act.wait_ge(summed, i * 4 + (j + 2))
                        for g in range(G):
                            b = bass.ds(i * 4 + (par * 2 + g), 1)
                            for n2 in range(2):
                                act.dma_start(o_v[b, c, n2, :, :, :], o[par, c][n2 * V:(n2 + 1) * V, :, g, :]).then_inc(o_out[par, c], 16)
                for k in slots:
                    act.wait_ge(o_out[k], 64 * (PAIRS // 2) + 1)

            @block.vector
            def _(dve):
                dve.sem_inc(summed, 1)
                with dve.Fori(0, PAIRS // 2, 1) as i:
                    for j, (par, c) in enumerate(slots):
                        h = H[:, bass.ds(i * 2 + par, 1), c, :].rearrange("p a (k g f) -> p (a k) g f", g=G, f=D)
                        yk = [yb[par, c][:, :, :, p, :].rearrange("p g k f -> p k g f") for p in range(PICKS)]
                        dve.wait_ge(y_in[par, c], (i + 1) * 64)
                        dve.wait_ge(o_out[par, c], i * 64 + 1)
                        dve.tensor_tensor(o[par, c][:, :, :, :], h, yk[0], ALU.add).then_inc(part, 1)
                        dve.wait_ge(part, i * 4 + (j + 1))
                        dve.tensor_tensor(o[par, c][:, :, :, :], o[par, c][:, :, :, :], yk[1], ALU.add).then_inc(summed, 1)


_INS = ["x", "L0_tok_W", "L0_attn_Wk", "L0_attn_Wq", "L0_attn_Wv", "L0_attn_Wlr", "L0_attn_blr", "L0_attn_Ws", "L0_attn_bs",
        "L0_ffn_gate_w", "L0_ffn_gate_b", "L0_ffn_w1", "L0_ffn_w2", "L0_ffn_w3"]


def kernel(**inputs):
    import numpy as _np
    import concourse.bacc as _bacc
    from concourse import mybir as _mybir
    from concourse.bass_utils import run_bass_kernel_spmd as _run

    nc = _bacc.Bacc("TRN2", target_bir_lowering=False, num_devices=1)
    arrays, args = {}, []
    for name in _INS:
        arrays[f"in_{name}_dram"] = _np.ascontiguousarray(inputs[name])
    arrays["in_consts_dram"] = constants()
    for name, a in arrays.items():
        args.append(nc.dram_tensor(name, a.shape, _mybir.dt.from_np(a.dtype), kind="ExternalInput").ap())
    out = nc.dram_tensor("out_0_dram", (B, TOK, D), _mybir.dt.float32, kind="ExternalOutput").ap()
    vit_tower(nc, *args, out)
    r = _run(nc, [arrays], core_ids=[0])
    return r.results[0]["out_0_dram"]
```

```python
import concourse.bass as bass
from concourse import mybir
from contextlib import ExitStack

F32 = mybir.dt.float32
F32R = mybir.dt.float32r
BF16 = mybir.dt.bfloat16
U32 = mybir.dt.uint32
ALU = mybir.AluOpType
ACT = mybir.ActivationFunctionType
AX = mybir.AxisListType

B, C, T, V = 16, 64, 128, 64
D = 64
LEN, STRIDE, NPATCH = 16, 8, 16
NF = LEN // 2 + 1
TOK = V * NPATCH
G = 2
PAIRS = B // G
CH = 512
BLK = CH // 128
NT = BLK * G
Q = 4
RP = STRIDE // Q
SLOTS = NPATCH // 2 + 1
NE, HID = 16, 128
PICKS = 2
LR, WD, EPS_ADAM, MAX_ALR, EPS_LN = 0.001, 0.01, 1e-8, 0.1, 1e-5
GRAD_SCALE = 0.5 * (MAX_ALR * 0.5) * (2.0 / D)

NTOK = B * TOK
ROW = 2 * D + 2
REGION = NTOK + 128
PAD_ROW = NE * REGION
NTILES = NTOK * PICKS // 128 + NE
GT = 4
GROUPS = NTILES // GT
DEPTH = 4
FIRST = 3
TURNS = (GROUPS - 2 - FIRST) // DEPTH
CLAMPED = "the table's entries are clamped to their range on the chip where they are made"
NO_ROW = 1 << 30

_CONST = dict(ident=128, fold=128, tri=128, ids=2 * NT * PICKS, mask=NE * NT * PICKS, keys=NE, first=NE,
              incl=NE, tile=NTILES, dft=LEN)
CONST_AT, CONST_N = {}, 0
for _name, _n in _CONST.items():
    CONST_AT[_name] = (CONST_N, CONST_N + _n)
    CONST_N += _n


def constants():
    import numpy as np
    c = np.zeros((128, CONST_N), np.float32)

    def put(name, a):
        c[:a.shape[0], CONST_AT[name][0]:CONST_AT[name][1]] = a

    i = np.arange(128)
    put("ident", np.eye(128))
    put("fold", (i[:, None] % D == i[None, :] % D) * 1.0)
    put("tri", (i[:, None] < i[None, :]) * 1.0)
    n2, v = i // V, i % V
    ch, k, g, pk = np.meshgrid(np.arange(2), np.arange(BLK), np.arange(G), np.arange(PICKS), indexing="ij")
    tok = (g * TOK + ch * 8 + 2 * k).reshape(1, -1) + (v * NPATCH + n2)[:, None]
    put("ids", PICKS * tok + pk.reshape(1, -1))
    put("mask", np.tile((np.arange(NE * NT * PICKS) % (NT * PICKS) != 0) * 1.0, (128, 1)))
    put("keys", np.tile(NE - np.arange(NE) * 1.0, (128, 1)))
    put("first", np.tile(np.arange(NE) * float(REGION) - 1, (128, 1)))
    e = np.arange(NE)
    put("incl", (e[:, None] <= e[None, :]) * 1.0)
    put("tile", np.tile(np.arange(NTILES) * 1.0, (NE, 1)))
    f, t = np.arange(NF), np.arange(LEN)
    a = 2 * np.pi * f[:, None] * t[None, :] / LEN
    put("dft", np.concatenate([np.cos(a), -np.sin(a)]) / np.sqrt(LEN))
    return c


def vit_tower(nc, x, tok_W, Wk, Wq, Wv, Wlr, blr, Ws, bs, gate_w, gate_b, w1, w2, w3, consts, out, debug=None):
    xs = nc.dram_tensor("routed_rows", (PAD_ROW + 128, ROW), F32, kind="Internal").ap()
    ys = nc.dram_tensor("expert_rows", (NTOK * PICKS, D), F32, kind="Internal").ap()
    ctx = ExitStack()
    with ctx:
        def sb(name, shape, dt=F32, at=ctx):
            return at.enter_context(nc.sbuf_tensor(name, shape, dt))

        def sem(name):
            return ctx.enter_context(nc.semaphore(name))

        def ps(name, at, shape=(128, CH)):
            return at.enter_context(nc.psum_tensor(name, list(shape), F32))

        cst = sb("cst", [128, CONST_N])

        def const(name, rows=128):
            return cst[0:rows, CONST_AT[name][0]:CONST_AT[name][1]]

        ident, fold = const("ident"), const("fold")
        wkq = sb("wkq", [128, 7, 128])
        WK, WV, WA, W0, W1, W1T, WQ = range(7)
        bias = sb("bias", [128, 4])
        hbias = sb("hbias", [128, 4])
        H = sb("H", [128, PAIRS, 2, CH])
        X = sb("X", [128, PAIRS, 2, CH])
        grads = sb("grads", [128, 2, 128])
        zsum = sb("zsum", [128, 2, 2 * PAIRS])

        nW = sb("nW", [128, 2, 128])
        nb = sb("nb", [128, 2])
        env = dict(x=x, tok_W=tok_W, Wk=Wk, Wq=Wq, Wv=Wv, Wlr=Wlr, blr=blr, Ws=Ws, bs=bs, gate_w=gate_w, gate_b=gate_b,
                   w1=w1, w2=w2, w3=w3, consts=consts, out=out, xs=xs, ys=ys, cst=cst, ident=ident, fold=fold, wkq=wkq,
                   bias=bias, hbias=hbias, H=H, X=X, grads=grads, zsum=zsum, nW=nW, nb=nb)

        phase_a(nc, ctx, sb, sem, ps, const, env)
        phase_g(nc, ctx, sb, sem, ps, const, env)
        w12h = sb("w12h", [128, NE, 2 * HID], F32R)
        w12l = sb("w12l", [128, NE, 2 * HID], F32R)
        w3s = sb("w3s", [HID, (NE + 1) * D])
        carry = sb("carry", [128, NE])
        table = sb("table", [1, 3, NTILES], U32)
        env.update(w12h=w12h, w12l=w12l, w3s=w3s, carry=carry, table=table)
        phase_b(nc, ctx, sb, sem, ps, const, env)
        phase_c(nc, ctx, sb, sem, ps, const, env)
        phase_d(nc, ctx, sb, sem, ps, const, env)
        if debug is not None:
            debug(nc, ctx, sb, sem, ps, env)


def inverse_root(dve, v, t, y, done, base):
    k = [0]

    def link(ins):
        k[0] += 1
        ins.then_inc(done, 1)
        dve.wait_ge(done, base + k[0])

    link(dve.tensor_scalar(y.bitcast(U32), v.bitcast(U32), 1, None, ALU.logical_shift_right))
    link(dve.tensor_scalar(y.bitcast(U32), y.bitcast(U32), -1.0, RSQRT_GUESS, ALU.mult, ALU.add))
    for _ in range(3):
        link(dve.tensor_tensor(t, y, y, ALU.mult))
        link(dve.tensor_tensor(t, t, v, ALU.mult))
        link(dve.tensor_scalar(t, t, -0.5, 1.5, ALU.mult, ALU.add))
        link(dve.tensor_tensor(y, y, t, ALU.mult))
    assert k[0] == ROOT_STEPS


ROOT_STEPS = 14
RSQRT_GUESS = float(0x5f3759df)


def phase_a(nc, ctx, sb, sem, ps, const, env):
    x, tok_W, Wk, Wq, Wv, Wlr, blr, Ws, bs, consts = (env[n] for n in "x tok_W Wk Wq Wv Wlr blr Ws bs consts".split())
    cst, ident, wkq, bias, hbias, H, X, grads, zsum = (env[n] for n in "cst ident wkq bias hbias H X grads zsum".split())
    WK, WV, WA, W0, W1, W1T, WQ = range(7)
    x_rows = x.rearrange("b c (m rp q) v -> b rp c m (q v)", rp=RP, q=Q)
    x_last = x.rearrange("b c t v -> b t c v")
    with ExitStack() as a:
        xb = sb("xb", [128, 2, G, SLOTS, Q * V], at=a)
        M = sb("M", [128, 2, Q, D], at=a)
        wlr = sb("wlr", [128, 1], at=a)

        def two(name):
            return sb(name, [128, 2, CH], at=a)

        hT, xt, sq, keys, s0, q0, x1, s1, q1, dd, tha, Z1, Z0, x1T, Z1T, Z0T = (two(n) for n in (
            "hT xt sq keys s0 q0 x1 s1 q1 dd tha Z1 Z0 x1T Z1T Z0T".split()))
        msum = sb("msum", [128, 2, NT], at=a)
        vsum = sb("vsum", [128, 2, NT], at=a)
        var = sb("var", [128, 2, NT], at=a)
        std = sb("std", [128, 2, NT], at=a)
        rstd = sb("rstd", [128, 2, NT], at=a)
        S = [ps(f"tok{c}", a) for c in range(2)]
        Bk = [[ps(f"chain{c}{i}", a) for i in range(2)] for c in range(2)]
        GB = ps("gradbank", a, (128, 2, 128))
        MB = ps("spare", a)

        c_in, w_in, w_in2, zeroed, m_ps, m_done, w_set, t_ps, wt_in = (
            sem("c_in"), sem("w_in"), sem("w_in2"), sem("zeroed"), sem("m_ps"), sem("m_done"), sem("w_set"), sem("t_ps"), sem("wt_in"))
        x_in = [sem("x_in0"), sem("x_in1")]
        s_tok = [sem("s_tok0"), sem("s_tok1")]
        names = ("hT Th Hs msum xc sq vs var rstd xt Tx X K keys z0 a0 p0 q0 x1 z1 a1 p1 q1 V A tha d1 d D Z1 dx E Z0 "
                 "Tx1 TZ1 TZ0 x1T Z1T Z0T g1 g0 gacc").split()
        s = {n: sem("s_" + n) for n in names}
        tw = X[0:2 * NF, 0:PAIRS, :, :].rearrange("p a b (o r c) -> p (a b o) r c", r=RP, c=C)
        tw_src = tok_W.rearrange("o (f c) -> f o c", c=C)
        dft = const("dft", 2 * NF)

        def load_half(q, it, half):
            for g in range(G):
                b = it * G + g
                n = SLOTS if half == 0 else SLOTS - 1
                for rp in range(RP):
                    q.dma_start(xb[rp * C:(rp + 1) * C, half, g, 0:n, :],
                                x_rows[bass.ds(b, 1), rp, :, half * 8:half * 8 + n, :]).then_inc(x_in[half], 16)
                    if half == 1:
                        q.dma_start(xb[rp * C:(rp + 1) * C, half, g, n, :].rearrange("p (q v) -> p q v", q=Q),
                                    x_last[bass.ds(b, 1), T - 1, :, :].rearrange("a c v -> c a v").to_broadcast([C, Q, V])
                                    ).then_inc(x_in[half], 16)

        per_half = [16 * G * RP, 32 * G * RP]

        with nc.Block() as block:

            @block.sync
            def _(sp):
                sp.dma_start(cst[:, :], consts[:, :]).then_inc(c_in, 16)
                for r in range(RP):
                    sp.dma_start(tw[:, :, r, :], tw_src).then_inc(wt_in, 16)
                load_half(sp, 0, 0)
                load_half(sp, 0, 1)
                with sp.Fori(0, PAIRS - 1, 1) as it:
                    for half in range(2):
                        sp.wait_ge(s_tok[half], it + 1)
                        load_half(sp, it + 1, half)

            @block.gpsimd
            def _(pool):
                for name in "x1 d".split():
                    pool.sem_inc(s[name], 1)
                pool.memset(wkq[:, :, :], 0.0).then_inc(zeroed, 1)
                pool.memset(bias[:, 3:4], EPS_LN).then_inc(zeroed, 1)
                with pool.Fori(0, PAIRS, 1) as it:
                    n = [pool.snap(it * 2 + 2), pool.snap(it * 2 + 3)]
                    old = pool.snap(it * 2 + 1)
                    for c in range(2):
                        pool.wait_ge(s["keys"], n[c])
                        pool.wait_ge(s["a0"], n[c])
                        pool.wait_ge(s["Tx1"], old)
                        pool.wait_ge(s["d1"], old)
                        pool.tensor_tensor(x1[:, c, :], keys[:, c, :], s0[:, c, :], ALU.add).then_inc(s["x1"], 1)
                    for c in range(2):
                        pool.wait_ge(s["d1"], n[c])
                        pool.wait_ge(s["a1"], n[c])
                        pool.tensor_tensor(dd[:, c, :], dd[:, c, :], s1[:, c, :], ALU.add).then_inc(s["d"], 1)

            @block.scalar
            def _(act):
                for name in "hT Hs sq X keys a0 a1 tha x1T Z1T Z0T".split():
                    act.sem_inc(s[name], 1)
                act.wait_ge(zeroed, 2)
                for g in range(G):
                    r = slice(g * D, (g + 1) * D)
                    for k, w in ((WK, Wk), (WV, Wv), (WQ, Wq), (W0, Ws[0]), (W1, Ws[1])):
                        act.dma_start(wkq[r, k, r], w).then_inc(w_in, 16)
                    act.dma_start(wlr[r, :], Wlr).then_inc(w_in2, 16)
                    for l in range(2):
                        act.dma_start(bias[r, l:l + 1], bs[l, :].rearrange("(d a) -> d a", a=1)).then_inc(w_in2, 16)
                act.dma_start(bias[:, 2:3], blr.rearrange("(a n) -> a n", a=1).to_broadcast([128, 1])).then_inc(w_in2, 16)
                with act.Fori(0, PAIRS, 1) as it:
                    n = [act.snap(it * 2 + 2), act.snap(it * 2 + 3)]
                    one = act.snap(it + 2)
                    old = act.snap(it * 2 + 1)
                    for c in range(2):
                        act.wait_ge(s_tok[c], it + 1)
                        act.wait_ge(s["Th"], old)
                        act.copy(hT[:, c, :], S[c][:, :]).then_inc(s["hT"], 1)
                    for c in range(2):
                        act.wait_ge(s["Th"], n[c])
                        if c == 0:
                            act.wait_ge(m_done, 2)
                        act.copy(H[:, bass.ds(it, 1), c, :], Bk[c][0][:, :]).then_inc(s["Hs"], 1)
                    for c in range(2):
                        act.wait_ge(s["xc"], n[c])
                        act.wait_ge(s["vs"], old)
                        act.activation(sq[:, c, :], xt[:, c, :], ACT.Square).then_inc(s["sq"], 1)
                    for c in range(2):
                        act.wait_ge(s["Tx"], n[c])
                        act.copy(X[:, bass.ds(it, 1), c, :], Bk[c][1][:, :]).then_inc(s["X"], 1)
                    for c in range(2):
                        act.wait_ge(s["K"], n[c])
                        act.wait_ge(s["z0"], old)
                        act.wait_ge(s["x1"], old)
                        act.copy(keys[:, c, :], Bk[c][0][:, :]).then_inc(s["keys"], 1)
                    for c in range(2):
                        act.wait_ge(s["z0"], n[c])
                        act.wait_ge(s["q0"], old)
                        act.wait_ge(s["Z0"], old)
                        act.activation(s0[:, c, :], Bk[c][1][:, :], ACT.Silu, bias=bias[:, 0:1])
                        act.activation(q0[:, c, :], Bk[c][1][:, :], ACT.Tanh, bias=hbias[:, 0:1], scale=0.5).then_inc(s["a0"], 1)
                    for c in range(2):
                        act.wait_ge(s["z1"], n[c])
                        act.wait_ge(s["d"], old)
                        act.wait_ge(s["Z1"], old)
                        act.activation(s1[:, c, :], Bk[c][0][:, :], ACT.Silu, bias=bias[:, 1:2])
                        act.activation(q1[:, c, :], Bk[c][0][:, :], ACT.Tanh, bias=hbias[:, 1:2], scale=0.5).then_inc(s["a1"], 1)
                    for c in range(2):
                        act.wait_ge(s["A"], n[c])
                        act.wait_ge(s["D"], old)
                        act.activation(tha[:, c, :], Bk[c][0][:, :], ACT.Tanh, bias=hbias[:, 2:3], scale=0.5).then_inc(s["tha"], 1)
                    for name, src, dst, bank, used in (("x1T", "Tx1", x1T, 0, "g1"), ("Z1T", "TZ1", Z1T, 1, "g1"),
                                                       ("Z0T", "TZ0", Z0T, 0, "g0")):
                        for c in range(2):
                            act.wait_ge(s[src], n[c])
                            act.wait_ge(s[used], old)
                            act.copy(dst[:, c, :], Bk[c][bank][:, :]).then_inc(s[name], 1)

            @block.vector
            def _(dve):
                for name in "msum xc vs var xt p0 q0 d1 p1 q1 D Z1 E Z0 gacc".split():
                    dve.sem_inc(s[name], 1)
                def bc(t):
                    return t.unsqueeze(2).to_broadcast([128, NT, D])

                def tiles(t):
                    return t.rearrange("p (t f) -> p t f", f=D)

                for oh in range(2):
                    dve.wait_ge(m_ps, oh + 1)
                    for r in range(RP):
                        rows = slice(r * C, (r + 1) * C)
                        src = (S[oh][rows, :] if oh < 2 else None).rearrange("p (o hh r q) -> p hh r q o", hh=2, r=RP, q=Q)
                        for hh in range(2):
                            i = dve.tensor_copy(M[rows, hh, :, oh * 32:(oh + 1) * 32], src[:, hh, r, :, :])
                    i.then_inc(m_done, 1)
                dve.wait_ge(w_in2, 16 * 7)
                dve.wait_ge(zeroed, 2)
                for g in range(G):
                    r = slice(g * D, (g + 1) * D)
                    dve.tensor_copy(wkq[r, WA, r], wlr[r, :].to_broadcast([D, D]))
                dve.tensor_scalar(hbias[:, :], bias[:, :], 0.5, None, ALU.mult).then_inc(w_set, 1)
                dve.wait_ge(t_ps, 1)
                dve.tensor_scalar(wkq[:, W1T, :], MB[:, 0:128], 0.5, None, ALU.mult).then_inc(w_set, 1)
                dve.memset(grads[:, :, :], 0.0).then_inc(s["gacc"], 1)
                with dve.Fori(0, PAIRS, 1) as it:
                    n = [dve.snap(it * 2 + 2), dve.snap(it * 2 + 3)]
                    old = dve.snap(it * 2 + 1)
                    one = dve.snap(it + 2)
                    for c in range(2):
                        h = tiles(H[:, bass.ds(it, 1), c, :].rearrange("p a n -> p (a n)"))
                        dve.wait_ge(s["Hs"], n[c])
                        dve.tensor_reduce(msum[:, c, :], h, AX.X, ALU.add).then_inc(s["msum"], 1)
                    for c in range(2):
                        h = tiles(H[:, bass.ds(it, 1), c, :].rearrange("p a n -> p (a n)"))
                        dve.wait_ge(s["msum"], n[c])
                        dve.wait_ge(s["g0"], old)
                        dve.scalar_tensor_tensor(tiles(xt[:, c, :]), bc(msum[:, c, :]), -1.0 / D, h, ALU.mult, ALU.add).then_inc(s["xc"], 1)
                    for c in range(2):
                        dve.wait_ge(s["sq"], n[c])
                        dve.tensor_reduce(vsum[:, c, :], tiles(sq[:, c, :]), AX.X, ALU.add).then_inc(s["vs"], 1)
                    dve.wait_ge(s["vs"], n[1])
                    dve.tensor_scalar(var[:, :, :], vsum[:, :, :], 1.0 / D, EPS_LN, ALU.mult, ALU.add).then_inc(s["var"], 1)
                    dve.wait_ge(s["var"], one)
                    inverse_root(dve, var[:, :, :], std[:, :, :], rstd[:, :, :], s["rstd"], it * ROOT_STEPS)
                    for c in range(2):
                        dve.tensor_tensor(tiles(xt[:, c, :]), tiles(xt[:, c, :]), bc(rstd[:, c, :]), ALU.mult).then_inc(s["xt"], 1)

                    def slopes(sl, th, ready, p, q):
                        for c in range(2):
                            dve.wait_ge(s[ready], n[c])
                            dve.scalar_tensor_tensor(th[:, c, :], sl[:, c, :], -1.0, th[:, c, :], ALU.add, ALU.mult).then_inc(s[p], 1)
                        for c in range(2):
                            dve.wait_ge(s[p], n[c])
                            dve.scalar_tensor_tensor(th[:, c, :], sl[:, c, :], 1.0, th[:, c, :], ALU.add, ALU.subtract).then_inc(s[q], 1)

                    slopes(s0, q0, "a0", "p0", "q0")
                    for c in range(2):
                        dve.wait_ge(s["V"], n[c])
                        dve.wait_ge(s["x1"], n[c])
                        dve.wait_ge(s["Z1"], old)
                        dve.tensor_tensor(dd[:, c, :], x1[:, c, :], Bk[c][1][:, :], ALU.subtract).then_inc(s["d1"], 1)
                    slopes(s1, q1, "a1", "p1", "q1")
                    for c in range(2):
                        dve.wait_ge(s["tha"], n[c])
                        dve.wait_ge(s["d"], n[c])
                        dve.scalar_tensor_tensor(dd[:, c, :], tha[:, c, :], 1.0, dd[:, c, :], ALU.add, ALU.mult).then_inc(s["D"], 1)
                    for c in range(2):
                        dve.wait_ge(s["D"], n[c])
                        dve.wait_ge(s["q1"], n[c])
                        dve.wait_ge(s["TZ1"], old)
                        dve.scalar_tensor_tensor(Z1[:, c, :], q1[:, c, :], 1.0, dd[:, c, :], ALU.mult, ALU.mult,
                                                 accum_out=zsum[:, 0, bass.ds(it * 2 + c, 1)]).then_inc(s["Z1"], 1)
                    for c in range(2):
                        dve.wait_ge(s["dx"], n[c])
                        dve.wait_ge(s["TZ0"], old)
                        dve.tensor_tensor(Z0[:, c, :], dd[:, c, :], Bk[c][1][:, :], ALU.add).then_inc(s["E"], 1)
                    for c in range(2):
                        dve.wait_ge(s["E"], n[c])
                        dve.scalar_tensor_tensor(Z0[:, c, :], q0[:, c, :], 1.0, Z0[:, c, :], ALU.mult, ALU.mult,
                                                 accum_out=zsum[:, 1, bass.ds(it * 2 + c, 1)]).then_inc(s["Z0"], 1)
                    dve.wait_ge(s["g0"], n[1])
                    dve.wait_ge(s["gacc"], one)
                    dve.tensor_tensor(grads[:, :, :], grads[:, :, :], GB[:, :, :], ALU.add).then_inc(s["gacc"], 1)

            @block.tensor
            def _(pe):
                for name in "Th Tx K z0 z1 V A dx Tx1 TZ1 TZ0 g1 g0".split():
                    pe.sem_inc(s[name], 1)
                def stage1(half):
                    for hh in range(2):
                        for q in range(Q):
                            for g in range(G):
                                last = pe.matmul(S[half][g * D:(g + 1) * D, :].rearrange("p (m v) -> p m v", v=V), M[:, hh, q, :],
                                                 xb[:, half, g, hh:hh + 8, q * V:(q + 1) * V],
                                                 start=(hh == 0 and q == 0), stop=(hh == 1 and q == Q - 1))
                            if hh == 1 and q == Q - 1:
                                last.then_inc(s_tok[half], 1)
                            yield

                pe.wait_ge(c_in, 16)
                pe.wait_ge(wt_in, 16 * RP)
                for o in range(D):
                    last = pe.matmul(S[o // 32][:, (o % 32) * LEN:(o % 32 + 1) * LEN], tw[:, o, :, :], dft,
                                     start=True, stop=True)
                    if o % 32 == 31:
                        last.then_inc(m_ps, 1)
                pe.wait_ge(w_in, 16 * 10)
                pe.transpose(MB[:, 0:128], wkq[:, W1, :], ident).then_inc(t_ps, 1)
                pe.wait_ge(m_done, 2)
                for half in range(2):
                    pe.wait_ge(x_in[half], per_half[half])
                    for _ in stage1(half):
                        pass
                pe.wait_ge(w_set, 2)

                def transposes(c, bank, src):
                    for k in range(BLK):
                        last = pe.transpose(Bk[c][bank][:, k * 128:(k + 1) * 128], src[:, c, k * 128:(k + 1) * 128], ident)
                    return last

                def body(it, more):
                    n = [pe.snap(it * 2 + 2), pe.snap(it * 2 + 3)] if more else [it * 2 + 2, it * 2 + 3]
                    old = pe.snap(it * 2 + 1) if more else it * 2 + 1

                    def mm(c, bank, w, mov):
                        return pe.matmul(Bk[c][bank][:, :], wkq[:, w, :], mov, start=True, stop=True)

                    def xk(c):
                        return X[:, bass.ds(it, 1), c, :].rearrange("p a n -> p (a n)")

                    def t_h(c):
                        pe.wait_ge(s["hT"], n[c])
                        pe.wait_ge(s["Z0T"], old)
                        transposes(c, 0, hT).then_inc(s["Th"], 1)

                    def t_x(c):
                        pe.wait_ge(s["xt"], n[c])
                        transposes(c, 1, xt).then_inc(s["Tx"], 1)

                    def k_(c):
                        pe.wait_ge(s["X"], n[c])
                        mm(c, 0, WK, xk(c)).then_inc(s["K"], 1)

                    def z_0(c):
                        pe.wait_ge(s["keys"], n[c])
                        mm(c, 1, W0, keys[:, c, :]).then_inc(s["z0"], 1)

                    def z_1(c):
                        pe.wait_ge(s["x1"], n[c])
                        mm(c, 0, W1, x1[:, c, :]).then_inc(s["z1"], 1)

                    def v_(c):
                        pe.wait_ge(s["a0"], n[c])
                        mm(c, 1, WV, xk(c)).then_inc(s["V"], 1)

                    def a_(c):
                        pe.wait_ge(s["a1"], n[c])
                        mm(c, 0, WA, xk(c)).then_inc(s["A"], 1)

                    def dx(c):
                        pe.wait_ge(s["Z1"], n[c])
                        mm(c, 1, W1T, Z1[:, c, :]).then_inc(s["dx"], 1)

                    def t_x1(c):
                        pe.wait_ge(s["tha"], n[c])
                        transposes(c, 0, x1).then_inc(s["Tx1"], 1)

                    def t_z1(c):
                        pe.wait_ge(s["E"], n[c])
                        transposes(c, 1, Z1).then_inc(s["TZ1"], 1)

                    def t_z0(c):
                        pe.wait_ge(s["Z0"], n[c])
                        pe.wait_ge(s["x1T"], n[c])
                        transposes(c, 0, Z0).then_inc(s["TZ0"], 1)

                    def grad(c, slot, lhs, rhs, name):
                        for k in range(BLK):
                            cols = slice(k * 128, (k + 1) * 128)
                            last = pe.matmul(GB[:, slot, :], lhs[:, c, cols], rhs[:, c, cols],
                                             start=(c == 0 and k == 0), stop=(c == 1 and k == BLK - 1))
                        last.then_inc(s[name], 1)

                    def g_1(c):
                        pe.wait_ge(s["x1T"], n[c])
                        pe.wait_ge(s["Z1T"], n[c])
                        pe.wait_ge(s["gacc"], pe.snap(it + 2) if more else it + 2)
                        grad(c, 0, x1T, Z1T, "g1")

                    def g_0(c):
                        pe.wait_ge(s["Z0T"], n[c])
                        grad(c, 1, xt, Z0T, "g0")

                    steps = [t_h, t_x, k_, z_0, z_1, v_, a_, dx, t_x1, t_z1, t_z0, g_1, g_0]
                    fill = iter(())
                    for i, step in enumerate(steps):
                        for c in range(2):
                            step(c)
                            if more and i == 0 and c == 1:
                                pe.wait_ge(x_in[0], (it + 2) * per_half[0])
                                fill = stage1(0)
                            if more and i == 6 and c == 0:
                                for _ in fill:
                                    pass
                                pe.wait_ge(x_in[1], (it + 2) * per_half[1])
                                fill = stage1(1)
                            next(fill, None)
                    for _ in fill:
                        pass

                with pe.Fori(0, PAIRS - 1, 1) as it:
                    body(it, True)
                body(PAIRS - 1, False)


def phase_g(nc, ctx, sb, sem, ps, const, env):
    wkq, bias, grads, zsum, fold, nW, nb = (env[n] for n in "wkq bias grads zsum fold nW nb".split())
    WK, W0, W1 = 0, 3, 4
    with ExitStack() as a:
        pack = sb("pack", [128, 2, D + 1], at=a)
        x0 = sb("gx0", [128, D], at=a)
        gr = sb("gr", [128, 2, D + 1], at=a)
        par = sb("par", [128, 2, D + 1], at=a)
        den = sb("den", [128, 2, D + 1], at=a)
        sgn = sb("sgn", [128, 2, D + 1], at=a)
        P = ps("gfold", a, (128, 2, D + 1))
        P2 = ps("gw0", a, (128, D))
        v, p_, z = sem("g_vec"), sem("g_pe"), sem("g_zero")
        with nc.Block() as block:
            @block.gpsimd
            def _(pool):
                pool.memset(nW[:, :, :], 0.0).then_inc(z, 1)

            @block.tensor
            def _(pe):
                pe.wait_ge(v, 1)
                pe.matmul(P[:, :, :], fold, pack[:, :, :], start=True, stop=True).then_inc(p_, 1)
                pe.wait_ge(v, 2)
                pe.matmul(P2[:, :], wkq[:, WK, :], x0[:, :], start=True, stop=True).then_inc(p_, 1)

            @block.vector
            def _(dve):
                for g in range(G):
                    r = slice(g * D, (g + 1) * D)
                    dve.tensor_copy(pack[r, 0, 0:D], grads[r, 1, r])
                    dve.tensor_copy(pack[r, 1, 0:D], grads[r, 0, r])
                    for l, w in ((0, W0), (1, W1)):
                        dve.tensor_copy(par[r, l, 0:D], wkq[r, w, r])
                dve.tensor_copy(par[:, :, D:D + 1], bias[:, 0:2].unsqueeze(2))
                dve.tensor_reduce(pack[:, 0, D:D + 1], zsum[:, 1, :], AX.X, ALU.add)
                dve.tensor_reduce(pack[:, 1, D:D + 1], zsum[:, 0, :], AX.X, ALU.add).then_inc(v, 1)
                dve.wait_ge(p_, 1)
                dve.tensor_copy(x0[:, :], P[:, 0, 0:D]).then_inc(v, 1)
                dve.tensor_scalar(gr[:, 1, :], P[:, 1, :], GRAD_SCALE, None, ALU.mult)
                dve.tensor_scalar(gr[:, 0, D:D + 1], P[:, 0, D:D + 1], GRAD_SCALE, None, ALU.mult)
                dve.wait_ge(p_, 2)
                dve.tensor_scalar(gr[:, 0, 0:D], P2[:, :], GRAD_SCALE, None, ALU.mult).then_inc(v, 1)
                dve.wait_ge(v, 3)
                dve.scalar_tensor_tensor(sgn[:, :, :], gr[:, :, :], -1.0, gr[:, :, :], ALU.mult, ALU.max).then_inc(v, 1)
                dve.wait_ge(v, 4)
                dve.tensor_scalar(den[:, :, :], sgn[:, :, :], EPS_ADAM, None, ALU.add).then_inc(v, 1)
                dve.wait_ge(v, 5)
                dve.reciprocal(sgn[:, :, :], den[:, :, :]).then_inc(v, 1)
                dve.wait_ge(v, 6)
                dve.scalar_tensor_tensor(den[:, :, :], sgn[:, :, :], -LR, gr[:, :, :], ALU.mult, ALU.mult).then_inc(v, 1)
                dve.wait_ge(v, 7)
                dve.wait_ge(z, 1)
                for g in range(G):
                    r = slice(g * D, (g + 1) * D)
                    dve.scalar_tensor_tensor(nW[r, :, r], par[r, :, 0:D], 1.0 - LR * WD, den[r, :, 0:D], ALU.mult, ALU.add)
                dve.scalar_tensor_tensor(nb[:, :].unsqueeze(2), par[:, :, D:D + 1], 1.0 - LR * WD, den[:, :, D:D + 1],
                                         ALU.mult, ALU.add).then_inc(v, 1)


def phase_b(nc, ctx, sb, sem, ps, const, env):
    wkq, H, X, nW, nb, bias, ident, xs, w12h, w12l, w3s, carry, table = (env[n] for n in
        "wkq H X nW nb bias ident xs w12h w12l w3s carry table".split())
    WQ = 6
    J = NT * PICKS
    with ExitStack() as a:
        def two(name, n=CH):
            return sb(name, [128, 2, n], at=a)

        w12 = sb("w12", [128, NE, 2 * HID], at=a)
        wg = sb("wg", [128, 2 * NE], at=a)
        gb = sb("gb", [128, NE], at=a)
        tri = sb("tri", [128, 128], BF16, at=a)
        ones = sb("ones", [128, 128], BF16, at=a)
        cnt = sb("cnt", [128, 2, NE], BF16, at=a)
        q, s0, x1, s1, r, xt, sq, x2 = (two(n) for n in "bq bs0 bx1 bs1 br bxt bsq bx2".split())
        rows = [sb(f"rows{c}", [128, PICKS, NT, ROW], at=a) for c in range(2)]
        msum, vsum, var, std, rstd, m1, m2, dm, th, km = (two(n, NT) for n in "bm bv bvar bstd brstd bm1 bm2 bdm bth bkm".split())
        L, ge = (two(n, NT * NE) for n in "bL bge".split())
        OH, SC, SL = (two(n, NE * J) for n in "bOH bSC bSL".split())
        base = two("bbase", NE)
        slotf = two("bslotf", J)
        slot = sb("bslot", [128, 2, J], U32, at=a)
        ids = sb("bids", [128, 2 * J], at=a)
        Bk = [[ps(f"bchain{c}{i}", a) for i in range(2)] for c in range(2)]
        RK = [ps(f"brank{c}", a, (128, 2, NE)) for c in range(2)]
        w_in, w_in2, z, z2, v0 = sem("bw_in"), sem("bw_in2"), sem("b_zero"), sem("b_gate_in"), sem("b_set")
        s = {n: sem("b_" + n) for n in ("Q q z0 s0 z1 s1 T h2 sq rstd hi x2 Tx x2T LG th cnt RK slot half2 w_hi v go go_sum".split())}
        sent = [sem("b_sent0"), sem("b_sent1")]
        free = [sem("b_free0"), sem("b_free1")]
        keys, mask, first = const("keys"), const("mask"), const("first")
        pad = sb("pad", [128, ROW], at=a)
        nf = sb("nf", [128, NE], at=a)
        nd = sb("nd", [NE, NE], at=a)
        ncol, nt, endc, both = (sb(n, [NE, w], at=a) for n, w in (("ncol", 1), ("ntl", 1), ("endc", 1), ("both", 2)))
        nu = sb("nu", [NE, 1], U32, at=a)
        GE = sb("GE", [NE, NTILES], at=a)
        ef, xf = (sb(n, [1, NTILES], at=a) for n in ("ef", "xf"))
        padrow = sb("padrow", [1, NE], U32, at=a)
        tv, tp, pads = sem("t_vec"), sem("t_pe"), sem("t_pads")

        with nc.Block() as block:

            @block.sync
            def _(sp):
                for g in range(G):
                    rs = slice(g * D, (g + 1) * D)
                    for k, w in ((0, env["w1"]), (1, env["w2"])):
                        sp.dma_start(w12[rs, :, k * HID:(k + 1) * HID], w.rearrange("e d h -> d e h")).then_inc(w_in, 16)
                sp.dma_start(gb[:, :], env["gate_b"].rearrange("(a n) -> a n", a=1).to_broadcast([128, NE])).then_inc(w_in2, 16)
                sp.wait_ge(z, 1)
                for g in range(G):
                    sp.dma_start(wg[g * D:(g + 1) * D, g * NE:(g + 1) * NE], env["gate_w"]).then_inc(z2, 16)
                sp.dma_start(w3s[:, 0:NE * D].rearrange("h (e o) -> h e o", o=D), env["w3"].rearrange("e h o -> h e o")).then_inc(w_in2, 16)
                for c in range(2):
                    sp.sem_inc(free[c], 1)
                with sp.Fori(0, PAIRS, 1) as it:
                    for c in range(2):
                        sp.wait_ge(sent[c], (it + 1) * (16 * J))
                        sp.sem_inc(free[c], 1)
                sp.wait_ge(z, 5)
                sp.wait_ge(tv, 1)
                sp.dma_start(xs[PAD_ROW:PAD_ROW + 128, :], pad[:, :]).then_inc(pads, 16)
                _, pad_rows = nc.values_load_multi_w_load_instructions(padrow[0:1, :], engines=(mybir.EngineType.SP,),
                                                                       min_val=0, max_val=PAD_ROW - 128)
                for row in pad_rows:
                    sp.dma_start(xs[bass.ds(row, 128), :], pad[:, :]).then_inc(pads, 16)
                sp.wait_ge(pads, 16 * (NE + 1))

            @block.gpsimd
            def _(pool):
                pool.memset(wg[:, :], 0.0).then_inc(z, 1)
                pool.memset(w3s[:, NE * D:], 0.0).then_inc(z, 1)
                pool.memset(ones[:, :], 1.0).then_inc(z, 1)
                pool.memset(pad[:, 0:2 * D + 1], 0.0).then_inc(z, 1)
                pool.memset(pad[:, 2 * D + 1:], 2.0).then_inc(z, 1)
                with pool.Fori(0, PAIRS, 1) as it:
                    n = [pool.snap(it * 2 + 2), pool.snap(it * 2 + 3)]
                    for c in range(2):
                        pool.wait_ge(s["slot"], n[c])
                        pool.wait_ge(s["half2"], n[c])
                        pool.sem_inc(s["go"], 1)
                        for t in range(NT):
                            for k in range(PICKS):
                                pool.indirect_dma_start(
                                    out=xs, out_offset=bass.IndirectOffsetOnAxis(ap=slot[:, c, t * PICKS + k:t * PICKS + k + 1], axis=0),
                                    in_=rows[c][:, k, t, :], in_offset=None).then_inc(sent[c], 16)
                for c in range(2):
                    pool.wait_ge(sent[c], 16 * J * PAIRS)

            @block.scalar
            def _(act):
                for name in "q s0 s1 sq x2T half2 th w_hi".split():
                    act.sem_inc(s[name], 1)
                act.wait_ge(w_in, 16 * 2 * G)
                with act.Fori(0, PAIRS, 1) as it:
                    n = [act.snap(it * 2 + 2), act.snap(it * 2 + 3)]
                    old = act.snap(it * 2 + 1)
                    for c in range(2):
                        act.wait_ge(s["Q"], n[c])
                        act.wait_ge(s["s0"], old)
                        act.copy(q[:, c, :], Bk[c][0][:, :]).then_inc(s["q"], 1)
                    act.copy(w12h[:, bass.ds(it * 2, 2), :], w12[:, bass.ds(it * 2, 2), :]).then_inc(s["w_hi"], 1)
                    for c in range(2):
                        act.wait_ge(s["z0"], n[c])
                        act.wait_ge(s["v"], it * K + 1)
                        act.activation(s0[:, c, :], Bk[c][1][:, :], ACT.Silu, bias=nb[:, 0:1]).then_inc(s["s0"], 1)
                    for c in range(2):
                        act.wait_ge(s["z1"], n[c])
                        act.activation(s1[:, c, :], Bk[c][0][:, :], ACT.Silu, bias=nb[:, 1:2]).then_inc(s["s1"], 1)
                    for c in range(2):
                        act.wait_ge(s["v"], it * K + 1 + AT["xc"][c])
                        act.activation(sq[:, c, :], xt[:, c, :], ACT.Square).then_inc(s["sq"], 1)
                    for c in range(2):
                        act.wait_ge(s["Tx"], n[c])
                        act.wait_ge(s["LG"], old)
                        act.copy(x2[:, c, :], Bk[c][0][:, :]).then_inc(s["x2T"], 1)
                    for c in range(2):
                        act.wait_ge(s["v"], it * K + 1 + AT["dm"][c])
                        act.activation(th[:, c, :], dm[:, c, :], ACT.Tanh, scale=0.5).then_inc(s["th"], 1)
                    for c in range(2):
                        act.wait_ge(s["v"], it * K + 1 + AT["lo"][c])
                        act.wait_ge(free[c], it + 1)
                        act.copy(rows[c][:, 1, :, 0:2 * D], rows[c][:, 0, :, 0:2 * D]).then_inc(s["half2"], 1)

            @block.vector
            def _(dve):
                for name in "v slot".split():
                    dve.sem_inc(s[name], 1)
                def bc(t, n=D):
                    return t.unsqueeze(2).to_broadcast([128, NT, n])

                def per_e(t):
                    return t.unsqueeze(1).to_broadcast([128, NT, NE])

                def tiles(t, f=D):
                    return t.rearrange("p (t f) -> p t f", f=f)

                dve.wait_ge(z, 3)
                dve.tensor_copy(tri[:, :], const("tri"))
                dve.tensor_copy(ids[:, :], const("ids"))
                dve.tensor_copy(carry[:, :], first).then_inc(v0, 1)
                dve.wait_ge(v0, 1)
                dve.wait_ge(w_in2, 32)
                with dve.Fori(0, PAIRS, 1) as it:
                    n = [dve.snap(it * 2 + 2), dve.snap(it * 2 + 3)]
                    done = dve.snap(it * K + 1)

                    def step(name, c, ins):
                        assert AT[name][c] == step.count + 1, (name, c, step.count)
                        step.count += 1
                        ins.then_inc(s["v"], 1)

                    step.count = 0

                    def after(name, c):
                        dve.wait_ge(s["v"], done + AT[name][c])

                    for c in range(2):
                        dve.wait_ge(s["q"], n[c])
                        dve.wait_ge(s["s0"], n[c])
                        step("x1", c, dve.tensor_tensor(x1[:, c, :], q[:, c, :], s0[:, c, :], ALU.add))
                    dve.wait_ge(s["w_hi"], it + 2)
                    for c in range(2):
                        e = bass.ds(it * 2 + c, 1)
                        step("wlo", c, dve.tensor_tensor(w12l[:, e, :], w12[:, e, :], w12h[:, e, :].bitcast(F32), ALU.subtract))
                    for c in range(2):
                        dve.wait_ge(s["s1"], n[c])
                        step("r", c, dve.tensor_tensor(r[:, c, :], x1[:, c, :], s1[:, c, :], ALU.add))

                    def Hc(c):
                        return H[:, bass.ds(it, 1), c, :].rearrange("p a n -> p (a n)")

                    for c in range(2):
                        dve.wait_ge(s["T"], n[c])
                        step("h2", c, dve.tensor_tensor(Hc(c), Hc(c), Bk[c][1][:, :], ALU.add))
                    for c in range(2):
                        after("h2", c)
                        dve.sem_inc(s["go_sum"], 1)
                        step("msum", c, dve.tensor_reduce(msum[:, c, :], tiles(Hc(c)), AX.X, ALU.add))
                    for c in range(2):
                        after("msum", c)
                        step("xc", c, dve.scalar_tensor_tensor(tiles(xt[:, c, :]), bc(msum[:, c, :]), -1.0 / D, tiles(Hc(c)), ALU.mult, ALU.add))
                    for c in range(2):
                        dve.wait_ge(s["sq"], n[c])
                        step("vsum", c, dve.tensor_reduce(vsum[:, c, :], tiles(sq[:, c, :]), AX.X, ALU.add))
                    for c in range(2):
                        after("vsum", c)
                        step("var", c, dve.tensor_scalar(var[:, c, :], vsum[:, c, :], 1.0 / D, EPS_LN, ALU.mult, ALU.add))
                    after("var", 1)
                    inverse_root(dve, var[:, :, :], std[:, :, :], rstd[:, :, :], s["rstd"], it * ROOT_STEPS)
                    for c in range(2):
                        step("x2", c, dve.tensor_tensor(tiles(xt[:, c, :]), tiles(xt[:, c, :]), bc(rstd[:, c, :]), ALU.mult))
                    for c in range(2):
                        dve.wait_ge(s["LG"], n[c])
                        step("L", c, dve.tensor_tensor(tiles(L[:, c, :], NE), tiles(Bk[c][1][:, 0:NT * NE], NE), per_e(gb[:, :]), ALU.add))
                    for pick, m in ((0, m1), (1, m2)):
                        p = f"p{pick}"
                        for c in range(2):
                            after("L" if pick == 0 else "L2", c)
                            step(p + "m", c, dve.tensor_reduce(m[:, c, :], tiles(L[:, c, :], NE), AX.X, ALU.max))
                        for c in range(2):
                            after(p + "m", c)
                            step(p + "ge", c, dve.tensor_tensor(tiles(ge[:, c, :], NE), tiles(L[:, c, :], NE), bc(m[:, c, :], NE), ALU.is_equal))
                        for c in range(2):
                            after(p + "ge", c)
                            step(p + "key", c, dve.tensor_tensor(tiles(ge[:, c, :], NE), tiles(ge[:, c, :], NE), per_e(keys), ALU.mult))
                        for c in range(2):
                            after(p + "key", c)
                            step(p + "km", c, dve.tensor_reduce(km[:, c, :], tiles(ge[:, c, :], NE), AX.X, ALU.max))
                        for c in range(2):
                            after(p + "km", c)
                            oh = OH[:, c, :].rearrange("p (e t k) -> p k t e", e=NE, k=PICKS)[:, pick]
                            step(p + "oh", c, dve.tensor_tensor(oh, tiles(ge[:, c, :], NE), bc(km[:, c, :], NE), ALU.is_equal))
                        if pick == 0:
                            for c in range(2):
                                after(p + "oh", c)
                                oh = OH[:, c, :].rearrange("p (e t k) -> p k t e", e=NE, k=PICKS)[:, 0]
                                step("L2", c, dve.scalar_tensor_tensor(tiles(L[:, c, :], NE), oh, -3.0e38, tiles(L[:, c, :], NE), ALU.mult, ALU.add))
                    for c in range(2):
                        after("p1m", c)
                        step("dm", c, dve.tensor_tensor(dm[:, c, :], m1[:, c, :], m2[:, c, :], ALU.subtract))
                    for c in range(2):
                        after("p1oh", c)
                        step("scan", c, dve.tensor_tensor_scan(SC[:, c, :], mask, OH[:, c, :], 0.0, ALU.mult, ALU.add))
                    for c in range(2):
                        after("scan", c)
                        step("cnt", c, dve.tensor_copy(cnt[:, c, :], SC[:, c, :].rearrange("p (e j) -> p e j", j=J)[:, :, J - 1]))
                    for c in range(2):
                        dve.wait_ge(s["RK"], n[c])
                        if c:
                            after("carry", 0)
                        step("base", c, dve.tensor_tensor(base[:, c, :], RK[c][:, 0, :], carry[:, :], ALU.add))
                        if c == 0:
                            after("base", 0)
                        else:
                            after("base", 1)
                        step("carry", c, dve.tensor_tensor(carry[:, :], RK[c][:, 1, :], carry[:, :], ALU.add))
                    for c in range(2):
                        ej = SC[:, c, :].rearrange("p (e j) -> p e j", j=J)
                        step("sl", c, dve.tensor_tensor(SL[:, c, :].rearrange("p (e j) -> p e j", j=J), ej,
                                                        base[:, c, :].unsqueeze(2).to_broadcast([128, NE, J]), ALU.add))
                    for c in range(2):
                        after("sl", c)
                        step("pick", c, dve.tensor_tensor(SL[:, c, :], SL[:, c, :], OH[:, c, :], ALU.mult))
                    for c in range(2):
                        after("pick", c)
                        step("slotf", c, dve.tensor_reduce(slotf[:, c, :], SL[:, c, :].rearrange("p (e j) -> p j e", j=J), AX.X, ALU.add))
                    for c in range(2):
                        dve.wait_ge(free[c], it + 1)
                        step("hi", c, dve.tensor_copy(rows[c][:, 0, :, 0:D].bitcast(F32R), tiles(xt[:, c, :])))
                        after("slotf", c)
                        step("slot", c, dve.tensor_copy(slot[:, c, :], slotf[:, c, :]))
                        after("hi", c)
                        step("lo", c, dve.tensor_tensor(rows[c][:, 0, :, D:2 * D], tiles(xt[:, c, :]), rows[c][:, 0, :, 0:D], ALU.subtract))
                        dve.wait_ge(s["th"], n[c])
                        step("wt1", c, dve.tensor_scalar(rows[c][:, 0, :, 2 * D], th[:, c, :], 0.5, 0.5, ALU.mult, ALU.add))
                        step("wt2", c, dve.tensor_scalar(rows[c][:, 1, :, 2 * D], th[:, c, :], -0.5, 0.5, ALU.mult, ALU.add))
                        step("id", c, dve.tensor_copy(rows[c][:, :, :, 2 * D + 1].bitcast(U32),
                                                      ids[:, c * J:(c + 1) * J].rearrange("p (t k) -> p k t", k=PICKS)))
                        after("id", c)
                        dve.tensor_scalar(ids[:, c * J:(c + 1) * J], ids[:, c * J:(c + 1) * J], float(PICKS * G * TOK), None,
                                          ALU.add).then_inc(s["slot"], 1)
                    dve.wait_ge(s["slot"], n[1])
                    assert step.count == K, step.count
                dve.wait_ge(s["v"], K * PAIRS + 1)
                dve.tensor_scalar(padrow[:, :], carry[0:1, :], 1.0, None, ALU.add).then_inc(tv, 1)
                dve.tensor_tensor(nf[:, :], carry[:, :], first, ALU.subtract).then_inc(tv, 1)
                dve.wait_ge(tv, 2)
                dve.tensor_tensor(nd[:, :], nf[0:NE, :], ident[0:NE, 0:NE], ALU.mult).then_inc(tv, 1)
                dve.wait_ge(tv, 3)
                dve.tensor_reduce(ncol[:, :], nd[:, :], AX.X, ALU.add).then_inc(tv, 1)
                dve.wait_ge(tv, 4)
                dve.tensor_copy(nu[:, :], ncol[:, :]).then_inc(tv, 1)
                dve.wait_ge(tv, 5)
                dve.tensor_scalar(nu[:, :], nu[:, :], 7, None, ALU.logical_shift_right).then_inc(tv, 1)
                dve.wait_ge(tv, 6)
                dve.tensor_scalar(nt[:, :], nu[:, :], 1.0, None, ALU.add).then_inc(tv, 1)
                dve.wait_ge(tv, 7)
                dve.memset(both[:, 0:1], 1.0)
                dve.tensor_scalar(both[:, 1:2], nt[:, :], -128.0, float(REGION), ALU.mult, ALU.add)
                dve.wait_ge(tp, 1)
                dve.tensor_copy(endc[:, :], Bk[0][0][0:NE, 0:1]).then_inc(tv, 1)
                dve.wait_ge(tv, 8)
                dve.tensor_scalar(GE[:, :], const("tile", NE), endc[:, 0:1], None, ALU.is_ge).then_inc(tv, 1)
                dve.wait_ge(tp, 2)
                dve.tensor_scalar(ef[:, :], Bk[0][1][0:1, 0:NTILES], float(NE - 1), None, ALU.min)
                dve.scalar_tensor_tensor(xf[:, :], const("tile", 1), 128.0, Bk[1][1][0:1, 0:NTILES], ALU.mult, ALU.add).then_inc(tv, 1)
                dve.wait_ge(tv, 10)
                dve.tensor_scalar(table[:, 0, :], ef[:, :], float(D), None, ALU.mult)
                dve.tensor_scalar(table[:, 1, :], xf[:, :], float(PAD_ROW), None, ALU.min)
                dve.tensor_scalar(table[:, 2, :], ef[:, :], float(2 * HID), None, ALU.mult).then_inc(tv, 1)

            @block.tensor
            def _(pe):
                for name in "Q z0 z1 T Tx LG RK".split():
                    pe.sem_inc(s[name], 1)
                pe.wait_ge(v0, 1)
                pe.wait_ge(z2, 32)
                pe.wait_ge(z, 3)
                with pe.Fori(0, PAIRS, 1) as it:
                    n = [pe.snap(it * 2 + 2), pe.snap(it * 2 + 3)]
                    old = pe.snap(it * 2 + 1)
                    done = pe.snap(it * K + 1)
                    for c in range(2):
                        pe.wait_ge(s["x2T"], old)
                        pe.matmul(Bk[c][0][:, :], wkq[:, WQ, :], X[:, bass.ds(it, 1), c, :].rearrange("p a n -> p (a n)"),
                                  start=True, stop=True).then_inc(s["Q"], 1)
                    for c in range(2):
                        pe.wait_ge(s["q"], n[c])
                        pe.wait_ge(s["v"], done)
                        pe.matmul(Bk[c][1][:, :], nW[:, 0, :], q[:, c, :], start=True, stop=True).then_inc(s["z0"], 1)
                    for c in range(2):
                        pe.wait_ge(s["v"], done + AT["x1"][c])
                        pe.matmul(Bk[c][0][:, :], nW[:, 1, :], x1[:, c, :], start=True, stop=True).then_inc(s["z1"], 1)
                    for name, bank, src, ready in (("T", 1, r, "r"), ("Tx", 0, xt, "x2")):
                        for c in range(2):
                            pe.wait_ge(s["v"], done + AT[ready][c])
                            for k in range(BLK):
                                last = pe.transpose(Bk[c][bank][:, k * 128:(k + 1) * 128], src[:, c, k * 128:(k + 1) * 128], ident)
                            last.then_inc(s[name], 1)
                    for c in range(2):
                        pe.wait_ge(s["x2T"], n[c])
                        for k in range(BLK):
                            last = pe.matmul(Bk[c][1][:, k * 2 * NE:(k + 1) * 2 * NE], x2[:, c, k * 128:(k + 1) * 128], wg[:, :],
                                             start=True, stop=True)
                        last.then_inc(s["LG"], 1)
                    for c in range(2):
                        pe.wait_ge(s["v"], done + AT["cnt"][c])
                        pe.matmul(RK[c][:, 0, :], tri[:, :], cnt[:, c, :], start=True, stop=True)
                        pe.matmul(RK[c][:, 1, :], ones[:, :], cnt[:, c, :], start=True, stop=True).then_inc(s["RK"], 1)
                pe.wait_ge(tv, 7)
                pe.matmul(Bk[0][0][0:NE, 0:1], const("incl", NE), nt[:, :], start=True, stop=True).then_inc(tp, 1)
                pe.wait_ge(tv, 9)
                pe.matmul(Bk[0][1][0:1, 0:NTILES], both[:, 0:1], GE[:, :], start=True, stop=True)
                pe.matmul(Bk[1][1][0:1, 0:NTILES], both[:, 1:2], GE[:, :], start=True, stop=True).then_inc(tp, 1)


_STEPS = ("x1 wlo r h2 msum xc vsum var x2 L p0m p0ge p0key p0km p0oh L2 p1m p1ge p1key p1km p1oh dm scan cnt").split()
AT = {name: (2 * i + 1, 2 * i + 2) for i, name in enumerate(_STEPS)}
_N = 2 * len(_STEPS)
AT["base"], AT["carry"] = (_N + 1, _N + 3), (_N + 2, _N + 4)
for _i, _name in enumerate(("sl", "pick", "slotf")):
    AT[_name] = (_N + 5 + 2 * _i, _N + 6 + 2 * _i)
_LAST = ("hi", "slot", "lo", "wt1", "wt2", "id")
for _i, _name in enumerate(_LAST):
    AT[_name] = (_N + 11 + _i, _N + 11 + len(_LAST) + _i)
K = _N + 10 + 2 * len(_LAST)


def phase_c(nc, ctx, sb, sem, ps, const, env):
    ident, xs, ys, w12h, w12l, w3s, table = (env[n] for n in "ident xs ys w12h w12l w3s table".split())
    with ExitStack() as a:
        xt = [sb(f"cx{j}", [128, GT, ROW], at=a) for j in range(DEPTH)]
        tag = [sb(f"ctag{j}", [128, GT, 2], at=a) for j in range(DEPTH)]
        y = [sb(f"cy{j}", [128, GT, D], at=a) for j in range(DEPTH)]
        xT = sb("cxT", [128, 2, GT * 128], F32R, at=a)
        gl, hid, hT = (sb(n, [128, 2, GT * HID], at=a) for n in ("cgl", "chid", "chT"))
        T1B = ps("ct1", a, (128, GT * 128))
        T2B = ps("ct2", a, (128, GT * 128))
        HP = [ps(f"ch{c}", a, (128, GT, 2 * HID)) for c in range(2)]
        YP = [ps(f"cyp{c}", a, (128, GT, 128)) for c in range(2)]
        x_in = [sem(f"c_in{j}") for j in range(DEPTH)]
        y_out = [sem(f"c_out{j}") for j in range(DEPTH)]
        s = {n: sem("c_" + n) for n in "T1 xT tag H gl hid T2 hT Y y go".split()}

        def wait(eng, name, g):
            if not (isinstance(g, int) and g < 0):
                eng.wait_ge(s[name], g + 1)

        def wait_dma(eng, sems, g, j):
            if not (isinstance(g, int) and g < 0):
                eng.wait_ge(sems[j], (g - j) * (16 * GT // DEPTH) + 16 * GT)

        def steps(eng, step):
            for g in range(-2, FIRST):
                step(g, g % DEPTH, False)
            with eng.Fori(0, TURNS, 1) as it:
                for u in range(DEPTH):
                    step(it * DEPTH + (FIRST + u), (FIRST + u) % DEPTH, True)
            for g in range(FIRST + TURNS * DEPTH, GROUPS + 1):
                step(g, g % DEPTH, False)

        def has(g, off, looped):
            return looped or 0 <= g + off < GROUPS

        with nc.Block() as block:

            @block.sync
            def _(sp):
                def load(g, j):
                    wait(sp, "T1", g - DEPTH)
                    wait(sp, "tag", g - DEPTH)
                    _, first_rows = nc.values_load_multi_w_load_instructions(
                        table[0:1, 1, bass.ds(g * GT, GT)], engines=(mybir.EngineType.SP,), min_val=0, max_val=PAD_ROW,
                        skip_runtime_bounds_check_because=CLAMPED)
                    for t, row in enumerate(first_rows):
                        sp.dma_start(xt[j][:, t, :], xs[bass.ds(row, 128), :]).then_inc(x_in[j], 16)

                for g in range(DEPTH):
                    load(g, g)
                with sp.Fori(1, GROUPS // DEPTH, 1) as it:
                    for j in range(DEPTH):
                        load(it * DEPTH + j, j)

            @block.gpsimd
            def _(pool):
                with pool.Fori(0, GROUPS // DEPTH, 1) as it:
                    for j in range(DEPTH):
                        wait(pool, "y", it * DEPTH + j)
                        pool.sem_inc(s["go"], 1)
                        for t in range(GT):
                            pool.indirect_dma_start(
                                out=ys, out_offset=bass.IndirectOffsetOnAxis(ap=tag[j][:, t, 1:2].bitcast(U32), axis=0),
                                in_=y[j][:, t, :], in_offset=None, bounds_check=NTOK * PICKS - 1, oob_is_err=False).then_inc(y_out[j], 16)
                for j in range(DEPTH):
                    pool.wait_ge(y_out[j], 16 * GT * (GROUPS // DEPTH))

            @block.scalar
            def _(act):
                def step(g, j, looped):
                    if has(g, 0, looped):
                        wait(act, "T2", g)
                        wait(act, "Y", g - 2)
                        act.copy(hT[:, j % 2, :], T2B[:, :]).then_inc(s["hT"], 1)
                    if has(g, 1, looped):
                        wait(act, "H", g + 1)
                        wait(act, "hid", g - 1)
                        act.activation(gl[:, (j + 1) % 2, :].rearrange("p (t h) -> p t h", h=HID), HP[(j + 1) % 2][:, :, 0:HID],
                                       ACT.Silu).then_inc(s["gl"], 1)
                    if has(g, 2, looped):
                        wait(act, "T1", g + 2)
                        wait(act, "H", g)
                        act.copy(xT[:, j % 2, :], T1B[:, :]).then_inc(s["xT"], 1)

                steps(act, step)

            @block.vector
            def _(dve):
                def step(g, j, looped):
                    if has(g, -1, looped):
                        k = (j - 1) % DEPTH
                        wait(dve, "Y", g - 1)
                        wait(dve, "tag", g - 1)
                        dve.tensor_tensor(y[k][:, :, :], YP[k % 2][:, :, 0:D], tag[k][:, :, 0:1].to_broadcast([128, GT, D]),
                                          ALU.mult).then_inc(s["y"], 1)
                    if has(g, 1, looped):
                        k = (j + 1) % DEPTH
                        wait_dma(dve, x_in, g + 1, k)
                        wait_dma(dve, y_out, g + 1 - DEPTH, k)
                        dve.tensor_copy(tag[k][:, :, :].bitcast(U32), xt[k][:, :, 2 * D:].bitcast(U32)).then_inc(s["tag"], 1)
                    if has(g, 1, looped):
                        k = (j + 1) % 2
                        wait(dve, "gl", g + 1)
                        wait(dve, "T2", g - 1)
                        dve.tensor_tensor(hid[:, k, :].rearrange("p (t h) -> p t h", h=HID),
                                          gl[:, k, :].rearrange("p (t h) -> p t h", h=HID), HP[k][:, :, HID:], ALU.mult).then_inc(s["hid"], 1)

                steps(dve, step)

            @block.tensor
            def _(pe):
                def weights(which, g):
                    return nc.values_load_multi_w_load_instructions(
                        table[0:1, which, bass.ds(g * GT, GT)], engines=(mybir.EngineType.PE,), min_val=0,
                        max_val=(NE - 1) * (2 * HID if which == 2 else D), skip_runtime_bounds_check_because=CLAMPED)[1]

                def step(g, j, looped):
                    if has(g, -1, looped):
                        k = (j - 1) % 2
                        cols = weights(0, g - 1)
                        wait(pe, "hT", g - 1)
                        wait(pe, "y", g - 3)
                        for t in range(GT):
                            last = pe.matmul(YP[k][:, t, :], hT[:, k, t * 128:(t + 1) * 128], w3s[:, bass.ds(cols[t], 128)],
                                             start=True, stop=True)
                        last.then_inc(s["Y"], 1)
                    if has(g, 0, looped):
                        wait(pe, "hid", g)
                        wait(pe, "hT", g - 1)
                        for t in range(GT):
                            last = pe.transpose(T2B[:, t * 128:(t + 1) * 128], hid[:, j % 2, t * 128:(t + 1) * 128], ident)
                        last.then_inc(s["T2"], 1)
                    if has(g, 1, looped):
                        k = (j + 1) % 2
                        cols = weights(2, g + 1)
                        wait(pe, "xT", g + 1)
                        wait(pe, "hid", g - 1)
                        for t in range(GT):
                            lhs = xT[:, k, t * 128:(t + 1) * 128]
                            pe.matmul(HP[k][:, t, :], lhs, w12h_f[:, bass.ds(cols[t], 2 * HID)], start=True, stop=False)
                            last = pe.matmul(HP[k][:, t, :], lhs, w12l_f[:, bass.ds(cols[t], 2 * HID)], start=False, stop=True)
                        last.then_inc(s["H"], 1)
                    if has(g, 2, looped):
                        k = (j + 2) % DEPTH
                        wait_dma(pe, x_in, g + 2, k)
                        wait(pe, "xT", g + 1)
                        for t in range(GT):
                            last = pe.transpose(T1B[:, t * 128:(t + 1) * 128], xt[k][:, t, 0:2 * D], ident)
                        last.then_inc(s["T1"], 1)

                w12h_f, w12l_f = (w[:, :, :].rearrange("p e n -> p (e n)") for w in (w12h, w12l))
                steps(pe, step)


def phase_d(nc, ctx, sb, sem, ps, const, env):
    H, ys, out = env["H"], env["ys"], env["out"]
    y_v = ys.rearrange("(b v c k n2 p) f -> b c n2 v k (p f)", v=V, c=2, k=BLK, n2=2, p=PICKS)
    o_v = out.rearrange("b (v c k n2) f -> b c n2 v k f", v=V, c=2, k=BLK, n2=2)
    with ExitStack() as a:
        slots = [(par, c) for par in range(2) for c in range(2)]
        yb = {k: sb(f"yb{k[0]}{k[1]}", [128, G, BLK, PICKS, D], at=a) for k in slots}
        o = {k: sb(f"o{k[0]}{k[1]}", [128, BLK, G, D], at=a) for k in slots}
        y_in = {k: sem(f"d_in{k[0]}{k[1]}") for k in slots}
        o_out = {k: sem(f"d_out{k[0]}{k[1]}") for k in slots}
        part, summed = sem("d_part"), sem("d_sum")
        with nc.Block() as block:
            @block.sync
            def _(sp):
                with sp.Fori(0, PAIRS // 2, 1) as i:
                    for j, (par, c) in enumerate(slots):
                        sp.wait_ge(summed, i * 4 + 1)
                        for g in range(G):
                            b = bass.ds(i * 4 + (par * 2 + g), 1)
                            for n2 in range(2):
                                sp.dma_start(yb[par, c][n2 * V:(n2 + 1) * V, g].rearrange("v k p f -> v k (p f)"),
                                             y_v[b, c, n2, :, :, :]).then_inc(y_in[par, c], 16)

            @block.scalar
            def _(act):
                for k in slots:
                    act.sem_inc(o_out[k], 1)
                with act.Fori(0, PAIRS // 2, 1) as i:
                    for j, (par, c) in enumerate(slots):
                        act.wait_ge(summed, i * 4 + (j + 2))
                        for g in range(G):
                            b = bass.ds(i * 4 + (par * 2 + g), 1)
                            for n2 in range(2):
                                act.dma_start(o_v[b, c, n2, :, :, :], o[par, c][n2 * V:(n2 + 1) * V, :, g, :]).then_inc(o_out[par, c], 16)
                for k in slots:
                    act.wait_ge(o_out[k], 64 * (PAIRS // 2) + 1)

            @block.vector
            def _(dve):
                dve.sem_inc(summed, 1)
                with dve.Fori(0, PAIRS // 2, 1) as i:
                    for j, (par, c) in enumerate(slots):
                        h = H[:, bass.ds(i * 2 + par, 1), c, :].rearrange("p a (k g f) -> p (a k) g f", g=G, f=D)
                        yk = [yb[par, c][:, :, :, p, :].rearrange("p g k f -> p k g f") for p in range(PICKS)]
                        dve.wait_ge(y_in[par, c], (i + 1) * 64)
                        dve.wait_ge(o_out[par, c], i * 64 + 1)
                        dve.tensor_tensor(o[par, c][:, :, :, :], h, yk[0], ALU.add).then_inc(part, 1)
                        dve.wait_ge(part, i * 4 + (j + 1))
                        dve.tensor_tensor(o[par, c][:, :, :, :], o[par, c][:, :, :, :], yk[1], ALU.add).then_inc(summed, 1)


_INS = ["x", "L0_tok_W", "L0_attn_Wk", "L0_attn_Wq", "L0_attn_Wv", "L0_attn_Wlr", "L0_attn_blr", "L0_attn_Ws", "L0_attn_bs",
        "L0_ffn_gate_w", "L0_ffn_gate_b", "L0_ffn_w1", "L0_ffn_w2", "L0_ffn_w3"]


def kernel(**inputs):
    import numpy as _np
    import concourse.bacc as _bacc
    from concourse import mybir as _mybir
    from concourse.bass_utils import run_bass_kernel_spmd as _run

    nc = _bacc.Bacc("TRN2", target_bir_lowering=False, num_devices=1)
    arrays, args = {}, []
    for name in _INS:
        arrays[f"in_{name}_dram"] = _np.ascontiguousarray(inputs[name])
    arrays["in_consts_dram"] = constants()
    for name, a in arrays.items():
        args.append(nc.dram_tensor(name, a.shape, _mybir.dt.from_np(a.dtype), kind="ExternalInput").ap())
    out = nc.dram_tensor("out_0_dram", (B, TOK, D), _mybir.dt.float32, kind="ExternalOutput").ap()
    vit_tower(nc, *args, out)
    r = _run(nc, [arrays], core_ids=[0])
    return r.results[0]["out_0_dram"]
```

```python
import concourse.bass as bass
from concourse import mybir
from contextlib import ExitStack

F32 = mybir.dt.float32
F32R = mybir.dt.float32r
BF16 = mybir.dt.bfloat16
U32 = mybir.dt.uint32
ALU = mybir.AluOpType
ACT = mybir.ActivationFunctionType
AX = mybir.AxisListType

B, C, T, V = 16, 64, 128, 64
D = 64
LEN, STRIDE, NPATCH = 16, 8, 16
NF = LEN // 2 + 1
TOK = V * NPATCH
G = 2
PAIRS = B // G
CH = 512
BLK = CH // 128
NT = BLK * G
Q = 4
RP = STRIDE // Q
SLOTS = NPATCH // 2 + 1
NE, HID = 16, 128
PICKS = 2
LR, WD, EPS_ADAM, MAX_ALR, EPS_LN = 0.001, 0.01, 1e-8, 0.1, 1e-5
GRAD_SCALE = 0.5 * (MAX_ALR * 0.5) * (2.0 / D)

NTOK = B * TOK
ROW = 2 * D + 2
REGION = NTOK + 128
PAD_ROW = NE * REGION
NTILES = NTOK * PICKS // 128 + NE
GT = 4
GROUPS = NTILES // GT
DEPTH = 4
FIRST = 3
TURNS = (GROUPS - 2 - FIRST) // DEPTH
CLAMPED = "the table's entries are clamped to their range on the chip where they are made"
NO_ROW = 1 << 30

OG = 4
OROWS = OG * 2 * NF

_CONST = dict(ident=128, fold=128, tri=128, ids=2 * NT * PICKS, mask=NE * NT * PICKS, keys=NE, first=NE,
              incl=NE, tile=NTILES, dft=OG * LEN)
CONST_AT, CONST_N = {}, 0
for _name, _n in _CONST.items():
    CONST_AT[_name] = (CONST_N, CONST_N + _n)
    CONST_N += _n


def constants():
    import numpy as np
    c = np.zeros((128, CONST_N), np.float32)

    def put(name, a):
        c[:a.shape[0], CONST_AT[name][0]:CONST_AT[name][1]] = a

    i = np.arange(128)
    put("ident", np.eye(128))
    put("fold", (i[:, None] % D == i[None, :] % D) * 1.0)
    put("tri", (i[:, None] < i[None, :]) * 1.0)
    n2, v = i // V, i % V
    ch, k, g, pk = np.meshgrid(np.arange(2), np.arange(BLK), np.arange(G), np.arange(PICKS), indexing="ij")
    tok = (g * TOK + ch * 8 + k).reshape(1, -1) + (v * NPATCH + n2 * BLK)[:, None]
    put("ids", PICKS * tok + pk.reshape(1, -1))
    put("mask", np.tile((np.arange(NE * NT * PICKS) % (NT * PICKS) != 0) * 1.0, (128, 1)))
    put("keys", np.tile(NE - np.arange(NE) * 1.0, (128, 1)))
    put("first", np.tile(np.arange(NE) * float(REGION) - 1, (128, 1)))
    e = np.arange(NE)
    put("incl", (e[:, None] <= e[None, :]) * 1.0)
    put("tile", np.tile(np.arange(NTILES) * 1.0, (NE, 1)))
    f, t = np.arange(NF), np.arange(LEN)
    a = 2 * np.pi * f[:, None] * t[None, :] / LEN
    put("dft", np.kron(np.eye(OG), np.concatenate([np.cos(a), -np.sin(a)]) / np.sqrt(LEN)))
    return c


def vit_tower(nc, x, tok_W, Wk, Wq, Wv, Wlr, blr, Ws, bs, gate_w, gate_b, w1, w2, w3, consts, out):
    xs = nc.dram_tensor("routed_rows", (PAD_ROW + 128, ROW), F32, kind="Internal").ap()
    ys = nc.dram_tensor("expert_rows", (NTOK * PICKS, D), F32, kind="Internal").ap()
    ctx = ExitStack()
    with ctx:
        def sb(name, shape, dt=F32, at=ctx):
            return at.enter_context(nc.sbuf_tensor(name, shape, dt))

        def sem(name):
            return ctx.enter_context(nc.semaphore(name))

        def ps(name, at, shape=(128, CH)):
            return at.enter_context(nc.psum_tensor(name, list(shape), F32))

        cst = sb("cst", [128, CONST_N])

        def const(name, rows=128):
            return cst[0:rows, CONST_AT[name][0]:CONST_AT[name][1]]

        ident, fold = const("ident"), const("fold")
        wkq = sb("wkq", [128, 7, 128])
        WK, WV, WA, W0, W1, W1T, WQ = range(7)
        bias = sb("bias", [128, 3])
        hbias = sb("hbias", [128, 3])
        H = sb("H", [128, PAIRS, 2, CH])
        X = sb("X", [128, PAIRS, 2, CH])
        grads = sb("grads", [128, 2, 128])
        zsum = sb("zsum", [128, 2, 2 * PAIRS])

        warm = sb("warm", [128, 1])
        nW = sb("nW", [128, 2, 128])
        nb = sb("nb", [128, 2])
        env = dict(x=x, tok_W=tok_W, Wk=Wk, Wq=Wq, Wv=Wv, Wlr=Wlr, blr=blr, Ws=Ws, bs=bs, gate_w=gate_w, gate_b=gate_b,
                   w1=w1, w2=w2, w3=w3, consts=consts, out=out, xs=xs, ys=ys, cst=cst, ident=ident, fold=fold, wkq=wkq,
                   bias=bias, hbias=hbias, H=H, X=X, grads=grads, zsum=zsum, nW=nW, nb=nb, warm=warm)

        phase_a(nc, ctx, sb, sem, ps, const, env)
        w12h = sb("w12h", [128, NE, 2 * HID], F32R)
        w12l = sb("w12l", [128, NE, 2 * HID], F32R)
        w3s = sb("w3s", [HID, (NE + 1) * D])
        carry = sb("carry", [128, NE])
        table = sb("table", [1, 3, NTILES], U32)
        env.update(w12h=w12h, w12l=w12l, w3s=w3s, carry=carry, table=table)
        phase_b(nc, ctx, sb, sem, ps, const, env)
        phase_c(nc, ctx, sb, sem, ps, const, env)
        phase_d(nc, ctx, sb, sem, ps, const, env)


def inverse_root(dve, v, t, y, done, base):
    k = [0]

    def link(ins):
        k[0] += 1
        ins.then_inc(done, 1)
        dve.wait_ge(done, base + k[0])

    link(dve.tensor_scalar(y.bitcast(U32), v.bitcast(U32), 1, None, ALU.logical_shift_right))
    link(dve.tensor_scalar(y.bitcast(U32), y.bitcast(U32), -1.0, RSQRT_GUESS, ALU.mult, ALU.add))
    for _ in range(3):
        link(dve.scalar_tensor_tensor(t, y, -0.5, y, ALU.mult, ALU.mult))
        link(dve.tensor_tensor(t, t, v, ALU.mult))
        link(dve.scalar_tensor_tensor(y, t, 1.5, y, ALU.add, ALU.mult))
    assert k[0] == ROOT_STEPS


ROOT_STEPS = 11
RSQRT_GUESS = float(0x5f3759df)


class Counts:

    def __init__(self, eng, it, back=0):
        def value(v):
            return v if isinstance(it, int) else eng.snap(v)

        self.n = [value(it * 2 + (2 + c + 2 * back)) for c in range(2)]
        self.old = value(it * 2 + (1 + 2 * back))
        self.one = value(it + (2 + back))


def phase_a(nc, ctx, sb, sem, ps, const, env):
    x, tok_W, Wk, Wq, Wv, Wlr, blr, Ws, bs, consts = (env[n] for n in "x tok_W Wk Wq Wv Wlr blr Ws bs consts".split())
    cst, ident, wkq, bias, hbias, H, X, grads, zsum = (env[n] for n in "cst ident wkq bias hbias H X grads zsum".split())
    warm = env["warm"]
    WK, WV, WA, W0, W1, W1T, WQ = range(7)
    x_rows = x.rearrange("b c (m rp q) v -> b rp c m (q v)", rp=RP, q=Q)
    x_last = x.rearrange("b c t v -> b t c v")
    with ExitStack() as a:
        xb = sb("xb", [128, 2, G, SLOTS, Q * V], at=a)
        M = sb("M", [128, 2, Q, D], at=a)
        wlr = sb("wlr", [128, 1], at=a)

        def two(name):
            return sb(name, [128, 2, CH], at=a)

        hT, xc, xt, sq, keys, s0, q0, x1, s1, q1, dd, tha, Z1, Z0, x1T, Z1T, Z0T = (two(n) for n in (
            "hT xc xt sq keys s0 q0 x1 s1 q1 dd tha Z1 Z0 x1T Z1T Z0T".split()))
        msum = sb("msum", [128, 2, NT], at=a)
        vsum = sb("vsum", [128, 2, NT], at=a)
        var = sb("var", [128, 2, NT], at=a)
        std = sb("std", [128, 2, NT], at=a)
        rstd = sb("rstd", [128, 2, NT], at=a)
        S = [ps(f"tok{c}", a) for c in range(2)]
        Bk = [[ps(f"chain{c}{i}", a) for i in range(2)] for c in range(2)]
        GB = ps("gradbank", a, (128, 4, 128))
        MB = ps("spare", a)

        def turns(eng, turn):
            turn(0, Counts(eng, 0), None)
            with eng.Fori(1, PAIRS, 1) as it:
                turn(it, Counts(eng, it), Counts(eng, it, -1))
            turn(None, None, Counts(eng, PAIRS, -1))

        c_in, w_in, w_in2, zeroed, m_ps, m_done, w_set, t_ps, wt_in = (
            sem("c_in"), sem("w_in"), sem("w_in2"), sem("zeroed"), sem("m_ps"), sem("m_done"), sem("w_set"), sem("t_ps"), sem("wt_in"))
        x_in = [sem("x_in0"), sem("x_in1")]
        s_tok = [sem("s_tok0"), sem("s_tok1")]
        names = ("hT Th Hs msum xc sq vs var rstd xt Tx X K keys z0 a0 p0 q0 x1 z1 a1 p1 q1 V A tha d1 d D Z1 dx E Z0 "
                 "Tx1 TZ1 TZ0 x1T Z1T Z0T g1 g0 gacc").split()
        s = {n: sem("s_" + n) for n in names}
        tw = X[0:OROWS, 0:D * RP * C // (OG * 2 * CH), :, :].rearrange("p a b (o r c) -> p (a b o) r c", r=RP, c=C)
        tw_src = tok_W.rearrange("(a o) (f c) -> (o f) a c", o=OG, c=C)
        dft = const("dft", OROWS)

        def load_half(q, it, half):
            for g in range(G):
                b = it * G + g
                n = SLOTS if half == 0 else SLOTS - 1
                for rp in range(RP):
                    q.dma_start(xb[rp * C:(rp + 1) * C, half, g, 0:n, :],
                                x_rows[bass.ds(b, 1), rp, :, half * 8:half * 8 + n, :]).then_inc(x_in[half], 16)
                    if half == 1:
                        q.dma_start(xb[rp * C:(rp + 1) * C, half, g, n, :].rearrange("p (q v) -> p q v", q=Q),
                                    x_last[bass.ds(b, 1), T - 1, :, :].rearrange("a c v -> c a v").to_broadcast([C, Q, V])
                                    ).then_inc(x_in[half], 16)

        per_half = [16 * G * RP, 32 * G * RP]

        with nc.Block() as block:

            @block.sync
            def _(sp):
                sp.dma_start(cst[:, :], consts[:, :]).then_inc(c_in, 16)
                for r in range(RP):
                    sp.dma_start(tw[:, :, r, :], tw_src).then_inc(wt_in, 16)
                load_half(sp, 0, 0)
                load_half(sp, 0, 1)
                with sp.Fori(0, PAIRS - 1, 1) as it:
                    for half in range(2):
                        sp.wait_ge(s_tok[half], it + 1)
                        load_half(sp, it + 1, half)

            @block.gpsimd
            def _(pool):
                for name in "x1 d".split():
                    pool.sem_inc(s[name], 1)
                pool.memset(wkq[:, :, :], 0.0).then_inc(zeroed, 1)
                pool.memset(warm[:, :], 0.0).then_inc(zeroed, 1)
                for g in range(G):
                    r = slice(g * D, (g + 1) * D)
                    pool.dma_start(wlr[r, :], Wlr).then_inc(w_in2, 16)
                    for l in range(2):
                        pool.dma_start(bias[r, l:l + 1], bs[l, :].rearrange("(d a) -> d a", a=1)).then_inc(w_in2, 16)
                pool.dma_start(bias[:, 2:3], blr.rearrange("(a n) -> a n", a=1).to_broadcast([128, 1])).then_inc(w_in2, 16)
                with pool.Fori(0, PAIRS, 1) as it:
                    k = Counts(pool, it)
                    for c in range(2):
                        pool.wait_ge(s["keys"], k.n[c])
                        pool.wait_ge(s["a0"], k.n[c])
                        pool.wait_ge(s["Tx1"], k.old)
                        pool.wait_ge(s["d1"], k.old)
                        pool.tensor_tensor(x1[:, c, :], keys[:, c, :], s0[:, c, :], ALU.add).then_inc(s["x1"], 1)
                    for c in range(2):
                        pool.wait_ge(s["d1"], k.n[c])
                        pool.wait_ge(s["a1"], k.n[c])
                        pool.tensor_tensor(dd[:, c, :], dd[:, c, :], s1[:, c, :], ALU.add).then_inc(s["d"], 1)

            @block.scalar
            def _(act):
                for name in "hT Hs sq X keys a0 a1 tha x1T Z1T Z0T".split():
                    act.sem_inc(s[name], 1)
                act.wait_ge(zeroed, 2)
                for g in range(G):
                    r = slice(g * D, (g + 1) * D)
                    for k, w in ((WK, Wk), (WV, Wv), (WQ, Wq), (W0, Ws[0]), (W1, Ws[1])):
                        act.dma_start(wkq[r, k, r], w).then_inc(w_in, 16)

                def turn(it, k, kt):
                    def tail_copy(src, dst, bank, name, used):
                        for c in range(2):
                            act.wait_ge(s[src], kt.n[c])
                            act.wait_ge(s[used], kt.old)
                            act.copy(dst[:, c, :], Bk[c][bank][:, :]).then_inc(s[name], 1)

                    if k:
                        act.activation(warm[:, :], warm[:, :], ACT.Silu)
                        for c in range(2):
                            act.wait_ge(s_tok[c], it + 1)
                            act.wait_ge(s["Th"], k.old)
                            act.copy(hT[:, c, :].rearrange("p (k n v) -> p k n v", k=BLK, v=V),
                                     S[c][:, :].rearrange("p (n k v) -> p k n v", k=BLK, v=V)).then_inc(s["hT"], 1)
                        for c in range(2):
                            act.wait_ge(s["Th"], k.n[c])
                            if isinstance(it, int) and c == 0:
                                act.wait_ge(m_done, 2)
                            act.copy(H[:, bass.ds(it, 1), c, :], Bk[c][0][:, :]).then_inc(s["Hs"], 1)
                    if kt:
                        tail_copy("TZ1", Z1T, 1, "Z1T", "g1")
                        tail_copy("TZ0", Z0T, 0, "Z0T", "g0")
                    if k:
                        for c in range(2):
                            act.wait_ge(s["xc"], k.n[c])
                            act.wait_ge(s["vs"], k.old)
                            act.activation(sq[:, c, :], xc[:, c, :], ACT.Square).then_inc(s["sq"], 1)
                    if kt:
                        tail_copy("Tx1", x1T, 0, "x1T", "g1")
                    if k:
                        for c in range(2):
                            act.wait_ge(s["Tx"], k.n[c])
                            act.copy(X[:, bass.ds(it, 1), c, :], Bk[c][1][:, :]).then_inc(s["X"], 1)
                        for c in range(2):
                            act.wait_ge(s["K"], k.n[c])
                            act.wait_ge(s["z0"], k.old)
                            act.wait_ge(s["x1"], k.old)
                            act.copy(keys[:, c, :], Bk[c][0][:, :]).then_inc(s["keys"], 1)
                        for c in range(2):
                            act.wait_ge(s["z0"], k.n[c])
                            act.wait_ge(s["q0"], k.old)
                            act.wait_ge(s["Z0"], k.old)
                            act.activation(s0[:, c, :], Bk[c][1][:, :], ACT.Silu, bias=bias[:, 0:1])
                            act.activation(q0[:, c, :], Bk[c][1][:, :], ACT.Tanh, bias=hbias[:, 0:1], scale=0.5).then_inc(s["a0"], 1)
                        for c in range(2):
                            act.wait_ge(s["z1"], k.n[c])
                            act.wait_ge(s["d"], k.old)
                            act.wait_ge(s["Z1"], k.old)
                            act.activation(s1[:, c, :], Bk[c][0][:, :], ACT.Silu, bias=bias[:, 1:2])
                            act.activation(q1[:, c, :], Bk[c][0][:, :], ACT.Tanh, bias=hbias[:, 1:2], scale=0.5).then_inc(s["a1"], 1)
                        for c in range(2):
                            act.wait_ge(s["A"], k.n[c])
                            act.wait_ge(s["D"], k.old)
                            act.activation(tha[:, c, :], Bk[c][0][:, :], ACT.Tanh, bias=hbias[:, 2:3], scale=0.5).then_inc(s["tha"], 1)

                turns(act, turn)

            @block.vector
            def _(dve):
                for name in "msum xc vs var xt p0 q0 d1 p1 q1 D Z1 E Z0 gacc".split():
                    dve.sem_inc(s[name], 1)
                def bc(t):
                    return t.unsqueeze(2).to_broadcast([128, NT, D])

                def tiles(t):
                    return t.rearrange("p (t f) -> p t f", f=D)

                for oh in range(2):
                    dve.wait_ge(m_ps, oh + 1)
                    for r in range(RP):
                        rows = slice(r * C, (r + 1) * C)
                        src = (S[oh][rows, :] if oh < 2 else None).rearrange("p (o hh r q) -> p hh r q o", hh=2, r=RP, q=Q)
                        for hh in range(2):
                            i = dve.tensor_copy(M[rows, hh, :, oh * 32:(oh + 1) * 32], src[:, hh, r, :, :])
                    i.then_inc(m_done, 1)
                dve.wait_ge(w_in2, 16 * 7)
                dve.wait_ge(zeroed, 2)
                for g in range(G):
                    r = slice(g * D, (g + 1) * D)
                    dve.tensor_copy(wkq[r, WA, r], wlr[r, :].to_broadcast([D, D]))
                dve.tensor_scalar(hbias[:, :], bias[:, :], 0.5, None, ALU.mult).then_inc(w_set, 1)
                dve.wait_ge(t_ps, 1)
                dve.tensor_scalar(wkq[:, W1T, :], MB[:, 0:128], 0.5, None, ALU.mult).then_inc(w_set, 1)
                dve.memset(grads[:, :, :], 0.0).then_inc(s["gacc"], 1)

                def turn(it, k, kt):
                    def tail():
                        dve.wait_ge(s["g0"], kt.n[1])
                        dve.wait_ge(s["g1"], kt.n[1])
                        dve.wait_ge(s["gacc"], kt.one)
                        dve.tensor_tensor(grads[:, :, :], grads[:, :, :], GB[:, 0:2, :], ALU.add).then_inc(s["gacc"], 1)

                    if not k:
                        return tail()
                    n, old, one = k.n, k.old, k.one
                    for c in range(2):
                        h = tiles(H[:, bass.ds(it, 1), c, :].rearrange("p a n -> p (a n)"))
                        dve.wait_ge(s["Hs"], n[c])
                        dve.tensor_reduce(msum[:, c, :], h, AX.X, ALU.add).then_inc(s["msum"], 1)
                    for c in range(2):
                        h = tiles(H[:, bass.ds(it, 1), c, :].rearrange("p a n -> p (a n)"))
                        dve.wait_ge(s["msum"], n[c])
                        dve.scalar_tensor_tensor(tiles(xc[:, c, :]), bc(msum[:, c, :]), -1.0 / D, h, ALU.mult, ALU.add).then_inc(s["xc"], 1)
                    for c in range(2):
                        dve.wait_ge(s["sq"], n[c])
                        dve.tensor_reduce(vsum[:, c, :], tiles(sq[:, c, :]), AX.X, ALU.add).then_inc(s["vs"], 1)
                    dve.wait_ge(s["vs"], n[1])
                    dve.tensor_scalar(var[:, :, :], vsum[:, :, :], 1.0 / D, EPS_LN, ALU.mult, ALU.add).then_inc(s["var"], 1)
                    dve.wait_ge(s["var"], one)
                    inverse_root(dve, var[:, :, :], std[:, :, :], rstd[:, :, :], s["rstd"], it * ROOT_STEPS)
                    for c in range(2):
                        dve.wait_ge(s["g0"], old)
                        dve.tensor_tensor(tiles(xt[:, c, :]), tiles(xc[:, c, :]), bc(rstd[:, c, :]), ALU.mult).then_inc(s["xt"], 1)
                    if kt:
                        tail()

                    def slopes(sl, th, ready, p, q):
                        for c in range(2):
                            dve.wait_ge(s[ready], n[c])
                            dve.scalar_tensor_tensor(th[:, c, :], sl[:, c, :], -1.0, th[:, c, :], ALU.add, ALU.mult).then_inc(s[p], 1)
                        for c in range(2):
                            dve.wait_ge(s[p], n[c])
                            dve.scalar_tensor_tensor(th[:, c, :], sl[:, c, :], 1.0, th[:, c, :], ALU.add, ALU.subtract).then_inc(s[q], 1)

                    slopes(s0, q0, "a0", "p0", "q0")
                    for c in range(2):
                        dve.wait_ge(s["V"], n[c])
                        dve.wait_ge(s["x1"], n[c])
                        dve.wait_ge(s["E"], old)
                        dve.tensor_tensor(dd[:, c, :], x1[:, c, :], Bk[c][1][:, :], ALU.subtract).then_inc(s["d1"], 1)
                    slopes(s1, q1, "a1", "p1", "q1")
                    for c in range(2):
                        dve.wait_ge(s["tha"], n[c])
                        dve.wait_ge(s["d"], n[c])
                        dve.scalar_tensor_tensor(dd[:, c, :], tha[:, c, :], 1.0, dd[:, c, :], ALU.add, ALU.mult).then_inc(s["D"], 1)
                    for c in range(2):
                        dve.wait_ge(s["D"], n[c])
                        dve.wait_ge(s["q1"], n[c])
                        dve.wait_ge(s["TZ1"], old)
                        dve.scalar_tensor_tensor(Z1[:, c, :], q1[:, c, :], 1.0, dd[:, c, :], ALU.mult, ALU.mult,
                                                 accum_out=zsum[:, 0, bass.ds(it * 2 + c, 1)]).then_inc(s["Z1"], 1)
                    for c in range(2):
                        dve.wait_ge(s["dx"], n[c])
                        dve.wait_ge(s["TZ0"], old)
                        dve.tensor_tensor(Z0[:, c, :], dd[:, c, :], Bk[c][1][:, :], ALU.add).then_inc(s["E"], 1)
                    for c in range(2):
                        dve.wait_ge(s["E"], n[c])
                        dve.scalar_tensor_tensor(Z0[:, c, :], q0[:, c, :], 1.0, Z0[:, c, :], ALU.mult, ALU.mult,
                                                 accum_out=zsum[:, 1, bass.ds(it * 2 + c, 1)]).then_inc(s["Z0"], 1)

                turns(dve, turn)

            @block.tensor
            def _(pe):
                for name in "Th Tx K z0 z1 V A dx Tx1 TZ1 TZ0 g1 g0".split():
                    pe.sem_inc(s[name], 1)
                def stage1(half):
                    for hh in range(2):
                        for q in range(Q):
                            for g in range(G):
                                last = pe.matmul(S[half][g * D:(g + 1) * D, :].rearrange("p (m v) -> p m v", v=V), M[:, hh, q, :],
                                                 xb[:, half, g, hh:hh + 8, q * V:(q + 1) * V],
                                                 start=(hh == 0 and q == 0), stop=(hh == 1 and q == Q - 1))
                            if hh == 1 and q == Q - 1:
                                last.then_inc(s_tok[half], 1)
                            yield

                pe.wait_ge(c_in, 16)
                pe.wait_ge(wt_in, 16 * RP)
                for o in range(D // OG):
                    half, at = divmod(o * OG * LEN, CH)
                    last = pe.matmul(S[half][:, at:at + OG * LEN], tw[:, o, :, :], dft, start=True, stop=True)
                    if at + OG * LEN == CH:
                        last.then_inc(m_ps, 1)
                pe.wait_ge(m_done, 2)
                for half in range(2):
                    pe.wait_ge(x_in[half], per_half[half])
                    for _ in stage1(half):
                        pass
                    if half == 0:
                        pe.wait_ge(w_in, 16 * 10)
                        pe.transpose(MB[:, 0:128], wkq[:, W1, :], ident).then_inc(t_ps, 1)
                pe.wait_ge(w_set, 2)

                def transposes(c, bank, src):
                    for k in range(BLK):
                        last = pe.transpose(Bk[c][bank][:, k * 128:(k + 1) * 128], src[:, c, k * 128:(k + 1) * 128], ident)
                    return last

                def body(it, k, kt, more):
                    if k:
                        n, old = k.n, k.old

                    def mm(c, bank, w, mov):
                        return pe.matmul(Bk[c][bank][:, :], wkq[:, w, :], mov, start=True, stop=True)

                    def xk(c):
                        return X[:, bass.ds(it, 1), c, :].rearrange("p a n -> p (a n)")

                    def t_h(c):
                        pe.wait_ge(s["hT"], n[c])
                        pe.wait_ge(s["tha"], old)
                        transposes(c, 0, hT).then_inc(s["Th"], 1)

                    def t_x(c):
                        pe.wait_ge(s["xt"], n[c])
                        pe.wait_ge(s["Z1T"], old)
                        transposes(c, 1, xt).then_inc(s["Tx"], 1)

                    def k_(c):
                        pe.wait_ge(s["X"], n[c])
                        pe.wait_ge(s["Hs"], n[c])
                        pe.wait_ge(s["x1T"], old)
                        mm(c, 0, WK, xk(c)).then_inc(s["K"], 1)

                    def z_0(c):
                        pe.wait_ge(s["keys"], n[c])
                        mm(c, 1, W0, keys[:, c, :]).then_inc(s["z0"], 1)

                    def z_1(c):
                        pe.wait_ge(s["x1"], n[c])
                        mm(c, 0, W1, x1[:, c, :]).then_inc(s["z1"], 1)

                    def v_(c):
                        pe.wait_ge(s["a0"], n[c])
                        mm(c, 1, WV, xk(c)).then_inc(s["V"], 1)

                    def a_(c):
                        pe.wait_ge(s["a1"], n[c])
                        mm(c, 0, WA, xk(c)).then_inc(s["A"], 1)

                    def dx(c):
                        pe.wait_ge(s["Z1"], n[c])
                        mm(c, 1, W1T, Z1[:, c, :]).then_inc(s["dx"], 1)

                    def t_z1(c):
                        pe.wait_ge(s["E"], kt.n[c])
                        transposes(c, 1, Z1).then_inc(s["TZ1"], 1)

                    def t_z0(c):
                        pe.wait_ge(s["Z0"], kt.n[c])
                        if k:
                            pe.wait_ge(s["Hs"], n[c])
                        transposes(c, 0, Z0).then_inc(s["TZ0"], 1)

                    def t_x1(c):
                        pe.wait_ge(s["Z0T"], kt.n[c])
                        transposes(c, 0, x1).then_inc(s["Tx1"], 1)

                    def grad(c, slot, lhs, rhs, name):
                        for b in range(BLK):
                            cols = slice(b * 128, (b + 1) * 128)
                            last = pe.matmul(GB[:, slot, :], lhs[:, c, cols], rhs[:, c, cols],
                                             start=(c == 0 and b == 0), stop=(c == 1 and b == BLK - 1))
                        last.then_inc(s[name], 1)

                    def g_0(c):
                        pe.wait_ge(s["Z0T"], kt.n[c])
                        pe.wait_ge(s["gacc"], kt.one)
                        grad(c, 1, xt, Z0T, "g0")

                    def g_1(c):
                        pe.wait_ge(s["x1T"], kt.n[c])
                        pe.wait_ge(s["Z1T"], kt.n[c])
                        grad(c, 0, x1T, Z1T, "g1")

                    def fills():
                        for half in range(2):
                            pe.wait_ge(x_in[half], (it + 2) * per_half[half])
                            yield from stage1(half)

                    fill = fills() if more else iter(())
                    front, tail, middle = [t_h, t_x], [t_z1, t_z0, g_0, t_x1, g_1], [k_, z_0, z_1, v_, a_, dx]
                    order = (front[:1] if k else []) + (tail if kt else []) + (front[1:] + middle if k else [])
                    for step in order:
                        for c in range(2):
                            step(c)
                            for _ in range((FILLS if kt else FIRST_FILLS).get(step.__name__, (0, 0))[c]):
                                next(fill, None)
                    for _ in fill:
                        pass

                body(0, Counts(pe, 0), None, True)
                with pe.Fori(1, PAIRS - 1, 1) as it:
                    body(it, Counts(pe, it), Counts(pe, it, -1), True)
                body(PAIRS - 1, Counts(pe, PAIRS - 1), Counts(pe, PAIRS - 1, -1), False)
                body(None, None, Counts(pe, PAIRS, -1), False)


FIRST_FILLS = dict(t_h=(0, 7), k_=(0, 1), z_0=(0, 1), z_1=(1, 1), v_=(0, 1), a_=(1, 3))
FILLS = dict(t_z0=(0, 1), g_0=(1, 0), t_x1=(1, 0), g_1=(0, 1), t_x=(1, 1), z_0=(1, 2), z_1=(2, 1), v_=(0, 1), a_=(0, 3))


def phase_b(nc, ctx, sb, sem, ps, const, env):
    wkq, H, X, nW, nb, bias, ident, xs, w12h, w12l, w3s, carry, table, grads, zsum, fold = (env[n] for n in
        "wkq H X nW nb bias ident xs w12h w12l w3s carry table grads zsum fold".split())
    warm = env["warm"]
    WK, W0, W1, WQ = 0, 3, 4, 6
    J = NT * PICKS
    with ExitStack() as a:
        def two(name, n=CH):
            return sb(name, [128, 2, n], at=a)

        w12 = sb("w12", [128, NE, 2 * HID], at=a)
        wg = sb("wg", [128, 2 * NE], at=a)
        gb = sb("gb", [128, NE], at=a)
        tri = sb("tri", [128, 128], BF16, at=a)
        ones = sb("ones", [128, 128], BF16, at=a)
        cnt = sb("cnt", [128, 2, NE], BF16, at=a)
        q, s0, s1, xt, sq, x2 = (two(n) for n in "bq bs0 bs1 bxt bsq bx2".split())
        rows = [sb(f"rows{c}", [128, PICKS, NT, ROW], at=a) for c in range(2)]
        msum, vsum, var, std, rstd, m1, m2, dm, th, km = (two(n, NT) for n in "bm bv bvar bstd brstd bm1 bm2 bdm bth bkm".split())
        L, ge = (two(n, NT * NE) for n in "bL bge".split())
        OH, SC, SL = (two(n, NE * J) for n in "bOH bSC bSL".split())
        base = two("bbase", NE)
        slotf = two("bslotf", J)
        slot = sb("bslot", [128, 2, J], U32, at=a)
        ids = sb("bids", [128, 2 * J], at=a)
        pack = sb("pack", [128, 2, D + 1], at=a)
        x0 = sb("gx0", [128, D], at=a)
        gr, par, den, mag = (sb(n, [128, 2, D + 1], at=a) for n in ("gr", "par", "den", "mag"))
        P = ps("gfold", a, (128, 2, CH // 2))
        P2 = ps("gw0", a)
        g_vec, g_pe, g_zero = sem("g_vec"), sem("g_pe"), sem("g_zero")
        Bk = [[ps(f"bchain{c}{i}", a) for i in range(2)] for c in range(2)]
        RK = [ps(f"brank{c}", a, (128, 2, CH // 2)) for c in range(2)]
        w_in, w_in2, z, z2, v0 = sem("bw_in"), sem("bw_in2"), sem("b_zero"), sem("b_gate_in"), sem("b_set")
        s = {n: sem("b_" + n) for n in ("Q q z0 s0 z1 s1 T sq rstd Tx x2T LG th RK slot half2 w_hi v go go_sum".split())}
        sent = [sem("b_sent0"), sem("b_sent1")]
        free = [sem("b_free0"), sem("b_free1")]
        G_DONE = 8
        keys, mask, first = const("keys"), const("mask"), const("first")
        pad = sb("pad", [128, ROW], at=a)
        nf = sb("nf", [128, NE], at=a)
        nd = sb("nd", [NE, NE], at=a)
        ncol, nt, endc, both = (sb(n, [NE, w], at=a) for n, w in (("ncol", 1), ("ntl", 1), ("endc", 1), ("both", 2)))
        nu = sb("nu", [NE, 1], U32, at=a)
        GE = sb("GE", [NE, NTILES], at=a)
        ef, xf = (sb(n, [1, NTILES], at=a) for n in ("ef", "xf"))
        padrow = sb("padrow", [1, NE], U32, at=a)
        tv, tp, pads = sem("t_vec"), sem("t_pe"), sem("t_pads")

        with nc.Block() as block:

            @block.sync
            def _(sp):
                sp.dma_start(gb[:, :], env["gate_b"].rearrange("(a n) -> a n", a=1).to_broadcast([128, NE])).then_inc(w_in2, 16)
                sp.wait_ge(z, 1)
                for g in range(G):
                    sp.dma_start(wg[g * D:(g + 1) * D, g * NE:(g + 1) * NE], env["gate_w"]).then_inc(z2, 16)
                sp.dma_start(w3s[:, 0:NE * D].rearrange("h (e o) -> h e o", o=D), env["w3"].rearrange("e h o -> h e o")).then_inc(w_in2, 16)
                for g in range(G):
                    rs = slice(g * D, (g + 1) * D)
                    for k, w in ((0, env["w1"]), (1, env["w2"])):
                        sp.dma_start(w12[rs, :, k * HID:(k + 1) * HID], w.rearrange("e d h -> d e h")).then_inc(w_in, 16)
                for c in range(2):
                    sp.sem_inc(free[c], 1)
                with sp.Fori(0, PAIRS, 1) as it:
                    for c in range(2):
                        sp.wait_ge(sent[c], (it + 1) * (16 * J))
                        sp.sem_inc(free[c], 1)

            @block.gpsimd
            def _(pool):
                pool.memset(nW[:, :, :], 0.0).then_inc(g_zero, 1)
                pool.memset(wg[:, :], 0.0).then_inc(z, 1)
                pool.memset(w3s[:, NE * D:], 0.0).then_inc(z, 1)
                pool.memset(ones[:, :], 1.0).then_inc(z, 1)
                pool.memset(pad[:, 0:2 * D + 1], 0.0).then_inc(z, 1)
                pool.memset(pad[:, 2 * D + 1:], 2.0).then_inc(z, 1)
                with pool.Fori(0, PAIRS, 1) as it:
                    n = [pool.snap(it * 2 + 2), pool.snap(it * 2 + 3)]
                    for c in range(2):
                        pool.wait_ge(s["slot"], n[c])
                        pool.wait_ge(s["half2"], n[c])
                        pool.sem_inc(s["go"], 1)
                        for t in range(NT):
                            for k in range(PICKS):
                                pool.indirect_dma_start(
                                    out=xs, out_offset=bass.IndirectOffsetOnAxis(ap=slot[:, c, t * PICKS + k:t * PICKS + k + 1], axis=0),
                                    in_=rows[c][:, k, t, :], in_offset=None).then_inc(sent[c], 16)
                for c in range(2):
                    pool.wait_ge(sent[c], 16 * J * PAIRS)

            @block.scalar
            def _(act):
                for name in "q s0 s1 sq x2T half2 th w_hi".split():
                    act.sem_inc(s[name], 1)

                def queries(it, k, c):
                    act.wait_ge(s["Q"], k.n[c])
                    act.wait_ge(s["T"], k.old)
                    act.copy(q[:, c, :], Bk[c][0][:, :]).then_inc(s["q"], 1)

                def silu(name, t, bank, z, b, k, c):
                    act.wait_ge(s[z], k.n[c])
                    act.wait_ge(s["T"], k.old)
                    act.activation(t[:, c, :], Bk[c][bank][:, :], ACT.Silu, bias=nb[:, b:b + 1]).then_inc(s[name], 1)

                def turn(it, more):
                    k, kf = Counts(act, it), Counts(act, it, 1)
                    for c in range(2):
                        act.wait_ge(s["v"], it * K + (1 + AT["xc"][c]))
                        act.activation(sq[:, c, :], xt[:, c, :], ACT.Square).then_inc(s["sq"], 1)
                    for c in range(2):
                        act.wait_ge(s["Tx"], k.n[c])
                        act.wait_ge(s["LG"], k.old)
                        act.copy(x2[:, c, :], Bk[c][0][:, :]).then_inc(s["x2T"], 1)
                    if more:
                        for c in range(2):
                            queries(it + 1, kf, c)
                    for c in range(2):
                        act.wait_ge(s["v"], it * K + (1 + AT["dm"][c]))
                        act.activation(th[:, c, :], dm[:, c, :], ACT.Tanh, scale=0.5).then_inc(s["th"], 1)
                        if more and c == 0:
                            for c1 in range(2):
                                silu("s0", s0, 1, "z0", 0, kf, c1)
                        act.wait_ge(s["v"], it * K + (1 + AT["lo"][c]))
                        act.wait_ge(free[c], it + 1)
                        act.copy(rows[c][:, 1, :, 0:2 * D], rows[c][:, 0, :, 0:2 * D]).then_inc(s["half2"], 1)
                        if c == 0:
                            act.wait_ge(w_in, 16 * 2 * G)
                            act.copy(w12h[:, bass.ds(it * 2, 2), :], w12[:, bass.ds(it * 2, 2), :]).then_inc(s["w_hi"], 1)
                            if more:
                                for c1 in range(2):
                                    silu("s1", s1, 0, "z1", 1, kf, c1)

                first_counts = Counts(act, 0)
                for c in range(2):
                    queries(0, first_counts, c)
                act.activation(warm[:, :], warm[:, :], ACT.Silu)
                act.wait_ge(g_vec, G_DONE)
                for c in range(2):
                    silu("s0", s0, 1, "z0", 0, first_counts, c)
                for c in range(2):
                    silu("s1", s1, 0, "z1", 1, first_counts, c)
                with act.Fori(0, PAIRS - 1, 1) as it:
                    turn(it, True)
                turn(PAIRS - 1, False)
                act.wait_ge(z, 5)
                act.dma_start(xs[PAD_ROW:PAD_ROW + 128, :], pad[:, :]).then_inc(pads, 16)
                act.wait_ge(tv, 1)
                _, pad_rows = nc.values_load_multi_w_load_instructions(
                    padrow[0:1, :], engines=(mybir.EngineType.Activation,), min_val=0, max_val=PAD_ROW - 128,
                    skip_runtime_bounds_check_because="a row of an expert's region, as counted on the chip")
                for row in pad_rows:
                    act.dma_start(xs[bass.ds(row, 128), :], pad[:, :]).then_inc(pads, 16)
                act.wait_ge(pads, 16 * (NE + 1))

            @block.vector
            def _(dve):
                for name in "v slot".split():
                    dve.sem_inc(s[name], 1)
                def bc(t, n=D):
                    return t.unsqueeze(2).to_broadcast([128, NT, n])

                def per_e(t):
                    return t.unsqueeze(1).to_broadcast([128, NT, NE])

                def tiles(t, f=D):
                    return t.rearrange("p (t f) -> p t f", f=f)

                for g in range(G):
                    r = slice(g * D, (g + 1) * D)
                    dve.tensor_copy(pack[r, 0, 0:D], grads[r, 1, r])
                    dve.tensor_copy(pack[r, 1, 0:D], grads[r, 0, r])
                dve.tensor_reduce(pack[:, 0, D:D + 1], zsum[:, 1, :], AX.X, ALU.add)
                dve.tensor_reduce(pack[:, 1, D:D + 1], zsum[:, 0, :], AX.X, ALU.add).then_inc(g_vec, 1)
                for g in range(G):
                    r = slice(g * D, (g + 1) * D)
                    for l, w in ((0, W0), (1, W1)):
                        dve.tensor_copy(par[r, l, 0:D], wkq[r, w, r])
                dve.tensor_copy(par[:, :, D:D + 1], bias[:, 0:2].unsqueeze(2))
                dve.wait_ge(g_pe, 1)
                dve.tensor_copy(x0[:, :], P[:, 0, 0:D]).then_inc(g_vec, 1)
                dve.tensor_scalar(gr[:, 1, :], P[:, 1, 0:D + 1], GRAD_SCALE, None, ALU.mult)
                dve.tensor_scalar(gr[:, 0, D:D + 1], P[:, 0, D:D + 1], GRAD_SCALE, None, ALU.mult)
                dve.wait_ge(g_pe, 2)
                dve.tensor_scalar(gr[:, 0, 0:D], P2[:, 0:D], GRAD_SCALE, None, ALU.mult).then_inc(g_vec, 1)
                dve.wait_ge(g_vec, 3)
                dve.scalar_tensor_tensor(mag[:, :, :], gr[:, :, :], -1.0, gr[:, :, :], ALU.mult, ALU.max).then_inc(g_vec, 1)
                dve.wait_ge(g_vec, 4)
                dve.tensor_scalar(den[:, :, :], mag[:, :, :], EPS_ADAM, None, ALU.add).then_inc(g_vec, 1)
                dve.wait_ge(g_vec, 5)
                dve.reciprocal(mag[:, :, :], den[:, :, :]).then_inc(g_vec, 1)
                dve.wait_ge(g_vec, 6)
                dve.scalar_tensor_tensor(den[:, :, :], mag[:, :, :], -LR, gr[:, :, :], ALU.mult, ALU.mult).then_inc(g_vec, 1)
                dve.wait_ge(g_vec, 7)
                dve.wait_ge(g_zero, 1)
                for g in range(G):
                    r = slice(g * D, (g + 1) * D)
                    dve.scalar_tensor_tensor(nW[r, :, r], par[r, :, 0:D], 1.0 - LR * WD, den[r, :, 0:D], ALU.mult, ALU.add)
                dve.scalar_tensor_tensor(nb[:, :].unsqueeze(2), par[:, :, D:D + 1], 1.0 - LR * WD, den[:, :, D:D + 1],
                                         ALU.mult, ALU.add).then_inc(g_vec, 1)
                dve.tensor_copy(tri[:, :], const("tri"))
                dve.tensor_copy(ids[:, :], const("ids"))
                dve.tensor_copy(carry[:, :], first).then_inc(v0, 1)
                dve.wait_ge(v0, 1)
                dve.wait_ge(w_in2, 32)
                with dve.Fori(0, PAIRS, 1) as it:
                    n = [dve.snap(it * 2 + 2), dve.snap(it * 2 + 3)]
                    done = dve.snap(it * K + 1)

                    def step(name, c, ins):
                        assert AT[name][c] == step.count + 1, (name, c, step.count)
                        step.count += 1
                        ins.then_inc(s["v"], 1)

                    step.count = 0

                    def after(name, c):
                        dve.wait_ge(s["v"], done + AT[name][c])

                    def Hc(c):
                        return H[:, bass.ds(it, 1), c, :].rearrange("p a n -> p (a n)")

                    def onehot(c, pick):
                        return OH[:, c, :].rearrange("p (e t k) -> p k t e", e=NE, k=PICKS)[:, pick]

                    def centre(c):
                        dve.wait_ge(s["T"], n[c])
                        step("h2", c, dve.tensor_tensor(Hc(c), Hc(c), Bk[c][1][:, :], ALU.add))
                        after("h2", c)
                        dve.sem_inc(s["go_sum"], 1)
                        step("msum", c, dve.tensor_reduce(msum[:, c, :], tiles(Hc(c)), AX.X, ALU.add))
                        after("msum", c)
                        step("xc", c, dve.scalar_tensor_tensor(tiles(xt[:, c, :]), bc(msum[:, c, :]), -1.0 / D, tiles(Hc(c)), ALU.mult, ALU.add))

                    def normalise(c):
                        dve.wait_ge(s["sq"], n[c])
                        step("vsum", c, dve.tensor_reduce(vsum[:, c, :], tiles(sq[:, c, :]), AX.X, ALU.add))
                        after("vsum", c)
                        step("var", c, dve.tensor_scalar(var[:, c, :], vsum[:, c, :], 1.0 / D, EPS_LN, ALU.mult, ALU.add))
                        after("var", c)
                        inverse_root(dve, var[:, c, :], std[:, c, :], rstd[:, c, :], s["rstd"], it * (2 * ROOT_STEPS) + c * ROOT_STEPS)
                        step("x2", c, dve.tensor_tensor(tiles(xt[:, c, :]), tiles(xt[:, c, :]), bc(rstd[:, c, :]), ALU.mult))

                    def largest(c, pick, m):
                        p = f"p{pick}"
                        after("L" if pick == 0 else "L2", c)
                        step(p + "m", c, dve.tensor_reduce(m[:, c, :], tiles(L[:, c, :], NE), AX.X, ALU.max))
                        after(p + "m", c)
                        step(p + "ge", c, dve.tensor_tensor(tiles(ge[:, c, :], NE), tiles(L[:, c, :], NE), bc(m[:, c, :], NE), ALU.is_equal))
                        after(p + "ge", c)
                        step(p + "key", c, dve.tensor_tensor(tiles(ge[:, c, :], NE), tiles(ge[:, c, :], NE), per_e(keys), ALU.mult))
                        after(p + "key", c)
                        step(p + "km", c, dve.tensor_reduce(km[:, c, :], tiles(ge[:, c, :], NE), AX.X, ALU.max))
                        after(p + "km", c)
                        step(p + "oh", c, dve.tensor_tensor(onehot(c, pick), tiles(ge[:, c, :], NE), bc(km[:, c, :], NE), ALU.is_equal))

                    def first_pick(c):
                        dve.wait_ge(s["LG"], n[c])
                        step("L", c, dve.tensor_tensor(tiles(L[:, c, :], NE), tiles(Bk[c][1][:, 0:NT * NE], NE), per_e(gb[:, :]), ALU.add))
                        largest(c, 0, m1)

                    def second_pick(c):
                        after("p0oh", c)
                        step("L2", c, dve.scalar_tensor_tensor(tiles(L[:, c, :], NE), onehot(c, 0), -3.0e38, tiles(L[:, c, :], NE), ALU.mult, ALU.add))
                        largest(c, 1, m2)

                    def count(c):
                        after("p1oh", c)
                        step("scan", c, dve.tensor_tensor_scan(SC[:, c, :], mask, OH[:, c, :], 0.0, ALU.mult, ALU.add))
                        step("dm", c, dve.tensor_tensor(dm[:, c, :], m1[:, c, :], m2[:, c, :], ALU.subtract))
                        after("scan", c)
                        step("cnt", c, dve.tensor_copy(cnt[:, c, :], SC[:, c, :].rearrange("p (e j) -> p e j", j=J)[:, :, J - 1]))

                    def slots(c):
                        dve.wait_ge(s["RK"], n[c])
                        if c:
                            after("carry", 0)
                        step("base", c, dve.tensor_tensor(base[:, c, :], RK[c][:, 0, 0:NE], carry[:, :], ALU.add))
                        after("base", c)
                        step("carry", c, dve.tensor_tensor(carry[:, :], RK[c][:, 1, 0:NE], carry[:, :], ALU.add))
                        ej = SC[:, c, :].rearrange("p (e j) -> p e j", j=J)
                        step("sl", c, dve.tensor_tensor(SL[:, c, :].rearrange("p (e j) -> p e j", j=J), ej,
                                                        base[:, c, :].unsqueeze(2).to_broadcast([128, NE, J]), ALU.add))
                        after("sl", c)
                        step("pick", c, dve.tensor_tensor(SL[:, c, :], SL[:, c, :], OH[:, c, :], ALU.mult))
                        after("pick", c)
                        step("slotf", c, dve.tensor_reduce(slotf[:, c, :], SL[:, c, :].rearrange("p (e j) -> p j e", j=J), AX.X, ALU.add))

                    def fill_rows(c):
                        dve.wait_ge(free[c], it + 1)
                        step("hi", c, dve.tensor_copy(rows[c][:, 0, :, 0:D].bitcast(F32R), tiles(xt[:, c, :])))
                        after("slotf", c)
                        step("slot", c, dve.tensor_copy(slot[:, c, :], slotf[:, c, :]))
                        after("hi", c)
                        step("lo", c, dve.tensor_tensor(rows[c][:, 0, :, D:2 * D], tiles(xt[:, c, :]), rows[c][:, 0, :, 0:D], ALU.subtract))
                        dve.wait_ge(s["th"], n[c])
                        step("wt1", c, dve.tensor_scalar(rows[c][:, 0, :, 2 * D], th[:, c, :], 0.5, 0.5, ALU.mult, ALU.add))
                        step("wt2", c, dve.tensor_scalar(rows[c][:, 1, :, 2 * D], th[:, c, :], -0.5, 0.5, ALU.mult, ALU.add))
                        step("id", c, dve.tensor_copy(rows[c][:, :, :, 2 * D + 1].bitcast(U32),
                                                      ids[:, c * J:(c + 1) * J].rearrange("p (t k) -> p k t", k=PICKS)))
                        after("id", c)
                        dve.tensor_scalar(ids[:, c * J:(c + 1) * J], ids[:, c * J:(c + 1) * J], float(PICKS * G * TOK), None,
                                          ALU.add).then_inc(s["slot"], 1)

                    centre(0)
                    centre(1)
                    normalise(0)
                    normalise(1)
                    first_pick(0)
                    second_pick(0)
                    count(0)
                    first_pick(1)
                    slots(0)
                    fill_rows(0)
                    second_pick(1)
                    count(1)
                    slots(1)
                    fill_rows(1)
                    dve.wait_ge(s["w_hi"], it + 2)
                    for c in range(2):
                        e = bass.ds(it * 2 + c, 1)
                        step("wlo", c, dve.tensor_tensor(w12l[:, e, :], w12[:, e, :], w12h[:, e, :].bitcast(F32), ALU.subtract))
                    dve.wait_ge(s["slot"], n[1])
                    assert step.count == K, step.count
                dve.wait_ge(s["v"], K * PAIRS + 1)
                dve.tensor_scalar(padrow[:, :], carry[0:1, :], 1.0, None, ALU.add).then_inc(tv, 1)
                dve.tensor_tensor(nf[:, :], carry[:, :], first, ALU.subtract).then_inc(tv, 1)
                dve.wait_ge(tv, 2)
                dve.tensor_tensor(nd[:, :], nf[0:NE, :], ident[0:NE, 0:NE], ALU.mult).then_inc(tv, 1)
                dve.wait_ge(tv, 3)
                dve.tensor_reduce(ncol[:, :], nd[:, :], AX.X, ALU.add).then_inc(tv, 1)
                dve.wait_ge(tv, 4)
                dve.tensor_copy(nu[:, :], ncol[:, :]).then_inc(tv, 1)
                dve.wait_ge(tv, 5)
                dve.tensor_scalar(nu[:, :], nu[:, :], 7, None, ALU.logical_shift_right).then_inc(tv, 1)
                dve.wait_ge(tv, 6)
                dve.tensor_scalar(nt[:, :], nu[:, :], 1.0, None, ALU.add).then_inc(tv, 1)
                dve.wait_ge(tv, 7)
                dve.memset(both[:, 0:1], 1.0)
                dve.tensor_scalar(both[:, 1:2], nt[:, :], -128.0, float(REGION), ALU.mult, ALU.add)
                dve.wait_ge(tp, 1)
                dve.tensor_copy(endc[:, :], Bk[0][0][0:NE, 0:1]).then_inc(tv, 1)
                dve.wait_ge(tv, 8)
                dve.tensor_scalar(GE[:, :], const("tile", NE), endc[:, 0:1], None, ALU.is_ge).then_inc(tv, 1)
                dve.wait_ge(tp, 2)
                dve.tensor_scalar(ef[:, :], Bk[0][1][0:1, 0:NTILES], float(NE - 1), None, ALU.min)
                dve.scalar_tensor_tensor(xf[:, :], const("tile", 1), 128.0, Bk[1][1][0:1, 0:NTILES], ALU.mult, ALU.add).then_inc(tv, 1)
                dve.wait_ge(tv, 10)
                dve.tensor_scalar(table[:, 0, :], ef[:, :], float(D), None, ALU.mult)
                dve.tensor_scalar(table[:, 1, :], xf[:, :], float(PAD_ROW), None, ALU.min)
                dve.tensor_scalar(table[:, 2, :], ef[:, :], float(2 * HID), None, ALU.mult).then_inc(tv, 1)

            @block.tensor
            def _(pe):
                for name in "Q z0 z1 T Tx LG RK".split():
                    pe.sem_inc(s[name], 1)

                def q_(it, k, c):
                    pe.wait_ge(s["x2T"], k.old)
                    pe.matmul(Bk[c][0][:, :], wkq[:, WQ, :], X[:, bass.ds(it, 1), c, :].rearrange("p a n -> p (a n)"),
                              start=True, stop=True).then_inc(s["Q"], 1)

                def z_0(it, k, c, peeled=False):
                    pe.wait_ge(s["q"], k.n[c])
                    if not peeled:
                        pe.wait_ge(s["v"], it * K + (1 - K + AT["L"][c]))
                    pe.matmul(Bk[c][1][:, :], nW[:, 0, :], q[:, c, :], start=True, stop=True).then_inc(s["z0"], 1)

                def z_1(it, k, c):
                    pe.matmul(Bk[c][0][:, :], nW[:, 1, :], q[:, c, :], start=True, stop=False)
                    pe.wait_ge(s["s0"], k.n[c])
                    pe.matmul(Bk[c][0][:, :], nW[:, 1, :], s0[:, c, :], start=False, stop=True).then_inc(s["z1"], 1)

                def t_r(it, k, c):
                    pe.wait_ge(s["s1"], k.n[c])
                    for b in range(BLK):
                        cols = slice(b * 128, (b + 1) * 128)
                        for i, part in enumerate((q, s0, s1)):
                            last = pe.matmul(Bk[c][1][:, cols], part[:, c, cols], ident, start=i == 0, stop=i == 2)
                    last.then_inc(s["T"], 1)

                def turn(it, more):
                    k, kf = Counts(pe, it), Counts(pe, it, 1)
                    def t_x(c):
                        pe.wait_ge(s["v"], it * K + (1 + AT["x2"][c]))
                        for b in range(BLK):
                            last = pe.transpose(Bk[c][0][:, b * 128:(b + 1) * 128], xt[:, c, b * 128:(b + 1) * 128], ident)
                        last.then_inc(s["Tx"], 1)

                    def logits(c):
                        pe.wait_ge(s["x2T"], k.n[c])
                        for b in range(BLK):
                            last = pe.matmul(Bk[c][1][:, b * 2 * NE:(b + 1) * 2 * NE], x2[:, c, b * 128:(b + 1) * 128], wg[:, :],
                                             start=True, stop=True)
                        last.then_inc(s["LG"], 1)

                    def ranks(c):
                        pe.wait_ge(s["v"], it * K + (1 + AT["cnt"][c]))
                        pe.matmul(RK[c][:, 0, 0:NE], tri[:, :], cnt[:, c, :], start=True, stop=True)
                        pe.matmul(RK[c][:, 1, 0:NE], ones[:, :], cnt[:, c, :], start=True, stop=True).then_inc(s["RK"], 1)

                    t_x(0)
                    pe.wait_ge(z2, 32)
                    logits(0)
                    t_x(1)
                    logits(1)
                    if more:
                        q_(it + 1, kf, 0)
                        q_(it + 1, kf, 1)
                    pe.wait_ge(z, 3)
                    ranks(0)
                    if more:
                        z_0(it + 1, kf, 0)
                        z_0(it + 1, kf, 1)
                        z_1(it + 1, kf, 0)
                        z_1(it + 1, kf, 1)
                        t_r(it + 1, kf, 0)
                    ranks(1)
                    if more:
                        t_r(it + 1, kf, 1)

                pe.wait_ge(g_vec, 1)
                pe.matmul(P[:, :, 0:D + 1], fold, pack[:, :, :], start=True, stop=True).then_inc(g_pe, 1)
                pe.wait_ge(g_vec, 2)
                pe.matmul(P2[:, 0:D], wkq[:, WK, :], x0[:, :], start=True, stop=True).then_inc(g_pe, 1)
                first_counts = Counts(pe, 0)
                for c in range(2):
                    q_(0, first_counts, c)
                pe.wait_ge(g_vec, G_DONE)
                for c in range(2):
                    z_0(0, first_counts, c, peeled=True)
                for step in (z_1, t_r):
                    for c in range(2):
                        step(0, first_counts, c)
                with pe.Fori(0, PAIRS - 1, 1) as it:
                    turn(it, True)
                turn(PAIRS - 1, False)
                pe.wait_ge(tv, 7)
                pe.matmul(Bk[0][0][0:NE, 0:1], const("incl", NE), nt[:, :], start=True, stop=True).then_inc(tp, 1)
                pe.wait_ge(tv, 9)
                pe.matmul(Bk[0][1][0:1, 0:NTILES], both[:, 0:1], GE[:, :], start=True, stop=True)
                pe.matmul(Bk[1][1][0:1, 0:NTILES], both[:, 1:2], GE[:, :], start=True, stop=True).then_inc(tp, 1)


_CENTRE, _NORM, _FIRST, _SECOND, _COUNT, _SLOTS, _ROWS = (n.split() for n in (
    "h2 msum xc", "vsum var x2", "L p0m p0ge p0key p0km p0oh", "L2 p1m p1ge p1key p1km p1oh", "scan dm cnt",
    "base carry sl pick slotf", "hi slot lo wt1 wt2 id"))
_ORDER = [(name, c) for names, c in ((_CENTRE, 0), (_CENTRE, 1), (_NORM, 0), (_NORM, 1), (_FIRST, 0), (_SECOND, 0), (_COUNT, 0),
                                     (_FIRST, 1), (_SLOTS, 0), (_ROWS, 0), (_SECOND, 1), (_COUNT, 1), (_SLOTS, 1), (_ROWS, 1),
                                     (["wlo"], 0), (["wlo"], 1)) for name in names]
AT = {}
for _i, (_name, _c) in enumerate(_ORDER):
    AT.setdefault(_name, [0, 0])[_c] = _i + 1
K = len(_ORDER)


def phase_c(nc, ctx, sb, sem, ps, const, env):
    ident, xs, ys, w12h, w12l, w3s, table = (env[n] for n in "ident xs ys w12h w12l w3s table".split())
    with ExitStack() as a:
        xt = [sb(f"cx{j}", [128, GT, ROW], at=a) for j in range(DEPTH)]
        tag = [sb(f"ctag{j}", [128, GT, 2], at=a) for j in range(DEPTH)]
        y = [sb(f"cy{j}", [128, GT, D], at=a) for j in range(DEPTH)]
        xT = sb("cxT", [128, 2, GT * 128], F32R, at=a)
        gl, hid, hT = (sb(n, [128, 2, GT * HID], at=a) for n in ("cgl", "chid", "chT"))
        T1B = ps("ct1", a, (128, GT * 128))
        T2B = ps("ct2", a, (128, GT * 128))
        HP = [ps(f"ch{c}", a, (128, GT, 2 * HID)) for c in range(2)]
        YP = [ps(f"cyp{c}", a, (128, GT, 128)) for c in range(2)]
        x_in = [sem(f"c_in{j}") for j in range(DEPTH)]
        y_out = [sem(f"c_out{j}") for j in range(DEPTH)]
        s = {n: sem("c_" + n) for n in "T1 xT tag H gl hid T2 hT Y y go".split()}

        def wait(eng, name, g):
            if not (isinstance(g, int) and g < 0):
                eng.wait_ge(s[name], g + 1)

        def wait_dma(eng, sems, g, j):
            if not (isinstance(g, int) and g < 0):
                eng.wait_ge(sems[j], (g - j) * (16 * GT // DEPTH) + 16 * GT)

        def steps(eng, step):
            for g in range(-2, FIRST):
                step(g, g % DEPTH, False)
            with eng.Fori(0, TURNS, 1) as it:
                for u in range(DEPTH):
                    step(it * DEPTH + (FIRST + u), (FIRST + u) % DEPTH, True)
            for g in range(FIRST + TURNS * DEPTH, GROUPS + 1):
                step(g, g % DEPTH, False)

        def has(g, off, looped):
            return looped or 0 <= g + off < GROUPS

        with nc.Block() as block:

            @block.sync
            def _(sp):
                def load(g, j):
                    wait(sp, "T1", g - DEPTH)
                    wait(sp, "tag", g - DEPTH)
                    _, first_rows = nc.values_load_multi_w_load_instructions(
                        table[0:1, 1, bass.ds(g * GT, GT)], engines=(mybir.EngineType.SP,), min_val=0, max_val=PAD_ROW,
                        skip_runtime_bounds_check_because=CLAMPED)
                    for t, row in enumerate(first_rows):
                        sp.dma_start(xt[j][:, t, :], xs[bass.ds(row, 128), :]).then_inc(x_in[j], 16)

                for g in range(DEPTH):
                    load(g, g)
                with sp.Fori(1, GROUPS // DEPTH, 1) as it:
                    for j in range(DEPTH):
                        load(it * DEPTH + j, j)

            @block.gpsimd
            def _(pool):
                with pool.Fori(0, GROUPS // DEPTH, 1) as it:
                    for j in range(DEPTH):
                        wait(pool, "y", it * DEPTH + j)
                        pool.sem_inc(s["go"], 1)
                        for t in range(GT):
                            pool.indirect_dma_start(
                                out=ys, out_offset=bass.IndirectOffsetOnAxis(ap=tag[j][:, t, 1:2].bitcast(U32), axis=0),
                                in_=y[j][:, t, :], in_offset=None, bounds_check=NTOK * PICKS - 1, oob_is_err=False).then_inc(y_out[j], 16)
                for j in range(DEPTH):
                    pool.wait_ge(y_out[j], 16 * GT * (GROUPS // DEPTH))

            @block.scalar
            def _(act):
                def step(g, j, looped):
                    if has(g, 0, looped):
                        wait(act, "T2", g)
                        wait(act, "Y", g - 2)
                        act.copy(hT[:, j % 2, :], T2B[:, :]).then_inc(s["hT"], 1)
                    if has(g, 1, looped):
                        wait(act, "H", g + 1)
                        wait(act, "hid", g - 1)
                        act.activation(gl[:, (j + 1) % 2, :].rearrange("p (t h) -> p t h", h=HID), HP[(j + 1) % 2][:, :, 0:HID],
                                       ACT.Silu).then_inc(s["gl"], 1)
                    if has(g, 2, looped):
                        wait(act, "T1", g + 2)
                        wait(act, "H", g)
                        act.copy(xT[:, j % 2, :], T1B[:, :]).then_inc(s["xT"], 1)

                steps(act, step)

            @block.vector
            def _(dve):
                def step(g, j, looped):
                    if has(g, -1, looped):
                        k = (j - 1) % DEPTH
                        wait(dve, "Y", g - 1)
                        wait(dve, "tag", g - 1)
                        dve.tensor_tensor(y[k][:, :, :], YP[k % 2][:, :, 0:D], tag[k][:, :, 0:1].to_broadcast([128, GT, D]),
                                          ALU.mult).then_inc(s["y"], 1)
                    if has(g, 1, looped):
                        k = (j + 1) % DEPTH
                        wait_dma(dve, x_in, g + 1, k)
                        wait_dma(dve, y_out, g + 1 - DEPTH, k)
                        dve.tensor_copy(tag[k][:, :, :].bitcast(U32), xt[k][:, :, 2 * D:].bitcast(U32)).then_inc(s["tag"], 1)
                    if has(g, 1, looped):
                        k = (j + 1) % 2
                        wait(dve, "gl", g + 1)
                        wait(dve, "T2", g - 1)
                        dve.tensor_tensor(hid[:, k, :].rearrange("p (t h) -> p t h", h=HID),
                                          gl[:, k, :].rearrange("p (t h) -> p t h", h=HID), HP[k][:, :, HID:], ALU.mult).then_inc(s["hid"], 1)

                steps(dve, step)

            @block.tensor
            def _(pe):
                def weights(which, g):
                    return nc.values_load_multi_w_load_instructions(
                        table[0:1, which, bass.ds(g * GT, GT)], engines=(mybir.EngineType.PE,), min_val=0,
                        max_val=(NE - 1) * (2 * HID if which == 2 else D), skip_runtime_bounds_check_because=CLAMPED)[1]

                def step(g, j, looped):
                    if has(g, -1, looped):
                        k = (j - 1) % 2
                        cols = weights(0, g - 1)
                        wait(pe, "hT", g - 1)
                        wait(pe, "y", g - 3)
                        for t in range(GT):
                            last = pe.matmul(YP[k][:, t, :], hT[:, k, t * 128:(t + 1) * 128], w3s[:, bass.ds(cols[t], 128)],
                                             start=True, stop=True)
                        last.then_inc(s["Y"], 1)
                    if has(g, 0, looped):
                        wait(pe, "hid", g)
                        wait(pe, "hT", g - 1)
                        for t in range(GT):
                            last = pe.transpose(T2B[:, t * 128:(t + 1) * 128], hid[:, j % 2, t * 128:(t + 1) * 128], ident)
                        last.then_inc(s["T2"], 1)
                    if has(g, 1, looped):
                        k = (j + 1) % 2
                        cols = weights(2, g + 1)
                        wait(pe, "xT", g + 1)
                        wait(pe, "hid", g - 1)
                        for t in range(GT):
                            lhs = xT[:, k, t * 128:(t + 1) * 128]
                            pe.matmul(HP[k][:, t, :], lhs, w12h_f[:, bass.ds(cols[t], 2 * HID)], start=True, stop=False)
                            last = pe.matmul(HP[k][:, t, :], lhs, w12l_f[:, bass.ds(cols[t], 2 * HID)], start=False, stop=True)
                        last.then_inc(s["H"], 1)
                    if has(g, 2, looped):
                        k = (j + 2) % DEPTH
                        wait_dma(pe, x_in, g + 2, k)
                        wait(pe, "xT", g + 1)
                        for t in range(GT):
                            last = pe.transpose(T1B[:, t * 128:(t + 1) * 128], xt[k][:, t, 0:2 * D], ident)
                        last.then_inc(s["T1"], 1)

                w12h_f, w12l_f = (w[:, :, :].rearrange("p e n -> p (e n)") for w in (w12h, w12l))
                steps(pe, step)


def phase_d(nc, ctx, sb, sem, ps, const, env):
    H, X, ys, out = env["H"], env["X"], env["ys"], env["out"]
    y_v = ys.rearrange("(q g v c n2 k p) f -> q g n2 v c (k p f)", g=G, v=V, c=2, k=BLK, n2=2, p=PICKS)
    o_v = out.rearrange("(q g) (v c n2 k) f -> q g n2 v c (k f)", g=G, v=V, c=2, k=BLK, n2=2)
    with ExitStack() as a:
        BUFS = 4
        yb = [sb(f"yb{j}", [128, G, 2, BLK, PICKS, D], at=a) for j in range(BUFS)]
        o = X[:, :, :, :].rearrange("p q c n -> p q (c n)").rearrange("p q (g c k f) -> p q g c k f", g=G, c=2, k=BLK)
        y_in = [sem(f"d_in{j}") for j in range(BUFS)]
        o_out, o_out2, part, summed = sem("d_out"), sem("d_out2"), sem("d_part"), sem("d_sum")
        with nc.Block() as block:
            @block.sync
            def _(sp):
                def load(pair, j):
                    for n2 in range(2):
                        for g in range(G):
                            sp.dma_start(yb[j][n2 * V:(n2 + 1) * V, g].rearrange("v c k p f -> v c (k p f)"),
                                         y_v[bass.ds(pair, 1), g, n2]).then_inc(y_in[j], 16)

                for j in range(BUFS):
                    load(j, j)
                with sp.Fori(1, PAIRS // BUFS, 1) as turn:
                    for j in range(BUFS):
                        sp.wait_ge(summed, turn * (2 * BUFS) + (2 * j + 2 - 2 * BUFS))
                        load(turn * BUFS + j, j)

            def store(eng, pair, n2, done):
                for g in range(G):
                    eng.dma_start(o_v[bass.ds(pair, 1), g, n2], o[n2 * V:(n2 + 1) * V, bass.ds(pair, 1), g]
                                  .rearrange("v q c k f -> v (q c) (k f)")).then_inc(done, 16)

            @block.scalar
            def _(act):
                with act.Fori(0, PAIRS, 1) as pair:
                    act.wait_ge(summed, pair * 2 + 2)
                    store(act, pair, 0, o_out)
                act.wait_ge(o_out, 16 * G * PAIRS)

            @block.gpsimd
            def _(pool):
                with pool.Fori(0, PAIRS, 1) as pair:
                    pool.wait_ge(summed, pair * 2 + 2)
                    store(pool, pair, 1, o_out2)
                pool.wait_ge(o_out2, 16 * G * PAIRS)

            @block.vector
            def _(dve):
                with dve.Fori(0, PAIRS // BUFS, 1) as turn:
                    for j in range(BUFS):
                        pair = bass.ds(turn * BUFS + j, 1)
                        dve.wait_ge(y_in[j], turn * (32 * G) + 32 * G)
                        for c in range(2):
                            h = H[:, pair, c, :].rearrange("p a (k g f) -> p g (a k) f", g=G, f=D)
                            oc = o[:, pair, :, c].rearrange("p a g k f -> p g (a k) f")
                            dve.tensor_tensor(oc, h, yb[j][:, :, c, :, 0, :], ALU.add).then_inc(part, 1)
                        for c in range(2):
                            oc = o[:, pair, :, c].rearrange("p a g k f -> p g (a k) f")
                            dve.wait_ge(part, turn * (2 * BUFS) + (2 * j + c + 1))
                            dve.tensor_tensor(oc, oc, yb[j][:, :, c, :, 1, :], ALU.add).then_inc(summed, 1)


_INS = ["x", "L0_tok_W", "L0_attn_Wk", "L0_attn_Wq", "L0_attn_Wv", "L0_attn_Wlr", "L0_attn_blr", "L0_attn_Ws", "L0_attn_bs",
        "L0_ffn_gate_w", "L0_ffn_gate_b", "L0_ffn_w1", "L0_ffn_w2", "L0_ffn_w3"]


def kernel(**inputs):
    import numpy as _np
    import concourse.bacc as _bacc
    from concourse import mybir as _mybir
    from concourse.bass_utils import run_bass_kernel_spmd as _run

    nc = _bacc.Bacc("TRN2", target_bir_lowering=False, num_devices=1)
    arrays, args = {}, []
    for name in _INS:
        arrays[f"in_{name}_dram"] = _np.ascontiguousarray(inputs[name])
    arrays["in_consts_dram"] = constants()
    for name, a in arrays.items():
        args.append(nc.dram_tensor(name, a.shape, _mybir.dt.from_np(a.dtype), kind="ExternalInput").ap())
    out = nc.dram_tensor("out_0_dram", (B, TOK, D), _mybir.dt.float32, kind="ExternalOutput").ap()
    vit_tower(nc, *args, out)
    r = _run(nc, [arrays], core_ids=[0])
    return r.results[0]["out_0_dram"]
```
